# Optimizing a Trainium2 kernel written in Bass

```python
import numpy as np
import jax
import jax.numpy as jnp

def _softmax(x, axis=-1):
    return jax.nn.softmax(x, axis=axis)

def _gelu(x):
    return jax.nn.gelu(x, approximate=True)

def _silu(x):
    return jax.nn.silu(x)

def _sigmoid(x):
    return jax.nn.sigmoid(x)

def _layernorm(x, axis=-1, eps=1e-05):
    m = jnp.mean(x, axis=axis, keepdims=True)
    v = jnp.var(x, axis=axis, keepdims=True)
    return (x - m) / jnp.sqrt(v + eps)

def _scatter_add(tgt, idx, src, axis=0):
    return tgt.at[idx].add(src)

def _segment_sum(src, seg, n):
    return jax.ops.segment_sum(src, seg, n)
kernel_name = 'mk_hybrid_d1_jaxref_r8_382574'

def setup_inputs(seed: int=0):
    np.random.seed(seed)
    _w = jnp.asarray

    def _L0_attn_a_setup():
        import jax, jax.numpy as jnp
        import numpy as np
        DIM = 128
        NHEAD = 16
        HEAD_DIM = DIM // NHEAD

        def _rotate_half(t):
            h = t.shape[-1] // 2
            return jnp.concatenate([-t[..., h:], t[..., :h]], axis=-1)
        key = jax.random.key(seed)
        ks = jax.random.split(key, 5)
        B, N = (4, 256)
        return {'x': jax.random.normal(ks[0], (B, N, DIM), dtype=jnp.float32), 'qkv_w': jax.random.normal(ks[1], (3 * DIM, DIM), dtype=jnp.float32) * 0.02, 'qkv_b': jax.random.normal(ks[2], (3 * DIM,), dtype=jnp.float32) * 0.02, 'proj_w': jax.random.normal(ks[3], (DIM, DIM), dtype=jnp.float32) * 0.02, 'proj_b': jax.random.normal(ks[4], (DIM,), dtype=jnp.float32) * 0.02}
    _L0_attn_a_in = _L0_attn_a_setup()

    def _L0_attn_b_setup():
        import jax, jax.numpy as jnp
        import numpy as np
        B, S, D, H, A = (2, 256, 128, 16, 64)
        INIT_STD = 0.02
        key = jax.random.key(seed)
        ks = jax.random.split(key, 5)
        return {'residual': jax.random.normal(ks[0], (B, S, D), dtype=jnp.float32), 'Wq': jax.random.normal(ks[1], (H, D, A), dtype=jnp.float32) * INIT_STD, 'Wk': jax.random.normal(ks[2], (H, D, A), dtype=jnp.float32) * INIT_STD, 'Wv': jax.random.normal(ks[3], (H, D, A), dtype=jnp.float32) * INIT_STD, 'Wo': jax.random.normal(ks[4], (H, A, D), dtype=jnp.float32) * INIT_STD, 'bq': jnp.zeros((H, A), dtype=jnp.float32), 'bk': jnp.zeros((H, A), dtype=jnp.float32), 'bv': jnp.zeros((H, A), dtype=jnp.float32), 'bo': jnp.zeros((D,), dtype=jnp.float32)}
    _L0_attn_b_in = _L0_attn_b_setup()

    def _L0_ffn_setup():
        import jax, jax.numpy as jnp
        import numpy as np
        B, S, H, F, G = (8, 256, 128, 512, 128)
        EPS = 1e-05

        def _dequant(q, scales, g):
            K, N = q.shape
            w = (q.astype(jnp.float32) - 128.0).reshape(K // g, g, N) * scales[:, None, :]
            return w.reshape(K, N)
        key = jax.random.key(seed)
        ks = jax.random.split(key, 8)
        x = jax.random.normal(ks[0], (B, S, H), dtype=jnp.float32)
        ln_gamma = jnp.ones((H,), jnp.float32)
        ln_beta = jnp.zeros((H,), jnp.float32)
        fc1_q = jax.random.randint(ks[1], (H, F), 0, 32, dtype=jnp.int32)
        fc2_q = jax.random.randint(ks[2], (F, H), 0, 32, dtype=jnp.int32)
        fc1_scales = jax.random.uniform(ks[3], (H // G, F), jnp.float32) * 0.02 + 0.001
        fc2_scales = jax.random.uniform(ks[4], (F // G, H), jnp.float32) * 0.02 + 0.001
        fc1_bias = jax.random.normal(ks[5], (F,), jnp.float32) * 0.02
        fc2_bias = jax.random.normal(ks[6], (H,), jnp.float32) * 0.02
        return {'x': x, 'ln_gamma': ln_gamma, 'ln_beta': ln_beta, 'fc1_q': fc1_q, 'fc1_scales': fc1_scales, 'fc1_bias': fc1_bias, 'fc2_q': fc2_q, 'fc2_scales': fc2_scales, 'fc2_bias': fc2_bias}
    _L0_ffn_in = _L0_ffn_setup()
    _d = {'L0_attn_a_x': _L0_attn_a_in['x'], 'L0_attn_a_qkv_w': _L0_attn_a_in['qkv_w'], 'L0_attn_a_qkv_b': _L0_attn_a_in['qkv_b'], 'L0_attn_a_proj_w': _L0_attn_a_in['proj_w'], 'L0_attn_a_proj_b': _L0_attn_a_in['proj_b'], 'L0_attn_b_Wq': _L0_attn_b_in['Wq'], 'L0_attn_b_Wk': _L0_attn_b_in['Wk'], 'L0_attn_b_Wv': _L0_attn_b_in['Wv'], 'L0_attn_b_Wo': _L0_attn_b_in['Wo'], 'L0_attn_b_bq': _L0_attn_b_in['bq'], 'L0_attn_b_bk': _L0_attn_b_in['bk'], 'L0_attn_b_bv': _L0_attn_b_in['bv'], 'L0_attn_b_bo': _L0_attn_b_in['bo'], 'L0_ffn_ln_gamma': _L0_ffn_in['ln_gamma'], 'L0_ffn_ln_beta': _L0_ffn_in['ln_beta'], 'L0_ffn_fc1_q': _L0_ffn_in['fc1_q'], 'L0_ffn_fc1_scales': _L0_ffn_in['fc1_scales'], 'L0_ffn_fc1_bias': _L0_ffn_in['fc1_bias'], 'L0_ffn_fc2_q': _L0_ffn_in['fc2_q'], 'L0_ffn_fc2_scales': _L0_ffn_in['fc2_scales'], 'L0_ffn_fc2_bias': _L0_ffn_in['fc2_bias']}
    _x0 = _d['L0_attn_a_x']
    _d['L0_attn_a_x'] = jax.random.normal(jax.random.fold_in(jax.random.key(seed), 1), (8, 512, 128), dtype=_x0.dtype)
    del _x0
    return _d

def reference(L0_attn_a_x, L0_attn_a_qkv_w, L0_attn_a_qkv_b, L0_attn_a_proj_w, L0_attn_a_proj_b, L0_attn_b_Wq, L0_attn_b_Wk, L0_attn_b_Wv, L0_attn_b_Wo, L0_attn_b_bq, L0_attn_b_bk, L0_attn_b_bv, L0_attn_b_bo, L0_ffn_ln_gamma, L0_ffn_ln_beta, L0_ffn_fc1_q, L0_ffn_fc1_scales, L0_ffn_fc1_bias, L0_ffn_fc2_q, L0_ffn_fc2_scales, L0_ffn_fc2_bias):

    def _L0_attn_a_ref(x, qkv_w, qkv_b, proj_w, proj_b):
        import jax, jax.numpy as jnp
        import numpy as np
        DIM = 128
        NHEAD = 16
        HEAD_DIM = DIM // NHEAD

        def _rotate_half(t):
            h = t.shape[-1] // 2
            return jnp.concatenate([-t[..., h:], t[..., :h]], axis=-1)
        B, N, D = x.shape
        H, hd = (NHEAD, HEAD_DIM)
        qkv = x @ qkv_w.T + qkv_b
        qkv = jnp.transpose(qkv.reshape(B, N, 3, H, hd), (2, 0, 3, 1, 4))
        q, k, v = (qkv[0], qkv[1], qkv[2])
        inv_freq = 1.0 / 10000.0 ** (jnp.arange(0, hd, 2, dtype=x.dtype) / hd)
        pos = jnp.arange(N, dtype=x.dtype)
        freqs = pos[:, None] * inv_freq[None, :]
        emb = jnp.concatenate([freqs, freqs], axis=-1)
        cos = jnp.cos(emb)[None, None, None]
        sin = jnp.sin(emb)[None, None, None]
        q = q * cos + _rotate_half(q) * sin
        k = k * cos + _rotate_half(k) * sin
        scale = hd ** (-0.5)
        attn = jnp.einsum('abhqd,abhkd->abhqk', q, k) * scale
        attn = jax.nn.softmax(attn, axis=-1)
        out = jnp.einsum('abhqk,bhkd->abhqd', attn, v)
        out = jnp.swapaxes(out, 1, 2).reshape(B, N, D)
        out = out @ proj_w.T + proj_b
        return out

    def _L0_attn_b_ref(residual, Wq, Wk, Wv, Wo, bq, bk, bv, bo):
        import jax, jax.numpy as jnp
        import numpy as np
        B, S, D, H, A = (2, 256, 128, 16, 64)
        INIT_STD = 0.02
        q = jnp.einsum('bsd,hda->bhsa', residual, Wq) + bq[None, :, None, :]
        k = jnp.einsum('bsd,hda->bhsa', residual, Wk) + bk[None, :, None, :]
        v = jnp.einsum('bsd,hda->bhsa', residual, Wv) + bv[None, :, None, :]
        scale = 1.0 / jnp.sqrt(jnp.float32(q.shape[-1]))
        scores = jnp.einsum('bhsa,bhta->bhst', q, k) * scale
        s = scores.shape[-1]
        causal = jnp.tril(jnp.ones((s, s), dtype=bool))
        masked = jnp.where(causal, scores, jnp.float32(-100000.0))
        pattern = jax.nn.softmax(masked, axis=-1)
        z = jnp.einsum('bhst,bhta->bshа'.replace('а', 'a'), pattern, v)
        out = jnp.einsum('bsha,had->bsd', z, Wo) + bo
        return out

    def _L0_ffn_ref(x, ln_gamma, ln_beta, fc1_q, fc1_scales, fc1_bias, fc2_q, fc2_scales, fc2_bias):
        import jax, jax.numpy as jnp
        import numpy as np
        B, S, H, F, G = (8, 256, 128, 512, 128)
        EPS = 1e-05

        def _dequant(q, scales, g):
            K, N = q.shape
            w = (q.astype(jnp.float32) - 128.0).reshape(K // g, g, N) * scales[:, None, :]
            return w.reshape(K, N)
        residual = x
        mu = jnp.mean(x, axis=-1, keepdims=True)
        var = jnp.mean(jnp.square(x - mu), axis=-1, keepdims=True)
        h = (x - mu) * jax.lax.rsqrt(var + EPS) * ln_gamma + ln_beta
        hf = h.reshape(-1, H)
        w1 = _dequant(fc1_q, fc1_scales, G)
        y = hf @ w1 + fc1_bias
        y = jax.nn.silu(y)
        w2 = _dequant(fc2_q, fc2_scales, G)
        z = y @ w2 + fc2_bias
        return residual + 0.5 * z.reshape(residual.shape)
    x = L0_attn_a_x
    x = x + _L0_attn_a_ref(_layernorm(x, axis=-1), L0_attn_a_qkv_w, L0_attn_a_qkv_b, L0_attn_a_proj_w, L0_attn_a_proj_b)
    x = x + _L0_ffn_ref(_layernorm(x, axis=-1), L0_ffn_ln_gamma, L0_ffn_ln_beta, L0_ffn_fc1_q, L0_ffn_fc1_scales, L0_ffn_fc1_bias, L0_ffn_fc2_q, L0_ffn_fc2_scales, L0_ffn_fc2_bias)
    x = x + _L0_attn_b_ref(_layernorm(x, axis=-1), L0_attn_b_Wq, L0_attn_b_Wk, L0_attn_b_Wv, L0_attn_b_Wo, L0_attn_b_bq, L0_attn_b_bk, L0_attn_b_bv, L0_attn_b_bo)
    x = x + _L0_ffn_ref(_layernorm(x, axis=-1), L0_ffn_ln_gamma, L0_ffn_ln_beta, L0_ffn_fc1_q, L0_ffn_fc1_scales, L0_ffn_fc1_bias, L0_ffn_fc2_q, L0_ffn_fc2_scales, L0_ffn_fc2_bias)
    return x

_drawn_inputs = setup_inputs


def setup_inputs(seed=0):
    import zlib

    import numpy as np

    out = dict(_drawn_inputs(seed))
    spreads = {'L0_attn_b_bq': (0.0, 0.8),
     'L0_attn_b_bk': (0.0, 2.0),
     'L0_attn_b_bv': (0.0, 0.8),
     'L0_attn_b_bo': (0.0, 2.0),
     'L0_ffn_ln_gamma': (1.0, 0.2),
     'L0_ffn_ln_beta': (0.0, 0.1)}
    factors = {'L0_attn_a_qkv_w': 8.0,
     'L0_attn_a_qkv_b': 8.0,
     'L0_attn_a_proj_w': 8.0,
     'L0_attn_a_proj_b': 8.0,
     'L0_attn_b_Wq': 8.0,
     'L0_attn_b_Wk': 8.0,
     'L0_attn_b_Wv': 8.0,
     'L0_attn_b_Wo': 8.0,
     'L0_ffn_fc1_bias': 8.0,
     'L0_ffn_fc2_bias': 37.275}
    for name, (base, spread) in spreads.items():
        noise = np.random.default_rng([zlib.crc32(name.encode()), seed]).standard_normal(out[name].shape)
        drawn = base * np.exp(spread * noise) if base else spread * noise
        out[name] = jnp.asarray(drawn.astype(out[name].dtype))
    for name, factor in factors.items():
        out[name] = (out[name] * factor).astype(out[name].dtype)
    return out
```

```python
from contextlib import ExitStack

import numpy as np

import concourse.bass as bass
from concourse import mybir

F32 = mybir.dt.float32
F32R = mybir.dt.float32r
BF16 = mybir.dt.bfloat16
I32 = mybir.dt.int32
ALU = mybir.AluOpType
ACT = mybir.ActivationFunctionType
AX = mybir.AxisListType

P = 128
D = 128
B, N = 8, 512
TT = N // P
BANK = 512
EPS = 1e-5
HA, DA = 16, 8
GH = 4
NG = HA // GH
HB, DB = 16, 64
NP = HB // 2
FF = 512
FT = FF // P
SCALE_A = float(DA) ** -0.5
SCALE_B = float(DB) ** -0.5
MASKED = -1e30


def fits(v):
    return not isinstance(v, int) or v > 0


def wait(eng, sem, v):
    if fits(v):
        eng.wait_ge(sem, v)


def waits(eng, met, *pairs):
    for _, n in pairs:
        if not isinstance(n, int):
            eng.compute_val(n)
    eng.wait_ge(*met)
    for sem, n in pairs:
        wait(eng, sem, n)


def mean_and_variance(nc, dve, stats_done, n, x_of_tile, stats, mv, consts):
    for t in range(TT):
        last = nc.vector.bn_stats(stats[:, t, :], x_of_tile(t))
    last.then_inc(stats_done, 1)
    waits(dve, consts, (stats_done, n + 1))
    for t in range(TT):
        last = nc.vector.bn_aggr(mv[:, t, :], stats[:, t, :])
    return last


def inverse_root(nc, pool, step, n, mv, ve, minus_half, out):
    nc.gpsimd.tensor_scalar(ve[:], mv[:, :, 1], EPS, None, ALU.add).then_inc(step, 1)
    pool.wait_ge(step, n + 2)
    return nc.gpsimd.tensor_tensor(out[:], ve[:], minus_half[:], ALU.pow)


def normalize(nc, x_of_tile, out, mv, rstd):
    for t in range(TT):
        last = nc.vector.tensor_scalar(out[:, t, :], x_of_tile(t), mv[:, t, 0:1], rstd[:, t:t + 1],
                                       ALU.subtract, ALU.mult)
    return last


def phase_a_inputs(nc, X, IDENT, d, scratch):
    q_d, k_d, v_d = scratch
    with ExitStack() as ctx:
        sb = lambda n, s, t: ctx.enter_context(nc.sbuf_tensor(n, s, t))
        ps = lambda n, s, t: ctx.enter_context(nc.psum_tensor(n, s, t))
        sem = lambda n: ctx.enter_context(nc.semaphore(n))
        W = sb("wa_raw", [P, 5, P], F32)
        WH = sb("wa_hi", [P, 4, P], F32R)
        WL = sb("wa_lo", [P, 4, P], F32R)
        BQK = sb("qk_bias", [P, 4], F32)
        BV = sb("v_bias", [P, P], F32)
        ROT = sb("rotary", [P, 2, N], F32)
        stats = sb("ln_stats", [P, TT, 6], F32)
        mv = sb("ln_mv", [P, TT, 2], F32)
        ve = sb("ln_var_eps", [P, TT], F32)
        minus_half = sb("minus_half", [P, TT], F32)
        rstd = sb("ln_rstd", [P, TT], F32)
        XN = sb("xn", [P, TT, P], F32)
        XT = sb("xt", [P, N], F32)
        XTH = sb("xt_hi", [P, N], F32R)
        XTL = sb("xt_lo", [P, N], F32R)
        T1 = sb("rot_cos", [P, 2, N], F32)
        T2 = sb("rot_sin", [P, 2, N], F32)
        QK = sb("qk_full", [P, 2, N], F32)
        QKH = sb("qk_hi", [P, 2, N], F32R)
        QKL = sb("qk_lo", [P, 2, N], F32R)
        V = sb("v_rows", [P, NG, TT, GH, 32], F32)
        pT = ps("p_xt", [P, N], F32)
        pQ = ps("p_qk", [P, 4, N], F32)
        pV = ps("p_v", [P, TT, P], F32)

        w_in = sem("a0_w_in")
        x_in = sem("a0_x_in")
        w_split = sem("a0_w_split")
        v_ready0 = sem("a0_v_const")
        ln_stats = sem("a0_ln_stats")
        ln_mv = sem("a0_ln_mv")
        ln_rstd = sem("a0_ln_rstd")
        root_step = sem("a0_root_step")
        xn_ready = sem("a0_xn")
        xt_ready = sem("a0_xt_psum")
        xt_copied = sem("a0_xt_copied")
        xt_split = sem("a0_xt_split")
        v_done = sem("a0_v_psum")
        qk_done = sem("a0_qk_psum")
        rot_done = sem("a0_rot")
        qk_sum = sem("a0_qk_sum")
        qk_hi = sem("a0_qk_hi")
        qk_lo = sem("a0_qk_lo")
        v_out = sem("a0_v_sbuf")
        stored_h = sem("a0_hi_stored")
        stored_l = sem("a0_lo_stored")
        stored_v = sem("a0_v_stored")

        block = ctx.enter_context(nc.Block())

        def each_batch(eng, batch):
            batch(0)
            with eng.Fori(1, B) as c:
                batch(c)

        @block.sync
        def _(sp):
            sp.dma_start(W[:], d["wa"]).then_inc(w_in, 16)
            for c in range(B):
                sp.dma_start(X[:, c * TT:(c + 1) * TT, :],
                             d["x"][c].rearrange("(t p) d -> p t d", p=P)).then_inc(x_in, 16)
                sp.wait_ge(x_in, 16 * (c + 1))
            def batch(c):
                for qk, dst in ((0, q_d), (1, k_d)):
                    sp.wait_ge(qk_hi, c * 2 + qk + 1)
                    for j in ((0, 3), (0, 2))[qk]:
                        sp.dma_start(dst[c, :, j * DA:(j + 1) * DA, :], QKH[:, qk, :].bitcast(F32))\
                            .then_inc(stored_h, 16)
                    sp.wait_ge(qk_lo, c * 2 + qk + 1)
                    for j in ((1, 2), (1, 3))[qk]:
                        sp.dma_start(dst[c, :, j * DA:(j + 1) * DA, :], QKL[:, qk, :].bitcast(F32))\
                            .then_inc(stored_l, 16)
                sp.wait_ge(v_out, c + 1)
                sp.dma_start(v_d[c], V[:]).then_inc(stored_v, 16)

            each_batch(sp, batch)
            sp.wait_ge(stored_h, 64 * B)
            sp.wait_ge(stored_l, 64 * B)
            sp.wait_ge(stored_v, 16 * B)

        @block.scalar
        def _(act):
            act.dma_start(BQK[:], d["bqk"]).then_inc(w_in, 16)
            act.dma_start(BV[:], d["bv"].partition_broadcast(P)).then_inc(w_in, 16)
            act.dma_start(ROT[:], d["rot"]).then_inc(w_in, 16)
            act.dma_start(IDENT[:], d["ident"]).then_inc(w_in, 16)

            def batch(c):
                act.wait_ge(xt_ready, c + 1)
                wait(act, v_done, c)
                wait(act, qk_done, c * 4)
                nc.scalar.activation(XT[:], pT[:], ACT.Copy).then_inc(xt_copied, 1)
                nc.scalar.activation(XTH[:], pT[:], ACT.Copy).then_inc(xt_copied, 1)
                for qk in range(2):
                    act.wait_ge(qk_sum, c * 2 + qk + 1)
                    wait(act, stored_h, c * 64)
                    nc.scalar.activation(QKH[:, qk, :], QK[:, qk, :], ACT.Copy).then_inc(qk_hi, 1)

            each_batch(act, batch)

        @block.gpsimd
        def _(pool):
            nc.gpsimd.memset(V[:], 0.0).then_inc(v_ready0, 1)
            pool.wait_ge(v_ready0, 1)
            nc.gpsimd.memset(V[:, :, :, :, DA:DA + 1], 1.0).then_inc(v_ready0, 1)

            def root(c):
                waits(pool, (root_step, 1), (ln_mv, c + 1))
                inverse_root(nc, pool, root_step, c, mv, ve, minus_half, rstd).then_inc(ln_rstd, 1)

            def rest(c, ahead):
                if ahead:
                    root(c + 1)
                for qk in range(2):
                    pool.wait_ge(rot_done, c * 2 + qk + 1)
                    wait(pool, qk_hi, c * 2)
                    nc.gpsimd.tensor_tensor(QK[:, qk, :], T1[:, qk, :], T2[:, qk, :], ALU.add)\
                        .then_inc(qk_sum, 1)
                for qk in range(2):
                    pool.wait_ge(qk_hi, c * 2 + qk + 1)
                    wait(pool, stored_l, c * 64)
                    nc.gpsimd.tensor_tensor(QKL[:, qk, :], QK[:, qk, :], QKH[:, qk, :].bitcast(F32),
                                            ALU.subtract).then_inc(qk_lo, 1)

            nc.gpsimd.memset(minus_half[:], -0.5).then_inc(root_step, 1)
            root(0)
            rest(0, True)
            with pool.Fori(1, B - 1) as c:
                rest(c, True)
            rest(B - 1, False)

        @block.tensor
        def _(pe):
            pe.wait_ge(w_in, 80)
            pe.wait_ge(w_split, 2)
            def batch(c):
                pe.wait_ge(xn_ready, c + 1)
                wait(pe, xt_split, c)
                for t in range(TT):
                    last = nc.tensor.transpose(pT[:, t * P:(t + 1) * P], XN[:, t, :], IDENT[:])
                last.then_inc(xt_ready, 1)
                pe.wait_ge(xt_copied, c * 2 + 1)
                wait(pe, v_out, c)
                for t in range(TT):
                    last = nc.tensor.matmul(pV[:, t, :], XT[:, t * P:(t + 1) * P], W[:, 4, :],
                                            start=True, stop=True)
                last.then_inc(v_done, 1)
                pe.wait_ge(xt_copied, c * 2 + 2)
                pe.wait_ge(xt_split, c + 1)
                for j in range(4):
                    wait(pe, rot_done, (c * 2 if j < 2 else c * 2))
                    nc.tensor.matmul(pQ[:, j, :], WH[:, j, :], XTH[:], start=True, stop=False)
                    nc.tensor.matmul(pQ[:, j, :], WL[:, j, :], XTH[:], start=False, stop=False)
                    nc.tensor.matmul(pQ[:, j, :], WH[:, j, :], XTL[:], start=False, stop=True)\
                        .then_inc(qk_done, 1)

            each_batch(pe, batch)

        @block.vector
        def _(dve):
            def stage_ln(c):
                waits(dve, (w_in, 80), (x_in, (c + 1) * 16))
                x = lambda t: X[:, c * TT + t, :]
                mean_and_variance(nc, dve, ln_stats, c, x, stats, mv, (w_in, 80)).then_inc(ln_mv, 1)
                dve.wait_ge(ln_rstd, c + 1)
                wait(dve, xt_ready, c)
                normalize(nc, x, XN, mv, rstd).then_inc(xn_ready, 1)

            def stage_rest(c, ahead):
                dve.wait_ge(xt_copied, c * 2 + 2)
                wait(dve, qk_done, c * 4)
                nc.vector.tensor_tensor(XTL[:], pT[:], XTH[:].bitcast(F32), ALU.subtract)\
                    .then_inc(xt_split, 1)
                if ahead:
                    stage_ln(c + 1)
                dve.wait_ge(v_done, c + 1)
                wait(dve, stored_v, c * 16)
                for g in range(NG):
                    src = pV[:, :, g * 32:(g + 1) * 32].rearrange("p t (h d) -> p t h d", h=GH)
                    bias = BV[:, g * 32:(g + 1) * 32].rearrange("p (h d) -> p h d", h=GH)
                    for t in range(TT):
                        last = nc.vector.tensor_tensor(V[:, g, t, :, 0:DA], src[:, t], bias, ALU.add)
                last.then_inc(v_out, 1)
                for qk in range(2):
                    dve.wait_ge(qk_done, c * 4 + qk * 2 + 1)
                    wait(dve, qk_sum, c * 2)
                    nc.vector.scalar_tensor_tensor(T1[:, qk, :], pQ[:, 2 * qk, :], BQK[:, 2 * qk:2 * qk + 1],
                                                   ROT[:, 0, :], ALU.add, ALU.mult)
                    dve.wait_ge(qk_done, c * 4 + qk * 2 + 2)
                    nc.vector.scalar_tensor_tensor(T2[:, qk, :], pQ[:, 2 * qk + 1, :],
                                                   BQK[:, 2 * qk + 1:2 * qk + 2],
                                                   ROT[:, 1, :], ALU.add, ALU.mult).then_inc(rot_done, 1)

            dve.wait_ge(w_in, 80)
            nc.vector.tensor_copy(WH[:], W[:, 0:4, :]).then_inc(w_split, 1)
            dve.wait_ge(w_split, 1)
            nc.vector.tensor_tensor(WL[:], W[:, 0:4, :], WH[:].bitcast(F32), ALU.subtract).then_inc(w_split, 1)
            dve.wait_ge(v_ready0, 2)
            stage_ln(0)
            stage_rest(0, True)
            with dve.Fori(1, B - 1) as c:
                stage_rest(c, True)
            stage_rest(B - 1, False)


def phase_a_attention(nc, IDENT, d, scratch, o_d):
    q_d, k_d, v_d = scratch
    SLOTS = B * NG
    with ExitStack() as ctx:
        sb = lambda n, s, t: ctx.enter_context(nc.sbuf_tensor(n, s, t))
        ps = lambda n, s, t: ctx.enter_context(nc.psum_tensor(n, s, t))
        sem = lambda n: ctx.enter_context(nc.semaphore(n))
        KR = 96
        Q = [sb(f"q_stack{g}", [KR, GH, N], F32R) for g in range(NG)]
        K = [sb(f"k_stack{g}", [KR, GH, N], F32R) for g in range(NG)]
        V = [sb(f"v_stack{g}", [P, TT, GH, 32], F32) for g in range(NG)]
        PR = [sb(f"probs{kt}", [P, GH, N], F32) for kt in range(TT)]
        NM = [sb(f"neg_max{r}", [P, TT, GH], F32) for r in range(2)]
        NMF = sb("neg_max_rows", [GH, N], F32)
        ZERO = sb("zero", [GH, N], F32)
        NMH = sb("neg_max_hi", [GH, N], F32R)
        NML = sb("neg_max_lo", [GH, N], F32R)
        OT = sb("o_t", [P, N], F32)
        SEL = sb("select_rows", [P, 36], F32)
        RD = sb("recip_den", [P, 4, GH], F32)
        OX = [sb(f"o_rows{r}", [32, GH, 16, DA], F32) for r in range(2)]
        pM = ps("p_max", [P, 2, N], F32)
        pS = [ps(f"p_scores{u}", [P, 2, N], F32) for u in range(2)]
        pO = ps("p_out", [P, N], F32)
        pX = ps("p_misc", [P, N], F32)

        stacks_set = sem("a_stacks_set")
        loaded = [sem(f"a_loaded{g}") for g in range(NG)]
        rows_in = [sem(f"a_rows{g}") for g in range(NG)]
        sm_filled = sem("a_sm_filled")
        sm_reduced = sem("a_sm_reduced")
        nm_turned = sem("a_nm_turned")
        nm_copied = sem("a_nm_copied")
        nm_split = sem("a_nm_split")
        st_filled = sem("a_st_filled")
        exp_done = sem("a_exp")
        pv_done = sem("a_pv")
        ot_copied = sem("a_ot_copied")
        o_turned = sem("a_o_turned")
        o_recip = sem("a_o_recip")
        o_done = sem("a_o_done")
        sel_in = sem("a_sel_in")
        zero_set = sem("a_zero_set")
        o_stored = [sem(f"a_o_stored{r}") for r in range(2)]

        block = ctx.enter_context(nc.Block())

        def batch_of(s_b, g, ahead):
            j = g + ahead
            return s_b + j // NG, j % NG

        def over_batches(eng, body):
            body(0, True, False)
            with eng.Fori(1, B - 1) as b:
                body(b, False, False)
            body(B - 1, False, True)

        @block.sync
        def _(sp):
            sp.wait_ge(stacks_set, 5)

            def load(b, g):
                wait(sp, pv_done, (b * NG + g - NG) * TT + TT)
                sp.dma_start(Q[g][0:32].bitcast(F32), q_d[b, g * GH:(g + 1) * GH].rearrange("h r n -> r h n"))\
                    .then_inc(loaded[g], 16)
                sp.dma_start(K[g][0:32].bitcast(F32), k_d[b, g * GH:(g + 1) * GH].rearrange("h r n -> r h n"))\
                    .then_inc(loaded[g], 16)
                sp.dma_start(V[g][:], v_d[b, :, g]).then_inc(loaded[g], 16)

            def rows(b, g):
                n = b * NG + g
                sp.wait_ge(nm_split, n * 2 + 1)
                sp.dma_start(Q[g][32:33].bitcast(F32), NMH[:].bitcast(F32)).then_inc(rows_in[g], 16)
                sp.wait_ge(nm_split, n * 2 + 2)
                sp.dma_start(Q[g][33:34].bitcast(F32), NML[:].bitcast(F32)).then_inc(rows_in[g], 16)

            def store(b, g):
                sp.wait_ge(o_done, b * NG + g + 1)
                sp.dma_start(o_d[g * GH:(g + 1) * GH, b].rearrange("h r c -> r h c"),
                             OX[g % 2][:].rearrange("r h j d -> r h (j d)")).then_inc(o_stored[g % 2], 16)

            sp.dma_start(SEL[:], d["sel"]).then_inc(sel_in, 16)
            for g in range(NG):
                load(0, g)
                if g >= 2:
                    rows(0, g - 2)
            with sp.Fori(1, B) as b:
                for g in range(NG):
                    load(b, g)
                    rows(*batch_of(b, g, -2))
                    store(*batch_of(b, g, -4))
            for g in range(NG):
                if g < 2:
                    rows(B - 1, g + 2)
                store(B - 1, g)
            for r in range(2):
                sp.wait_ge(o_stored[r], B * NG // 2 * 16)

        @block.gpsimd
        def _(pool):
            def split(b, g):
                n = b * NG + g
                pool.wait_ge(nm_copied, n + 1)
                pb, pg = batch_of(b, g, -1)
                wait(pool, rows_in[pg], (pb + 1) * 32)
                nc.gpsimd.tensor_tensor(NMH[:], NMF[:], ZERO[:], ALU.add).then_inc(nm_split, 1)
                pool.wait_ge(nm_split, n * 2 + 1)
                nc.gpsimd.tensor_tensor(NML[:], NMF[:], NMH[:].bitcast(F32), ALU.subtract).then_inc(nm_split, 1)

            nc.gpsimd.memset(ZERO[:], 0.0).then_inc(zero_set, 1)
            pool.wait_ge(zero_set, 1)
            for g in range(NG):
                split(0, g)
            with pool.Fori(1, B) as b:
                for g in range(NG):
                    split(b, g)

        @block.tensor
        def _(pe):
            def smax_unit(b, g, h, qt):
                n = (b * NG + g) * 16 + h * TT + qt
                if h == 0 and qt == 0:
                    pe.wait_ge(loaded[g], (b + 1) * 48)
                wait(pe, sm_reduced, n - 1)
                nc.tensor.matmul(pM[:, qt % 2, :], Q[g][0:32, h, qt * P:(qt + 1) * P], K[g][0:32, h, :],
                                 start=True, stop=True).then_inc(sm_filled, 1)

            def st_unit(b, g, kt, u):
                n = (b * NG + g) * 8 + kt * 2 + u
                if kt == 0 and u == 0:
                    pe.wait_ge(rows_in[g], (b + 1) * 32)
                wait(pe, exp_done, n - 1)
                for j in range(2):
                    last = nc.tensor.matmul(pS[u][:, j, :], K[g][:, 2 * u + j, kt * P:(kt + 1) * P],
                                            Q[g][:, 2 * u + j, :], start=True, stop=True)
                last.then_inc(st_filled, 1)

            def pv(b, g, kt):
                s = b * NG + g
                pe.wait_ge(exp_done, s * 8 + kt * 2 + 2)
                if kt == 0:
                    wait(pe, ot_copied, s)
                for h in range(GH):
                    last = nc.tensor.matmul(pO[32 * h:32 * h + 32, :], V[g][:, kt, h, :], PR[kt][:, h, :],
                                            start=(kt == 0), stop=(kt == TT - 1), skip_group_check=True)
                last.then_inc(pv_done, 1)

            def turn_max(b, g):
                s = b * NG + g
                pe.wait_ge(sm_reduced, s * 16 + 16)
                wait(pe, o_done, s - 2)
                for qt in range(TT):
                    last = nc.tensor.transpose(pX[0:GH, qt * P:(qt + 1) * P], NM[g % 2][:, qt, :], IDENT[:])
                last.then_inc(nm_turned, 1)

            def turn_out(b, g, next_turned):
                s = b * NG + g
                pe.wait_ge(ot_copied, s + 1)
                if next_turned:
                    pe.wait_ge(nm_copied, s + 3)
                else:
                    pe.wait_ge(o_done, s)
                tokens = OT[:].rearrange("p (r j) -> p j r", j=16)
                for j in range(16):
                    m = 32 * (j % 4)
                    last = nc.tensor.matmul(pX[m:m + 32, (j // 4) * 36:(j // 4 + 1) * 36], tokens[:, j, :], SEL[:],
                                            start=True, stop=True)
                last.then_inc(o_turned, 1)

            def body(b, first, last):
                for g in range(NG):
                    b2, g2 = batch_of(b, g, 2)
                    b1, g1 = batch_of(b, g, 1)
                    b0, g0 = batch_of(b, g, -1)
                    ahead = not (last and g >= NG - 2)
                    for kt in range(TT):
                        if ahead:
                            smax_unit(b2, g2, kt, 0)
                        st_unit(b, g, kt, 0)
                        if ahead:
                            smax_unit(b2, g2, kt, 1)
                        if kt == 0 and not (last and g == NG - 1):
                            turn_max(b1, g1)
                        if kt > 0:
                            pv(b, g, kt - 1)
                        if ahead:
                            smax_unit(b2, g2, kt, 2)
                        st_unit(b, g, kt, 1)
                        if kt == 1 and not (first and g == 0):
                            turn_out(b0, g0, not (last and g == NG - 1))
                        if ahead:
                            smax_unit(b2, g2, kt, 3)
                    pv(b, g, TT - 1)

            pe.wait_ge(sel_in, 16)
            for h in range(GH):
                for qt in range(TT):
                    smax_unit(0, 0, h, qt)
            for h in range(GH):
                for qt in range(TT):
                    smax_unit(0, 1, h, qt)
                if h == 0:
                    turn_max(0, 0)
            over_batches(pe, body)
            turn_out(B - 1, NG - 1, False)

        @block.scalar
        def _(act):
            def exp_unit(b, g, kt, u):
                s = b * NG + g
                act.wait_ge(st_filled, s * 8 + kt * 2 + u + 1)
                if u == 0:
                    wait(act, pv_done, (s - 1) * TT + kt + 1)
                nc.scalar.activation(PR[kt][:, 2 * u:2 * u + 2, :], pS[u][:], ACT.Exp, scale=SCALE_A)\
                    .then_inc(exp_done, 1)

            def copy_max(b, g):
                s = b * NG + g
                act.wait_ge(nm_turned, s + 1)
                wait(act, nm_split, s * 2)
                nc.scalar.activation(NMF[:], pX[0:GH, :], ACT.Copy).then_inc(nm_copied, 1)

            def copy_out(b, g):
                s = b * NG + g
                act.wait_ge(pv_done, s * TT + TT)
                wait(act, o_turned, s)
                nc.scalar.activation(OT[:], pO[:], ACT.Copy).then_inc(ot_copied, 1)

            def body(b, first, last):
                for g in range(NG):
                    for kt in range(TT):
                        exp_unit(b, g, kt, 0)
                        if kt == 0 and not (first and g == 0):
                            copy_out(*batch_of(b, g, -1))
                        exp_unit(b, g, kt, 1)
                        if kt == 0 and not (last and g == NG - 1):
                            copy_max(*batch_of(b, g, 1))

            copy_max(0, 0)
            over_batches(act, body)
            copy_out(B - 1, NG - 1)

        @block.vector
        def _(dve):
            def reduce_unit(b, g, h, qt):
                s = b * NG + g
                dve.wait_ge(sm_filled, s * 16 + h * TT + qt + 1)
                if h == 0 and qt == 0:
                    wait(dve, nm_turned, s - 1)
                nc.vector.tensor_reduce(NM[g % 2][:, qt, h:h + 1], pM[:, qt % 2, :], AX.X, ALU.max,
                                        negate=True).then_inc(sm_reduced, 1)

            def finish(b, g):
                s = b * NG + g
                dve.wait_ge(o_turned, s + 1)
                o = pX[:, 0:4 * 36].rearrange("p (k c) -> p k c", k=4)
                nc.vector.reciprocal(RD[:], o[:, :, 32:36]).then_inc(o_recip, 1)
                dve.wait_ge(o_recip, s + 1)
                pb, pg = batch_of(b, g, -2)
                wait(dve, o_stored[g % 2], (pb * 2 + pg // 2 + 1) * 16)
                for m in range(4):
                    part = slice(32 * m, 32 * m + 32)
                    dst = OX[g % 2][:, :, m:16:4, :].rearrange("r h k d -> r k h d")
                    last = nc.vector.tensor_tensor(dst, o[part, :, 0:32].rearrange("p k (h d) -> p k h d", h=GH),
                                                   RD[part].unsqueeze(3).broadcast_to([32, 4, GH, DA]), ALU.mult)
                last.then_inc(o_done, 1)

            def body(b, first, last):
                for g in range(NG):
                    ahead = not (last and g >= NG - 2)
                    for h in range(GH):
                        if ahead:
                            for qt in range(TT):
                                reduce_unit(*batch_of(b, g, 2), h, qt)
                        if h == 1 and not (first and g == 0):
                            finish(*batch_of(b, g, -1))

            for g in range(NG):
                nc.vector.memset(Q[g][:].bitcast(F32), 0.0)
                last = nc.vector.memset(K[g][:].bitcast(F32), 0.0)
            last.then_inc(stacks_set, 1)
            dve.wait_ge(stacks_set, 1)
            for g in range(NG):
                nc.vector.memset(K[g][32:34].bitcast(F32), 1.0).then_inc(stacks_set, 1)
            for g in range(2):
                for h in range(GH):
                    for qt in range(TT):
                        reduce_unit(0, g, h, qt)
            over_batches(dve, body)
            finish(B - 1, NG - 1)

def phase_ffn(nc, X, IDENT, d, name, attn=None, tail=None, out=None):
    with ExitStack() as ctx:
        sb = lambda n, s, t: ctx.enter_context(nc.sbuf_tensor(f"{name}_{n}", s, t))
        ps = lambda n, s, t: ctx.enter_context(nc.psum_tensor(f"{name}_{n}", s, t))
        sem = lambda n: ctx.enter_context(nc.semaphore(f"{name}_{n}"))
        Q1 = sb("fc1_q", [P, FF], I32)
        S1 = sb("fc1_scale", [P, FF], F32)
        W1 = sb("fc1_w", [P, FF], F32)
        W1H = sb("fc1_hi", [P, FF], F32R)
        W1L = sb("fc1_lo", [P, FF], F32R)
        Q2 = sb("fc2_q", [P, FT, P], I32)
        S2 = sb("fc2_scale", [P, FT, P], F32)
        W2 = sb("fc2_w", [P, FT, P], F32)
        GB = sb("gamma_beta", [P, 2], F32)
        B1 = sb("fc1_bias", [P, FT], F32)
        B2 = sb("fc2_bias", [P, P], F32)
        stats = sb("ln_stats", [P, TT, 6], F32)
        mv = sb("ln_mv", [P, TT, 2], F32)
        root = [sb(f"ln_root{k}", [P, TT], F32) for k in range(6)]
        minus_half = sb("minus_half", [P, TT], F32)
        XN = sb("xn", [P, TT, P], F32)
        H = sb("h", [P, TT, P], F32)
        XS = sb("xn_bias", [P, TT, P], F32)
        XR = sb("residual", [P, TT, P], F32)
        HT = sb("ht", [P, N], F32)
        HTH = sb("ht_hi", [P, N], F32R)
        HTL = sb("ht_lo", [P, N], F32R)
        Y = sb("silu", [P, FT, N], F32)
        pT = ps("p_t", [P, N], F32)
        pF = ps("p_f", [P, 2, N], F32)
        pZ = ps("p_z", [P, TT, P], F32)

        w_in = sem("w_in")
        w_deq = sem("w_deq")
        w_split = sem("w_split")
        pool_set = sem("pool_set")
        ln_stats = sem("ln_stats")
        ln_mv = sem("ln_mv")
        ln_root = sem("ln_root")
        ln_rstd = sem("ln_rstd")
        h_ready = sem("h")
        xn_ready = sem("xn")
        ht_turned = sem("ht_turned")
        ht_full = sem("ht_full")
        ht_hi = sem("ht_hi")
        ht_lo = sem("ht_lo")
        fc1_done = sem("fc1")
        silu_done = sem("silu")
        fc2_done = sem("fc2")
        xs_ready = sem("xn_plus_bias")
        xr_ready = sem("residual")
        x_new = sem("x_new")
        W_LOADS = 7
        if attn is not None:
            o_d = attn
            WP = sb("proj_w", [P, P], F32)
            PB = sb("proj_b", [P, P], F32)
            OT = sb("o_t", [P, N], F32)
            pP = ps("p_proj", [P, TT, P], F32)
            OC = sb("o_now", [P, TT, P], F32)
            oc_in = sem("oc_in")
            biased = sem("x_biased")
            ot_turned = sem("ot_turned")
            ot_copied = sem("ot_copied")
            proj_done = sem("proj")
            x_mid = sem("x_mid")
            W_LOADS += 2
        if tail is not None:
            XTH_all, XTL_all, v_d = tail
            WV = sb("v_w", [P, HB * DB], F32)
            WVH = sb("v_w_hi", [P, HB * DB], F32R)
            WVL = sb("v_w_lo", [P, HB * DB], F32R)
            WO = sb("o_w", [P, NP, P], F32)
            BV = sb("v_b", [P, NP], F32)
            BVB = sb("v_b_wide", [P, NP, P], F32)
            BO = sb("o_b", [P, P], F32)
            BOV = sb("o_b_total", [P, P], F32)
            stats3 = sb("ln3_stats", [P, TT, 6], F32)
            mv3 = sb("ln3_mv", [P, TT, 2], F32)
            ve3 = sb("ln3_ve", [P, TT], F32)
            rstd3 = sb("ln3_rstd", [P, TT], F32)
            XN3 = sb("xn3", [P, TT, P], F32)
            XTH = sb("xt_hi", [P, N], F32R)
            XTL = sb("xt_lo", [P, N], F32R)
            V = sb("v", [P, TT, HB * DB], F32)
            pT3 = ps("p_t3", [P, N], F32)
            pV = ps("p_v", [P, 2, N], F32)
            bias_wide = sem("bias_wide")
            bias_sum = sem("bias_sum")
            bias_total = sem("bias_total")
            ln3_stats = sem("ln3_stats")
            ln3_mv = sem("ln3_mv")
            ln3_root = sem("ln3_root")
            ln3_rstd = sem("ln3_rstd")
            xn3_ready = sem("xn3")
            x_out_biased = sem("x_out_biased")
            xt_turned = sem("xt_turned")
            xt_hi = sem("xt_hi")
            xt_lo = sem("xt_lo")
            v_mm = sem("v_mm")
            v_act = sem("v_act")
            v_dve = sem("v_dve")
            xt_kept = sem("xt_kept")
            v_stored = sem("v_stored")
            W_LOADS += 4
        stored = sem("stored")

        block = ctx.enter_context(nc.Block())

        def tiles(c):
            return bass.ds(c * TT, TT) if not isinstance(c, int) else slice(c * TT, c * TT + TT)

        def over_batches(eng, first, ahead, body, behind):
            first(0)
            body(0, True, False)
            with eng.Fori(1, B - 1) as c:
                body(c, True, True)
            body(B - 1, False, True)
            behind(B - 1)

        @block.sync
        def _(sp):
            sp.dma_start(Q1[:], d["fc1_q"]).then_inc(w_in, 16)
            sp.dma_start(S1[:], d["fc1_s"].partition_broadcast(P)).then_inc(w_in, 16)
            sp.dma_start(Q2[:], d["fc2_q"].rearrange("(f p) n -> p f n", p=P)).then_inc(w_in, 16)
            sp.dma_start(S2[:], d["fc2_s"].partition_broadcast(P)).then_inc(w_in, 16)
            sp.dma_start(GB[:], d["gb"]).then_inc(w_in, 16)
            sp.dma_start(B1[:], d["b1"]).then_inc(w_in, 16)
            sp.dma_start(B2[:], d["b2"].partition_broadcast(P)).then_inc(w_in, 16)
            if attn is not None:
                sp.dma_start(WP[:], d["wp"]).then_inc(w_in, 16)
                sp.dma_start(PB[:], d["bp"].partition_broadcast(P)).then_inc(w_in, 16)
            if tail is not None:
                sp.dma_start(WV[:], d["wv2"]).then_inc(w_in, 16)
                sp.dma_start(WO[:], d["wo"].rearrange("(p r) n -> r p n", r=P)).then_inc(w_in, 16)
                sp.dma_start(BV[:], d["bv2"]).then_inc(w_in, 16)
                sp.dma_start(BO[:], d["bo"].partition_broadcast(P)).then_inc(w_in, 16)

            if attn is not None:
                o_rows = o_d.rearrange("(c a) b r n -> c (a b r) n", c=B)

            def load_o(c):
                if attn is not None:
                    wait(sp, ot_turned, c)
                    sp.dma_start(OC[:], o_rows[c].rearrange("(t p) n -> p t n", p=P)).then_inc(oc_in, 16)

            def keep(c):
                if tail is not None:
                    waits(sp, (w_in, 16 * W_LOADS), (xt_hi, c + 1))
                    sp.dma_start(XTH_all[:, bass.ds(c * N, N)].bitcast(F32), XTH[:].bitcast(F32)).then_inc(xt_kept, 16)
                    waits(sp, (w_in, 16 * W_LOADS), (xt_lo, c + 1))
                    sp.dma_start(XTL_all[:, bass.ds(c * N, N)].bitcast(F32), XTL[:].bitcast(F32)).then_inc(xt_kept, 16)
                    for t in range(TT):
                        sp.wait_ge(v_act, c * TT + t + 1)
                        sp.wait_ge(v_dve, c * TT + t + 1)
                        sp.dma_start(v_d[c, :, :, t, :].rearrange("j p e -> p j e"),
                                     V[:, t, :].rearrange("p (j e) -> p j e", j=NP)).then_inc(v_stored, 16)

            def body(c, ahead, behind):
                if ahead:
                    load_o(c + 1)
                if behind:
                    keep(c - 1)

            if tail is not None:
                over_batches(sp, load_o, None, body, keep)
                sp.wait_ge(xt_kept, 32 * B)
                sp.wait_ge(v_stored, 16 * TT * B)
            if out is not None:
                with sp.Fori(0, B) as c:
                    sp.wait_ge(x_new, c + 1)
                    sp.dma_start(out[c].rearrange("(t p) d -> p t d", p=P), X[:, tiles(c), :]).then_inc(stored, 16)
                sp.wait_ge(stored, 16 * B)

        @block.gpsimd
        def _(pool):
            def bias_x(c):
                nc.gpsimd.tensor_tensor(X[:, tiles(c), :], X[:, tiles(c), :],
                                        PB[:].unsqueeze(1).broadcast_to([P, TT, P]), ALU.add).then_inc(biased, 1)

            def roots(c):
                def step(k, ins):
                    ins.then_inc(ln_root, 1)
                    waits(pool, (pool_set, 1), (ln_root, c * 5 + k))
                waits(pool, (pool_set, 1), (ln_mv, c + 1), (xn_ready, c))
                step(1, nc.gpsimd.tensor_scalar(root[0][:], mv[:, :, 1], EPS, None, ALU.add))
                step(2, nc.gpsimd.tensor_tensor(root[1][:], root[0][:], minus_half[:], ALU.pow))
                step(3, nc.gpsimd.tensor_tensor(root[2][:], root[1][:], root[1][:], ALU.mult))
                step(4, nc.gpsimd.tensor_tensor(root[3][:], root[2][:], mv[:, :, 1], ALU.mult))
                step(5, nc.gpsimd.tensor_scalar(root[4][:], root[3][:], EPS, None, ALU.add))
                nc.gpsimd.tensor_tensor(root[2][:], root[4][:], minus_half[:], ALU.pow).then_inc(ln_rstd, 1)
                pool.wait_ge(ln_rstd, c * 2 + 1)
                nc.gpsimd.tensor_tensor(root[5][:], root[2][:], root[1][:], ALU.mult).then_inc(ln_rstd, 1)

            def residual(c):
                pool.wait_ge(xn_ready, c + 1)
                nc.gpsimd.tensor_tensor(XS[:], XN[:], B2[:].unsqueeze(1).broadcast_to([P, TT, P]), ALU.add)\
                    .then_inc(xs_ready, 1)
                waits(pool, (pool_set, 1), (xs_ready, c + 1), (x_new, c))
                nc.gpsimd.tensor_tensor(XR[:], XS[:], X[:, tiles(c), :], ALU.add).then_inc(xr_ready, 1)

            def first(c):
                if attn is not None:
                    bias_x(c)
                roots(c)
                residual(c)

            def root3(c):
                waits(pool, (pool_set, 1), (ln3_mv, c + 1))
                nc.gpsimd.tensor_scalar(ve3[:], mv3[:, :, 1], EPS, None, ALU.add).then_inc(ln3_root, 1)
                pool.wait_ge(ln3_root, c + 1)
                nc.gpsimd.tensor_tensor(rstd3[:], ve3[:], minus_half[:], ALU.pow).then_inc(ln3_rstd, 1)

            def bias_out(c):
                waits(pool, (pool_set, 1), (xn3_ready, c + 1))
                nc.gpsimd.tensor_tensor(X[:, tiles(c), :], X[:, tiles(c), :],
                                        BOV[:].unsqueeze(1).broadcast_to([P, TT, P]), ALU.add)\
                    .then_inc(x_out_biased, 1)

            def body(c, ahead, behind):
                if ahead:
                    if attn is not None:
                        bias_x(c + 1)
                    roots(c + 1)
                if tail is not None:
                    root3(c)
                if ahead:
                    residual(c + 1)
                if tail is not None:
                    bias_out(c)

            nc.gpsimd.memset(minus_half[:], -0.5).then_inc(pool_set, 1)
            pool.wait_ge(pool_set, 1)
            pool.wait_ge(w_in, 16 * W_LOADS)
            pool.wait_ge(w_deq, 5)
            if tail is not None:
                pool.wait_ge(bias_total, 1)
            over_batches(pool, first, None, body, lambda c: None)

        @block.scalar
        def _(act):
            def copy_ot(c):
                act.wait_ge(ot_turned, c + 1)
                wait(act, proj_done, c)
                nc.scalar.activation(OT[:], pT[:], ACT.Copy).then_inc(ot_copied, 1)

            def copy_ht(c):
                act.wait_ge(ht_turned, c + 1)
                wait(act, ht_lo, c)
                wait(act, ht_hi, c)
                nc.scalar.activation(HT[:], pT[:], ACT.Identity, scale=GB[:, 0:1], bias=GB[:, 1:2])\
                    .then_inc(ht_full, 1)

            def silu(c, f):
                act.wait_ge(fc1_done, c * FT + f + 1)
                if f == 0:
                    wait(act, fc2_done, c)
                nc.scalar.activation(Y[:, f, :], pF[:, f % 2, :], ACT.Silu, bias=B1[:, f:f + 1])\
                    .then_inc(silu_done, 1)

            def turn_hi(c):
                act.wait_ge(xt_turned, c + 1)
                wait(act, v_mm, c * 8)
                wait(act, xt_kept, c * 32)
                nc.scalar.activation(XTH[:], pT3[:], ACT.Copy).then_inc(xt_hi, 1)

            def v_left(c, t):
                act.wait_ge(v_mm, c * 8 + t * 2 + 1)
                if t == 0:
                    wait(act, v_stored, c * 64)
                nc.scalar.activation(V[:, t, 0:N], pV[:, 0, :], ACT.Copy).then_inc(v_act, 1)

            def first(c):
                if attn is not None:
                    copy_ot(c)
                copy_ht(c)

            def body(c, ahead, behind):
                if behind and tail is not None:
                    turn_hi(c - 1)
                silu(c, 0)
                silu(c, 1)
                if ahead and attn is not None:
                    copy_ot(c + 1)
                silu(c, 2)
                silu(c, 3)
                if behind and tail is not None:
                    for t in range(TT):
                        v_left(c - 1, t)
                if ahead:
                    copy_ht(c + 1)

            def behind(c):
                if tail is not None:
                    turn_hi(c)
                    for t in range(TT):
                        v_left(c, t)

            act.wait_ge(w_in, 16 * W_LOADS)
            over_batches(act, first, None, body, behind)

        @block.tensor
        def _(pe):
            def turn_ot(c):
                pe.wait_ge(oc_in, (c + 1) * 16)
                wait(pe, ht_full, c)
                for t in range(TT):
                    last = nc.tensor.transpose(pT[:, t * P:(t + 1) * P], OC[:, t, :], IDENT[:])
                last.then_inc(ot_turned, 1)

            def project(c):
                pe.wait_ge(ot_copied, c + 1)
                wait(pe, x_mid, c)
                for t in range(TT):
                    last = nc.tensor.matmul(pP[:, t, :], OT[:, t * P:(t + 1) * P], WP[:], start=True, stop=True)
                last.then_inc(proj_done, 1)

            def turn_h(c):
                pe.wait_ge(h_ready, c + 1)
                if attn is not None:
                    pe.wait_ge(ot_copied, c + 1)
                else:
                    wait(pe, ht_full, c)
                for t in range(TT):
                    last = nc.tensor.transpose(pT[:, t * P:(t + 1) * P], H[:, t, :], IDENT[:])
                last.then_inc(ht_turned, 1)

            def fc1(c, f):
                if f == 0:
                    pe.wait_ge(ht_hi, c + 1)
                    pe.wait_ge(ht_lo, c + 1)
                wait(pe, silu_done, c * FT + f - 1)
                w = slice(f * P, (f + 1) * P)
                nc.tensor.matmul(pF[:, f % 2, :], W1H[:, w], HTH[:], start=True, stop=False)
                nc.tensor.matmul(pF[:, f % 2, :], W1L[:, w], HTH[:], start=False, stop=False)
                nc.tensor.matmul(pF[:, f % 2, :], W1H[:, w], HTL[:], start=False, stop=True).then_inc(fc1_done, 1)

            def fc2(c):
                pe.wait_ge(silu_done, c * FT + FT)
                wait(pe, x_new, c)
                for t in range(TT):
                    for f in range(FT):
                        last = nc.tensor.matmul(pZ[:, t, :], Y[:, f, t * P:(t + 1) * P], W2[:, f, :],
                                                start=(f == 0), stop=(f == FT - 1))
                last.then_inc(fc2_done, 1)

            def turn_xt(c):
                pe.wait_ge(xn3_ready, c + 1)
                wait(pe, xt_lo, c)
                for t in range(TT):
                    last = nc.tensor.transpose(pT3[:, t * P:(t + 1) * P], XN3[:, t, :], IDENT[:])
                last.then_inc(xt_turned, 1)

            def values(c, t):
                if t == 0:
                    pe.wait_ge(xt_hi, c + 1)
                    pe.wait_ge(xt_lo, c + 1)
                xt = slice(t * P, (t + 1) * P)
                for half in range(2):
                    w = slice(half * N, (half + 1) * N)
                    wait(pe, (v_act, v_dve)[half], c * TT + t)
                    nc.tensor.matmul(pV[:, half, :], XTH[:, xt], WVH[:, w], start=True, stop=False)
                    nc.tensor.matmul(pV[:, half, :], XTH[:, xt], WVL[:, w], start=False, stop=False)
                    nc.tensor.matmul(pV[:, half, :], XTL[:, xt], WVH[:, w], start=False, stop=True)\
                        .then_inc(v_mm, 1)

            def first(c):
                if attn is not None:
                    turn_ot(c)
                    project(c)
                turn_h(c)

            def body(c, ahead, behind):
                if behind and tail is not None:
                    turn_xt(c - 1)
                fc1(c, 0)
                fc1(c, 1)
                if ahead and attn is not None:
                    turn_ot(c + 1)
                fc1(c, 2)
                fc1(c, 3)
                if ahead and attn is not None:
                    project(c + 1)
                if behind and tail is not None:
                    values(c - 1, 0)
                    values(c - 1, 1)
                fc2(c)
                if behind and tail is not None:
                    values(c - 1, 2)
                    values(c - 1, 3)
                if ahead:
                    turn_h(c + 1)

            def behind(c):
                if tail is not None:
                    turn_xt(c)
                    for t in range(TT):
                        values(c, t)

            pe.wait_ge(w_split, 2 if tail is None else 4)
            pe.wait_ge(w_in, 16 * W_LOADS)
            if tail is not None:
                pe.wait_ge(bias_wide, 1)
                for j in range(NP):
                    last = nc.tensor.matmul(pV[:, 0, 0:P], BVB[:, j, :], WO[:, j, :], start=(j == 0), stop=(j == NP - 1))
                last.then_inc(bias_sum, 1)
                pe.wait_ge(bias_total, 1)
            over_batches(pe, first, None, body, behind)

        @block.vector
        def _(dve):
            def x_middle(c):
                dve.wait_ge(proj_done, c + 1)
                dve.wait_ge(biased, c + 1)
                nc.vector.tensor_tensor(X[:, tiles(c), :], pP[:], X[:, tiles(c), :], ALU.add).then_inc(x_mid, 1)

            def tile_of(c):
                return lambda t: X[:, c * TT + t, :]

            def ln(c):
                if attn is not None:
                    x_middle(c)
                    waits(dve, (w_in, 16 * W_LOADS), (x_mid, c + 1), (ln_rstd, c * 2))
                else:
                    waits(dve, (w_in, 16 * W_LOADS), (ln_rstd, c * 2))
                mean_and_variance(nc, dve, ln_stats, c, tile_of(c), stats, mv, (w_in, 16 * W_LOADS)).then_inc(ln_mv, 1)

            def norms(c):
                dve.wait_ge(ln_rstd, c * 2 + 2)
                wait(dve, ht_turned, c)
                wait(dve, xs_ready, c)
                normalize(nc, tile_of(c), H, mv, root[5]).then_inc(h_ready, 1)
                normalize(nc, tile_of(c), XN, mv, root[1]).then_inc(xn_ready, 1)

            def split_h(c):
                dve.wait_ge(ht_full, c + 1)
                wait(dve, fc1_done, c * FT)
                nc.vector.tensor_copy(HTH[:], HT[:]).then_inc(ht_hi, 1)
                dve.wait_ge(ht_hi, c + 1)
                nc.vector.tensor_tensor(HTL[:], HT[:], HTH[:].bitcast(F32), ALU.subtract).then_inc(ht_lo, 1)

            def x_final(c):
                dve.wait_ge(fc2_done, c + 1)
                dve.wait_ge(xr_ready, c + 1)
                nc.vector.scalar_tensor_tensor(X[:, tiles(c), :], pZ[:], 0.5, XR[:], ALU.mult, ALU.add)\
                    .then_inc(x_new, 1)

            def ln3(c):
                waits(dve, (w_in, 16 * W_LOADS), (x_new, c + 1), (ln3_rstd, c))
                mean_and_variance(nc, dve, ln3_stats, c, tile_of(c), stats3, mv3, (w_in, 16 * W_LOADS)).then_inc(ln3_mv, 1)

            def norm3(c):
                dve.wait_ge(ln3_rstd, c + 1)
                wait(dve, xt_turned, c)
                normalize(nc, tile_of(c), XN3, mv3, rstd3).then_inc(xn3_ready, 1)

            def turn_lo(c):
                dve.wait_ge(xt_hi, c + 1)
                wait(dve, v_mm, c * 8)
                wait(dve, xt_kept, c * 32)
                nc.vector.tensor_tensor(XTL[:], pT3[:], XTH[:].bitcast(F32), ALU.subtract).then_inc(xt_lo, 1)

            def v_right(c, t):
                dve.wait_ge(v_mm, c * 8 + t * 2 + 2)
                if t == 0:
                    wait(dve, v_stored, c * 64)
                nc.vector.tensor_copy(V[:, t, N:2 * N], pV[:, 1, :]).then_inc(v_dve, 1)

            def first(c):
                ln(c)
                norms(c)
                split_h(c)

            def body(c, ahead, behind):
                if behind and tail is not None:
                    turn_lo(c - 1)
                if ahead:
                    ln(c + 1)
                if behind and tail is not None:
                    v_right(c - 1, 0)
                    v_right(c - 1, 1)
                if ahead:
                    norms(c + 1)
                x_final(c)
                if tail is not None:
                    ln3(c)
                if behind and tail is not None:
                    v_right(c - 1, 2)
                    v_right(c - 1, 3)
                if tail is not None:
                    norm3(c)
                if ahead:
                    split_h(c + 1)

            def behind(c):
                if tail is not None:
                    turn_lo(c)
                    for t in range(TT):
                        v_right(c, t)

            dve.wait_ge(w_in, 16 * W_LOADS)
            nc.vector.scalar_tensor_tensor(W1[:], Q1[:], -128.0, S1[:], ALU.add, ALU.mult).then_inc(w_deq, 1)
            nc.vector.scalar_tensor_tensor(W2[:], Q2[:], -128.0, S2[:], ALU.add, ALU.mult).then_inc(w_deq, 1)
            nc.vector.tensor_scalar(B2[:], B2[:], 0.5, None, ALU.mult).then_inc(w_deq, 3)
            dve.wait_ge(w_deq, 5)
            nc.vector.tensor_copy(W1H[:], W1[:]).then_inc(w_split, 1)
            dve.wait_ge(w_split, 1)
            nc.vector.tensor_tensor(W1L[:], W1[:], W1H[:].bitcast(F32), ALU.subtract).then_inc(w_split, 1)
            if tail is not None:
                nc.vector.tensor_copy(WVH[:], WV[:]).then_inc(w_split, 1)
                dve.wait_ge(w_split, 3)
                nc.vector.tensor_tensor(WVL[:], WV[:], WVH[:].bitcast(F32), ALU.subtract).then_inc(w_split, 1)
                for j in range(NP):
                    last = nc.vector.tensor_copy(BVB[:, j, :], BV[:, j:j + 1].broadcast_to([P, P]))
                last.then_inc(bias_wide, 1)
                dve.wait_ge(bias_sum, 1)
                nc.vector.tensor_tensor(BOV[:], pV[:, 0, 0:P], BO[:], ALU.add).then_inc(bias_total, 1)
            over_batches(dve, first, None, body, behind)

def phase_b_attention(nc, X, IDENT, d, XTH, XTL, v_d):
    with ExitStack() as ctx:
        sb = lambda n, s, t: ctx.enter_context(nc.sbuf_tensor(f"b_{n}", s, t))
        ps = lambda n, s, t: ctx.enter_context(nc.psum_tensor(f"b_{n}", s, t))
        sem = lambda n: ctx.enter_context(nc.semaphore(f"b_{n}"))
        K2R = 96
        R = range(2)
        WQK = [sb(f"w{r}", [P, 2, P], F32) for r in R]
        WH = [sb(f"w_hi{r}", [P, 2, P], F32R) for r in R]
        WL = [sb(f"w_lo{r}", [P, 2, P], F32R) for r in R]
        V = [sb(f"v{r}", [P, TT, P], F32) for r in R]
        Q1 = [sb(f"q1_{r}", [P, 2, N], F32R) for r in R]
        K1 = [sb(f"k1_{r}", [P, 2, N], F32R) for r in R]
        Q2 = [sb(f"q2_{r}", [K2R, 2, N], F32R) for r in R]
        K2 = [sb(f"k2_{r}", [K2R, 2, N], F32R) for r in R]
        BQ = sb("bq", [DB, HB], F32)
        BK = sb("bk", [DB, HB], F32)
        WO = sb("wo", [P, NP, P], F32)
        ONES = sb("ones", [P, DB], F32)
        ZERO = sb("zero", [P, 2, P], F32)
        EYE = sb("eye", [P, P], BF16)
        MQ = sb("mask_q", [P, P], BF16)
        MK = sb("mask_k", [P, 3 * P], BF16)
        PA = [sb(f"probs_a{h}", [P, 2, N], F32) for h in R]
        PB = [sb(f"probs_b{h}", [P, N], F32) for h in R]
        DS = [sb(f"den_sum{h}", [P, N - P], F32) for h in R]
        NM = [sb(f"neg_max{r}", [P, TT, 2], F32) for r in R]
        NMH = sb("neg_max_hi", [2, N], F32R)
        NML = sb("neg_max_lo", [2, N], F32R)
        RD = sb("recip_den", [P, N], F32)
        Z = [sb(f"z{r}", [P, N], F32) for r in R]
        pM = ps("p_max", [P, 2, N], F32)
        pA = ps("p_scores_a", [P, 2 * N], F32)
        pB = ps("p_scores_b", [P, N], F32)
        pZ = ps("p_z", [P, N], F32)
        pU = [ps(f"p_misc{u}", [P, N], F32) for u in R]

        const_in = sem("const_in")
        masks_set = sem("masks_set")
        stacks_set = sem("stacks_set")
        w_in = [sem(f"w_in{r}") for r in R]
        v_in = [sem(f"v_in{r}") for r in R]
        w_split = sem("w_split")
        q_mm = sem("q_mm")
        k_mm = sem("k_mm")
        hi_done = sem("hi")
        lo_done = sem("lo")
        copied = [sem(f"copied{r}") for r in R]
        sm_filled = sem("sm_filled")
        sm_reduced = sem("sm_reduced")
        nm_turned = sem("nm_turned")
        nm_split = sem("nm_split")
        rows_in = [sem(f"rows_in{r}") for r in R]
        st_filled = sem("st_filled")
        exp_done = sem("exp")
        den_step = sem("den_step")
        pv_done = sem("pv")
        den_done = sem("den")
        recip_done = sem("recip")
        z_done = sem("z")
        wo_done = sem("wo_mm")
        x_added = sem("x_added")

        block = ctx.enter_context(nc.Block())

        HALF = NP // 2

        def over_slots(eng, body):
            body(0, 0, True, False)
            body(0, 1, False, False)
            with eng.Fori(1, B * HALF - 1) as m:
                body(m, 0, False, False)
                body(m, 1, False, False)
            body(B * HALF - 1, 0, False, False)
            body(B * HALF - 1, 1, False, True)

        def next_of(m, r):
            return (m, 1) if r == 0 else (m + 1, 0)

        def before(m, r):
            return (m, 0) if r == 1 else (m - 1, 1)

        def batch(m):
            return m // HALF

        def pair(m, r):
            return (m % HALF) * 2 + r

        def span(start, n):
            return slice(start, start + n) if isinstance(start, int) else bass.ds(start, n)

        @block.sync
        def _(sp):
            sp.dma_start(BQ[:], d["bq2"]).then_inc(const_in, 16)
            sp.dma_start(BK[:], d["bk2"]).then_inc(const_in, 16)
            sp.dma_start(WO[:], d["wo"].rearrange("(j r) n -> r j n", r=P)).then_inc(const_in, 16)

            def load(m, r):
                i = 2 * m + r
                now = pair(m, r) if isinstance(m, int) else sp.snap(pair(m, r))
                rows_of = batch(m) if isinstance(m, int) else sp.snap(batch(m))
                waits(sp, (stacks_set, 2), (w_split, 2 * i - 2))
                sp.dma_start(WQK[r][:], d["wqk2"][:, now]).then_inc(w_in[r], 16)
                waits(sp, (stacks_set, 2), (pv_done, 4 * i - 4))
                sp.dma_start(V[r][:], v_d[rows_of, now]).then_inc(v_in[r], 16)

            def copy_high(m, r):
                i = 2 * m + r
                sp.wait_ge(hi_done, 4 * i + 2)
                sp.dma_start(Q2[r][0:DB].bitcast(F32), Q1[r][0:DB].bitcast(F32)).then_inc(copied[r], 16)
                sp.wait_ge(hi_done, 4 * i + 4)
                sp.dma_start(K1[r][DB:2 * DB].bitcast(F32), K1[r][0:DB].bitcast(F32)).then_inc(copied[r], 16)

            def rows(m, r):
                i = 2 * m + r
                sp.wait_ge(nm_split, 2 * i + 1)
                sp.dma_start(Q2[r][DB:DB + 1].bitcast(F32), NMH[:].bitcast(F32)).then_inc(rows_in[r], 16)
                sp.wait_ge(nm_split, 2 * i + 2)
                sp.dma_start(Q2[r][DB + 1:DB + 2].bitcast(F32), NML[:].bitcast(F32)).then_inc(rows_in[r], 16)

            def body(m, r, first, last):
                if not last:
                    n = next_of(m, r)
                    copy_high(*n)
                    if not (isinstance(m, int) and m == B * HALF - 1):
                        load(m + 1, r)
                    rows(*n)

            sp.wait_ge(stacks_set, 2)
            for r in R:
                load(0, r)
            copy_high(0, 0)
            rows(0, 0)
            over_slots(sp, body)

        @block.gpsimd
        def _(pool):
            def split(m, r):
                i = 2 * m + r
                pool.wait_ge(w_in[r], (m + 1) * 16)
                wait(pool, k_mm, i - 1)
                nc.gpsimd.tensor_tensor(WH[r][:], WQK[r][:], ZERO[:], ALU.add).then_inc(w_split, 1)
                pool.wait_ge(w_split, 2 * i + 1)
                nc.gpsimd.tensor_tensor(WL[r][:], WQK[r][:], WH[r][:].bitcast(F32), ALU.subtract)\
                    .then_inc(w_split, 1)

            def body(m, r, first, last):
                i = 2 * m + r
                for h in R:
                    n = i * 6 + h * 3
                    pool.wait_ge(exp_done, i * 4 + h * 2 + 1)
                    wait(pool, den_done, i * 2 + h - 1)
                    nc.gpsimd.tensor_tensor(DS[h][:], PA[h][:, 0, P:N], PA[h][:, 1, 0:N - P], ALU.add)\
                        .then_inc(den_step, 1)
                    pool.wait_ge(exp_done, i * 4 + h * 2 + 2)
                    for k in range(2):
                        pool.wait_ge(den_step, n + k + 1)
                        nc.gpsimd.tensor_tensor(DS[h][:, P:N - P], DS[h][:, P:N - P],
                                                PB[h][:, k * 256:k * 256 + 256], ALU.add).then_inc(den_step, 1)
                if not last:
                    if r == 0:
                        split(m + 1, 0) if not (isinstance(m, int) and m == B * HALF - 1) else None
                    else:
                        split(m + 1, 1)

            nc.gpsimd.memset(MQ[:], MASKED).then_inc(masks_set, 1)
            nc.gpsimd.memset(MK[:, 0:2 * P], MASKED).then_inc(masks_set, 1)
            nc.gpsimd.memset(ONES[:], 1.0).then_inc(masks_set, 1)
            nc.gpsimd.memset(EYE[:], 1.0).then_inc(masks_set, 1)
            nc.gpsimd.memset(ZERO[:], 0.0).then_inc(masks_set, 1)
            pool.wait_ge(masks_set, 5)
            nc.gpsimd.affine_select(out=MQ[:], in_=MQ[:], compare_op=ALU.is_gt, fill=0.0, base=0,
                                    pattern=[[1, P]], channel_multiplier=-1).then_inc(masks_set, 1)
            nc.gpsimd.affine_select(out=MK[:, P:2 * P], in_=MK[:, P:2 * P], compare_op=ALU.is_gt, fill=0.0,
                                    base=0, pattern=[[-1, P]], channel_multiplier=1).then_inc(masks_set, 1)
            nc.gpsimd.affine_select(out=EYE[:], in_=EYE[:], compare_op=ALU.is_equal, fill=0.0, base=0,
                                    pattern=[[-1, P]], channel_multiplier=1).then_inc(masks_set, 1)
            for r in R:
                split(0, r)
            over_slots(pool, body)

        @block.tensor
        def _(pe):
            def project(m, r, qk):
                i = 2 * m + r
                pe.wait_ge(w_split, 2 * i + 2)
                if qk == 0:
                    wait(pe, nm_split, 2 * i)
                    wait(pe, recip_done, i - 1)
                else:
                    wait(pe, x_added, i - 2)
                xt = span(batch(m) * N, N)
                u = pU[1 - qk]
                nc.tensor.matmul(u[:], WH[r][:, qk, :], XTH[:, xt], start=True, stop=False)
                nc.tensor.matmul(u[:], WL[r][:, qk, :], XTH[:, xt], start=False, stop=False)
                nc.tensor.matmul(u[:], WH[r][:, qk, :], XTL[:, xt], start=False, stop=True)\
                    .then_inc((q_mm, k_mm)[qk], 1)

            def out_product(m, r, projected):
                i = 2 * m + r
                pe.wait_ge(z_done, i + 1)
                pe.wait_ge(hi_done, 4 * projected)
                pe.wait_ge(lo_done, 4 * projected)
                wait(pe, x_added, i)
                for t in range(TT):
                    last = nc.tensor.matmul(pU[0][:, t * P:(t + 1) * P], Z[r][:, t * P:(t + 1) * P],
                                            WO[:, pair(m, r), :], start=True, stop=True)
                last.then_inc(wo_done, 1)

            def smax_unit(m, r, h, qt):
                i = 2 * m + r
                if qt == 0:
                    if h == 0:
                        pe.wait_ge(copied[r], (m + 1) * 32)
                    pe.wait_ge(lo_done, i * 4 + 4)
                wait(pe, sm_reduced, i * 8 + h * 4 + qt - 1)
                n = max((qt + 1) * P, 256)
                bank = pM[:, qt % 2, :]
                nc.tensor.matmul(bank[:, 0:n], Q1[r][:, h, qt * P:(qt + 1) * P], K1[r][:, h, 0:n],
                                 start=True, stop=False)
                nc.tensor.matmul(bank[:, qt * P:(qt + 1) * P], EYE[:], MQ[:], start=False, stop=True)\
                    .then_inc(sm_filled, 1)

            def scores(m, r, h, part):
                i = 2 * m + r
                if h == 0 and part == 0:
                    pe.wait_ge(rows_in[r], (m + 1) * 32)
                wait(pe, exp_done, i * 4 + h * 2 + part - 1)
                for kt in (2 * part, 2 * part + 1):
                    q0 = min(kt * P, 256)
                    n = N - q0
                    bank = pA[:, kt * N:kt * N + n] if part == 0 else pB[:, (kt - 2) * 256:(kt - 2) * 256 + n]
                    keys = slice(kt * P, (kt + 1) * P)
                    nc.tensor.matmul(bank, K1[r][:, h, keys], Q1[r][:, h, q0:N], start=True, stop=False)
                    nc.tensor.matmul(bank, K2[r][:, h, keys], Q2[r][:, h, q0:N], start=False, stop=False)
                    if kt < 3:
                        last = nc.tensor.matmul(bank[:, 0:P], EYE[:], MK[:, P:2 * P], start=False, stop=True)
                    else:
                        last = nc.tensor.matmul(bank, EYE[:], MK[:, 0:2 * P], start=False, stop=True)
                last.then_inc(st_filled, 1)

            def pv(m, r, kt):
                i = 2 * m + r
                pe.wait_ge(exp_done, i * 4 + (3 if kt < 2 else 4))
                if kt == 0:
                    pe.wait_ge(v_in[r], (m + 1) * 16)
                    wait(pe, z_done, i)
                for h in R:
                    probs = PA[h][:, kt, 0:N - kt * P] if kt < 2 else \
                        PB[h][:, (kt - 2) * 256 + (kt - 2) * P:(kt - 1) * 256]
                    last = nc.tensor.matmul(pZ[h * DB:(h + 1) * DB, kt * P:N], V[r][:, kt, h * DB:(h + 1) * DB],
                                            probs, start=(kt == 0), stop=(kt == TT - 1), skip_group_check=True)
                last.then_inc(pv_done, 1)

            def denominators(m, r):
                i = 2 * m + r
                for h in R:
                    pe.wait_ge(den_step, i * 6 + h * 3 + 3)
                    rows = pU[1][h * DB:(h + 1) * DB, :]
                    nc.tensor.matmul(rows[:, 0:P], ONES[:], PA[h][:, 0, 0:P], start=True, stop=True)
                    nc.tensor.matmul(rows[:, P:N], ONES[:], DS[h][:], start=True, stop=True).then_inc(den_done, 1)

            def turn_max(m, r):
                i = 2 * m + r
                pe.wait_ge(sm_reduced, i * 8 + 8)
                pe.wait_ge(hi_done, 4 * i + 4)
                for qt in range(TT):
                    last = nc.tensor.transpose(pU[1][0:2, qt * P:(qt + 1) * P], NM[r][:, qt, :], IDENT[:])
                last.then_inc(nm_turned, 1)

            def body(m, r, first, last):
                nm_, nr = next_of(m, r)
                if not last:
                    project(nm_, nr, 0)
                scores(m, r, 0, 0)
                if not last:
                    project(nm_, nr, 1)
                scores(m, r, 0, 1)
                scores(m, r, 1, 0)
                if not first:
                    out_product(*before(m, r), 2 * m + r + (1 if last else 2))
                scores(m, r, 1, 1)
                pv(m, r, 0)
                if not last:
                    for h in R:
                        for qt in range(TT):
                            smax_unit(nm_, nr, h, qt)
                            if h == 1 and qt == 0:
                                pv(m, r, 1)
                    turn_max(nm_, nr)
                else:
                    pv(m, r, 1)
                pv(m, r, 2)
                pv(m, r, 3)
                if not last:
                    pe.wait_ge(nm_split, (2 * m + r + 1) * 2 + 2)
                denominators(m, r)

            pe.wait_ge(const_in, 48)
            pe.wait_ge(masks_set, 8)
            pe.wait_ge(stacks_set, 2)
            project(0, 0, 0)
            project(0, 0, 1)
            for h in R:
                for qt in range(TT):
                    smax_unit(0, 0, h, qt)
            turn_max(0, 0)
            over_slots(pe, body)
            out_product(B * HALF - 1, 1, 2 * B * HALF)

        @block.scalar
        def _(act):
            def high(m, r, qk):
                i = 2 * m + r
                act.wait_ge((q_mm, k_mm)[qk], i + 1)
                wait(act, st_filled, 4 * (i - 1))
                dst, bias = ((Q1, BQ), (K1, BK))[qk]
                for h in R:
                    nc.scalar.activation(dst[r][0:DB, h, :], pU[1 - qk][h * DB:(h + 1) * DB, :], ACT.Identity,
                                         bias=bias[:, bias_col(m, r, h)]).then_inc(hi_done, 1)

            def bias_col(m, r, h):
                return span(pair(m, r) * 2 + h, 1)

            def exp_unit(m, r, h, part):
                i = 2 * m + r
                act.wait_ge(st_filled, i * 4 + h * 2 + part + 1)
                if part == 0:
                    wait(act, pv_done, 4 * i)
                    wait(act, den_done, 2 * i)
                    nc.scalar.activation(PA[h][:].rearrange("p a n -> p (a n)")[:, 0:2 * N - P], pA[:, 0:2 * N - P],
                                         ACT.Exp, scale=SCALE_B).then_inc(exp_done, 1)
                else:
                    nc.scalar.activation(PB[h][:], pB[:], ACT.Exp, scale=SCALE_B).then_inc(exp_done, 1)

            def body(m, r, first, last):
                n = next_of(m, r)
                if not last:
                    high(*n, 0)
                exp_unit(m, r, 0, 0)
                if not last:
                    high(*n, 1)
                exp_unit(m, r, 0, 1)
                exp_unit(m, r, 1, 0)
                exp_unit(m, r, 1, 1)

            act.wait_ge(const_in, 48)
            high(0, 0, 0)
            high(0, 0, 1)

            over_slots(act, body)

        @block.vector
        def _(dve):
            def low(m, r, qk):
                i = 2 * m + r
                for h in R:
                    dve.wait_ge(hi_done, i * 4 + qk * 2 + h + 1)
                    src, hi, bias = ((pU[1], Q1, BQ), (pU[0], K1, BK))[qk]
                    dst = Q1[r][DB:2 * DB, h, :] if qk == 0 else K2[r][0:DB, h, :]
                    nc.vector.scalar_tensor_tensor(dst, src[h * DB:(h + 1) * DB, :],
                                                   bias[:, span(pair(m, r) * 2 + h, 1)],
                                                   hi[r][0:DB, h, :].bitcast(F32), ALU.add, ALU.subtract)\
                        .then_inc(lo_done, 1)

            def reduce_unit(m, r, h, qt):
                i = 2 * m + r
                dve.wait_ge(sm_filled, i * 8 + h * 4 + qt + 1)
                if h == 0 and qt == 0:
                    wait(dve, nm_turned, i - 1)
                nc.vector.tensor_reduce(NM[r][:, qt, h:h + 1], pM[:, qt % 2, 0:(qt + 1) * P], AX.X, ALU.max,
                                        negate=True).then_inc(sm_reduced, 1)

            def split_max(m, r):
                i = 2 * m + r
                dve.wait_ge(nm_turned, i + 1)
                if r == 0:
                    wait(dve, rows_in[1], m * 32)
                else:
                    dve.wait_ge(rows_in[0], (m + 1) * 32)
                nc.vector.tensor_copy(NMH[:], pU[1][0:2, :]).then_inc(nm_split, 1)
                dve.wait_ge(nm_split, 2 * i + 1)
                nc.vector.tensor_tensor(NML[:], pU[1][0:2, :], NMH[:].bitcast(F32), ALU.subtract)\
                    .then_inc(nm_split, 1)

            def normalize_z(m, r):
                i = 2 * m + r
                dve.wait_ge(den_done, 2 * i + 2)
                nc.vector.reciprocal(RD[:], pU[1][:]).then_inc(recip_done, 1)
                dve.wait_ge(recip_done, i + 1)
                dve.wait_ge(pv_done, 4 * i + 4)
                wait(dve, wo_done, i - 1)
                nc.vector.tensor_tensor(Z[r][:], pZ[:], RD[:], ALU.mult).then_inc(z_done, 1)

            def add_out(m, r):
                i = 2 * m + r
                dve.wait_ge(wo_done, i + 1)
                xb = X[:, span(batch(m) * TT, TT), :]
                nc.vector.tensor_tensor(xb, pU[0][:].rearrange("p (t n) -> p t n", t=TT), xb, ALU.add)\
                    .then_inc(x_added, 1)

            def body(m, r, first, last):
                n = next_of(m, r)
                if not first:
                    normalize_z(*before(m, r))
                if not last:
                    low(*n, 0)
                    low(*n, 1)
                if not first:
                    add_out(*before(m, r))
                if not last:
                    for h in R:
                        for qt in range(TT):
                            reduce_unit(*n, h, qt)
                    split_max(*n)

            for r in R:
                nc.vector.memset(Q2[r][:].bitcast(F32), 0.0)
                last_set = nc.vector.memset(K2[r][:].bitcast(F32), 0.0)
            last_set.then_inc(stacks_set, 1)
            dve.wait_ge(stacks_set, 1)
            for r in R:
                last_set = nc.vector.memset(K2[r][DB:DB + 2].bitcast(F32), 1.0)
            last_set.then_inc(stacks_set, 1)
            dve.wait_ge(const_in, 48)
            low(0, 0, 0)
            low(0, 0, 1)
            for h in R:
                for qt in range(TT):
                    reduce_unit(0, 0, h, qt)
            split_max(0, 0)
            over_slots(dve, body)
            normalize_z(B * HALF - 1, 1)
            add_out(B * HALF - 1, 1)


def program(nc, d, out):
    q_d = nc.dram_tensor("q_stacks", (B, HA, 4 * DA, N), F32).ap()
    k_d = nc.dram_tensor("k_stacks", (B, HA, 4 * DA, N), F32).ap()
    va_d = nc.dram_tensor("v_first", (B, P, NG, TT, GH, 32), F32).ap()
    vb_d = nc.dram_tensor("v_second", (B, NP, P, TT, P), F32).ap()
    o_d = nc.dram_tensor("o_first", (HA, B, 32, P), F32).ap()
    with nc.sbuf_tensor("x", [P, B * TT, P], F32) as X, nc.sbuf_tensor("ident", [P, P], F32) as IDENT:
        phase_a_inputs(nc, X, IDENT, d, (q_d, k_d, va_d))
        phase_a_attention(nc, IDENT, d, (q_d, k_d, va_d), o_d)
        with nc.sbuf_tensor("xt_all_hi", [P, B * N], F32R) as XTH, nc.sbuf_tensor("xt_all_lo", [P, B * N], F32R) as XTL:
            phase_ffn(nc, X, IDENT, d, "f1", attn=o_d, tail=(XTH, XTL, vb_d))
            phase_b_attention(nc, X, IDENT, d, XTH, XTL, vb_d)
        phase_ffn(nc, X, IDENT, d, "f2", out=out)


def lay_out(i):
    wq, wk, wv = np.split(i["L0_attn_a_qkv_w"], 3, axis=0)
    bq, bk, bv = np.split(i["L0_attn_a_qkv_b"], 3)
    half = np.arange(D).reshape(HA, DA)
    half = np.roll(half, DA // 2, axis=1).reshape(D)
    inv = (1.0 / 10000.0 ** (np.arange(0, DA, 2, dtype=np.float32) / DA)).astype(np.float32)
    ang = np.arange(N, dtype=np.float32)[:, None] * inv[None, :]
    cos = np.concatenate([np.cos(ang), np.cos(ang)], 1).T
    sin = np.concatenate([-np.sin(ang), np.sin(ang)], 1).T
    rot = np.stack([np.tile(cos, (HA, 1)), np.tile(sin, (HA, 1))], 1).astype(np.float32)
    sel = np.zeros((P, 36), np.float32)
    for h in range(GH):
        sel[32 * h:32 * h + DA, h * DA:(h + 1) * DA] = np.eye(DA)
        sel[32 * h + DA, 32 + h] = 1.0
    c = np.ascontiguousarray
    return {
        "x": c(i["L0_attn_a_x"]),
        "wa": c(np.stack([wq.T, wq[half].T, wk.T, wk[half].T, wv.T], 1)),
        "bqk": c(np.stack([bq, bq[half], bk, bk[half]], 1)),
        "bv": c(bv),
        "rot": c(rot),
        "sel": sel,
        "ident": np.eye(P, dtype=np.float32),
        "wp": c(i["L0_attn_a_proj_w"].T),
        "bp": c(i["L0_attn_a_proj_b"]),
        "fc1_q": c(i["L0_ffn_fc1_q"]),
        "fc1_s": c(i["L0_ffn_fc1_scales"].reshape(FF)),
        "fc2_q": c(i["L0_ffn_fc2_q"]),
        "fc2_s": c(i["L0_ffn_fc2_scales"]),
        "gb": c(np.stack([i["L0_ffn_ln_gamma"], i["L0_ffn_ln_beta"]], 1)),
        "b1": c(i["L0_ffn_fc1_bias"].reshape(FT, P).T),
        "b2": c(i["L0_ffn_fc2_bias"]),
        "wqk2": c(np.stack([i["L0_attn_b_Wq"].transpose(1, 0, 2).reshape(D, NP, P),
                            i["L0_attn_b_Wk"].transpose(1, 0, 2).reshape(D, NP, P)], 2)),
        "wv2": c(i["L0_attn_b_Wv"].transpose(1, 0, 2).reshape(D, HB * DB)),
        "wo": c(i["L0_attn_b_Wo"].reshape(HB * DB, D)),
        "bq2": c(i["L0_attn_b_bq"].T),
        "bk2": c(i["L0_attn_b_bk"].T),
        "bv2": c(i["L0_attn_b_bv"].reshape(NP, P).T),
        "bo": c(i["L0_attn_b_bo"]),
    }


def kernel(**inputs):
    import concourse.bacc as bacc
    from concourse.bass_utils import run_bass_kernel_spmd

    nc = bacc.Bacc("TRN2", target_bir_lowering=False, num_devices=1)
    arrays = lay_out({name: np.asarray(a) for name, a in inputs.items()})
    d = {name: nc.dram_tensor(f"in_{name}", a.shape, mybir.dt.from_np(a.dtype), kind="ExternalInput").ap()
         for name, a in arrays.items()}
    out = nc.dram_tensor("out", (B, N, D), F32, kind="ExternalOutput").ap()
    program(nc, d, out)
    r = run_bass_kernel_spmd(nc, [{f"in_{name}": a for name, a in arrays.items()}], core_ids=[0])
    return r.results[0]["out"]
```

```python
from contextlib import ExitStack

import numpy as np

import concourse.bass as bass
from concourse import mybir

F32 = mybir.dt.float32
F32R = mybir.dt.float32r
BF16 = mybir.dt.bfloat16
I32 = mybir.dt.int32
ALU = mybir.AluOpType
ACT = mybir.ActivationFunctionType
AX = mybir.AxisListType

P = 128
D = 128
B, N = 8, 512
TT = N // P
BANK = 512
EPS = 1e-5
HA, DA = 16, 8
GH = 4
NG = HA // GH
HB, DB = 16, 64
NP = HB // 2
FF = 512
FT = FF // P
SCALE_A = float(DA) ** -0.5
SCALE_B = float(DB) ** -0.5
MASKED = -1e30


def fits(v):
    return not isinstance(v, int) or v > 0


def wait(eng, sem, v):
    if fits(v):
        eng.wait_ge(sem, v)


def waits(eng, met, *pairs):
    for _, n in pairs:
        if not isinstance(n, int):
            eng.compute_val(n)
    eng.wait_ge(*met)
    for sem, n in pairs:
        wait(eng, sem, n)


def mean_and_variance(nc, dve, stats_done, n, x_of_tile, stats, mv, consts):
    for t in range(TT):
        last = nc.vector.bn_stats(stats[:, t, :], x_of_tile(t))
    last.then_inc(stats_done, 1)
    waits(dve, consts, (stats_done, n + 1))
    for t in range(TT):
        last = nc.vector.bn_aggr(mv[:, t, :], stats[:, t, :])
    return last


def inverse_root(nc, pool, step, n, mv, ve, minus_half, out):
    nc.gpsimd.tensor_scalar(ve[:], mv[:, :, 1], EPS, None, ALU.add).then_inc(step, 1)
    pool.wait_ge(step, n + 2)
    return nc.gpsimd.tensor_tensor(out[:], ve[:], minus_half[:], ALU.pow)


def normalize(nc, x_of_tile, out, mv, rstd):
    for t in range(TT):
        last = nc.vector.tensor_scalar(out[:, t, :], x_of_tile(t), mv[:, t, 0:1], rstd[:, t:t + 1],
                                       ALU.subtract, ALU.mult)
    return last


def phase_a_inputs(nc, X, IDENT, d, scratch):
    q_d, k_d, v_d = scratch
    with ExitStack() as ctx:
        sb = lambda n, s, t: ctx.enter_context(nc.sbuf_tensor(n, s, t))
        ps = lambda n, s, t: ctx.enter_context(nc.psum_tensor(n, s, t))
        sem = lambda n: ctx.enter_context(nc.semaphore(n))
        W = sb("wa_raw", [P, 5, P], F32)
        WH = sb("wa_hi", [P, 4, P], F32R)
        WL = sb("wa_lo", [P, 4, P], F32R)
        BQK = sb("qk_bias", [P, 4], F32)
        BV = sb("v_bias", [P, P], F32)
        ROT = sb("rotary", [P, 2, N], F32)
        stats = sb("ln_stats", [P, TT, 6], F32)
        mv = sb("ln_mv", [P, TT, 2], F32)
        ve = sb("ln_var_eps", [P, TT], F32)
        minus_half = sb("minus_half", [P, TT], F32)
        rstd = sb("ln_rstd", [P, TT], F32)
        XN = sb("xn", [P, TT, P], F32)
        XT = sb("xt", [P, N], F32)
        XTH = sb("xt_hi", [P, N], F32R)
        XTL = sb("xt_lo", [P, N], F32R)
        T1 = sb("rot_cos", [P, 2, N], F32)
        T2 = sb("rot_sin", [P, 2, N], F32)
        QK = sb("qk_full", [P, 2, N], F32)
        QKH = sb("qk_hi", [P, 2, N], F32R)
        QKL = sb("qk_lo", [P, 2, N], F32R)
        V = sb("v_rows", [P, NG, TT, GH, 32], F32)
        pT = ps("p_xt", [P, N], F32)
        pQ = ps("p_qk", [P, 4, N], F32)
        pV = ps("p_v", [P, TT, P], F32)

        w_in = sem("a0_w_in")
        x_in = sem("a0_x_in")
        w_split = sem("a0_w_split")
        v_ready0 = sem("a0_v_const")
        ln_stats = sem("a0_ln_stats")
        ln_mv = sem("a0_ln_mv")
        ln_rstd = sem("a0_ln_rstd")
        root_step = sem("a0_root_step")
        xn_ready = sem("a0_xn")
        xt_ready = sem("a0_xt_psum")
        xt_copied = sem("a0_xt_copied")
        xt_split = sem("a0_xt_split")
        v_done = sem("a0_v_psum")
        qk_done = sem("a0_qk_psum")
        rot_done = sem("a0_rot")
        qk_sum = sem("a0_qk_sum")
        qk_hi = sem("a0_qk_hi")
        qk_lo = sem("a0_qk_lo")
        v_out = sem("a0_v_sbuf")
        stored_h = sem("a0_hi_stored")
        stored_l = sem("a0_lo_stored")
        stored_v = sem("a0_v_stored")

        block = ctx.enter_context(nc.Block())

        def each_batch(eng, batch):
            batch(0)
            with eng.Fori(1, B) as c:
                batch(c)

        @block.sync
        def _(sp):
            sp.dma_start(W[:], d["wa"]).then_inc(w_in, 16)
            for c in range(B):
                sp.dma_start(X[:, c * TT:(c + 1) * TT, :],
                             d["x"][c].rearrange("(t p) d -> p t d", p=P)).then_inc(x_in, 16)
                sp.wait_ge(x_in, 16 * (c + 1))
            def batch(c):
                for qk, dst in ((0, q_d), (1, k_d)):
                    sp.wait_ge(qk_hi, c * 2 + qk + 1)
                    for j in ((0, 3), (0, 2))[qk]:
                        sp.dma_start(dst[c, :, j * DA:(j + 1) * DA, :], QKH[:, qk, :].bitcast(F32))\
                            .then_inc(stored_h, 16)
                    sp.wait_ge(qk_lo, c * 2 + qk + 1)
                    for j in ((1, 2), (1, 3))[qk]:
                        sp.dma_start(dst[c, :, j * DA:(j + 1) * DA, :], QKL[:, qk, :].bitcast(F32))\
                            .then_inc(stored_l, 16)
                sp.wait_ge(v_out, c + 1)
                sp.dma_start(v_d[c], V[:]).then_inc(stored_v, 16)

            each_batch(sp, batch)
            sp.wait_ge(stored_h, 64 * B)
            sp.wait_ge(stored_l, 64 * B)
            sp.wait_ge(stored_v, 16 * B)

        @block.scalar
        def _(act):
            act.dma_start(BQK[:], d["bqk"]).then_inc(w_in, 16)
            act.dma_start(BV[:], d["bv"].partition_broadcast(P)).then_inc(w_in, 16)
            act.dma_start(ROT[:], d["rot"]).then_inc(w_in, 16)
            act.dma_start(IDENT[:], d["ident"]).then_inc(w_in, 16)

            def batch(c):
                act.wait_ge(xt_ready, c + 1)
                wait(act, v_done, c)
                wait(act, qk_done, c * 4)
                nc.scalar.activation(XT[:], pT[:], ACT.Copy).then_inc(xt_copied, 1)
                nc.scalar.activation(XTH[:], pT[:], ACT.Copy).then_inc(xt_copied, 1)
                for qk in range(2):
                    act.wait_ge(qk_sum, c * 2 + qk + 1)
                    wait(act, stored_h, c * 64)
                    nc.scalar.activation(QKH[:, qk, :], QK[:, qk, :], ACT.Copy).then_inc(qk_hi, 1)

            each_batch(act, batch)

        @block.gpsimd
        def _(pool):
            nc.gpsimd.memset(V[:], 0.0).then_inc(v_ready0, 1)
            pool.wait_ge(v_ready0, 1)
            nc.gpsimd.memset(V[:, :, :, :, DA:DA + 1], 1.0).then_inc(v_ready0, 1)

            def root(c):
                waits(pool, (root_step, 1), (ln_mv, c + 1))
                inverse_root(nc, pool, root_step, c, mv, ve, minus_half, rstd).then_inc(ln_rstd, 1)

            def rest(c, ahead):
                if ahead:
                    root(c + 1)
                for qk in range(2):
                    pool.wait_ge(rot_done, c * 2 + qk + 1)
                    wait(pool, qk_hi, c * 2)
                    nc.gpsimd.tensor_tensor(QK[:, qk, :], T1[:, qk, :], T2[:, qk, :], ALU.add)\
                        .then_inc(qk_sum, 1)
                for qk in range(2):
                    pool.wait_ge(qk_hi, c * 2 + qk + 1)
                    wait(pool, stored_l, c * 64)
                    nc.gpsimd.tensor_tensor(QKL[:, qk, :], QK[:, qk, :], QKH[:, qk, :].bitcast(F32),
                                            ALU.subtract).then_inc(qk_lo, 1)

            nc.gpsimd.memset(minus_half[:], -0.5).then_inc(root_step, 1)
            root(0)
            rest(0, True)
            with pool.Fori(1, B - 1) as c:
                rest(c, True)
            rest(B - 1, False)

        @block.tensor
        def _(pe):
            pe.wait_ge(w_in, 80)
            pe.wait_ge(w_split, 2)
            def batch(c):
                pe.wait_ge(xn_ready, c + 1)
                wait(pe, xt_split, c)
                for t in range(TT):
                    last = nc.tensor.transpose(pT[:, t * P:(t + 1) * P], XN[:, t, :], IDENT[:])
                last.then_inc(xt_ready, 1)
                pe.wait_ge(xt_copied, c * 2 + 1)
                wait(pe, v_out, c)
                for t in range(TT):
                    last = nc.tensor.matmul(pV[:, t, :], XT[:, t * P:(t + 1) * P], W[:, 4, :],
                                            start=True, stop=True)
                last.then_inc(v_done, 1)
                pe.wait_ge(xt_copied, c * 2 + 2)
                pe.wait_ge(xt_split, c + 1)
                for j in range(4):
                    wait(pe, rot_done, (c * 2 if j < 2 else c * 2))
                    nc.tensor.matmul(pQ[:, j, :], WH[:, j, :], XTH[:], start=True, stop=False)
                    nc.tensor.matmul(pQ[:, j, :], WL[:, j, :], XTH[:], start=False, stop=False)
                    nc.tensor.matmul(pQ[:, j, :], WH[:, j, :], XTL[:], start=False, stop=True)\
                        .then_inc(qk_done, 1)

            each_batch(pe, batch)

        @block.vector
        def _(dve):
            def stage_ln(c):
                waits(dve, (w_in, 80), (x_in, (c + 1) * 16))
                x = lambda t: X[:, c * TT + t, :]
                mean_and_variance(nc, dve, ln_stats, c, x, stats, mv, (w_in, 80)).then_inc(ln_mv, 1)
                dve.wait_ge(ln_rstd, c + 1)
                wait(dve, xt_ready, c)
                normalize(nc, x, XN, mv, rstd).then_inc(xn_ready, 1)

            def stage_rest(c, ahead):
                dve.wait_ge(xt_copied, c * 2 + 2)
                wait(dve, qk_done, c * 4)
                nc.vector.tensor_tensor(XTL[:], pT[:], XTH[:].bitcast(F32), ALU.subtract)\
                    .then_inc(xt_split, 1)
                if ahead:
                    stage_ln(c + 1)
                dve.wait_ge(v_done, c + 1)
                wait(dve, stored_v, c * 16)
                for g in range(NG):
                    src = pV[:, :, g * 32:(g + 1) * 32].rearrange("p t (h d) -> p t h d", h=GH)
                    bias = BV[:, g * 32:(g + 1) * 32].rearrange("p (h d) -> p h d", h=GH)
                    for t in range(TT):
                        last = nc.vector.tensor_tensor(V[:, g, t, :, 0:DA], src[:, t], bias, ALU.add)
                last.then_inc(v_out, 1)
                for qk in range(2):
                    dve.wait_ge(qk_done, c * 4 + qk * 2 + 1)
                    wait(dve, qk_sum, c * 2)
                    nc.vector.scalar_tensor_tensor(T1[:, qk, :], pQ[:, 2 * qk, :], BQK[:, 2 * qk:2 * qk + 1],
                                                   ROT[:, 0, :], ALU.add, ALU.mult)
                    dve.wait_ge(qk_done, c * 4 + qk * 2 + 2)
                    nc.vector.scalar_tensor_tensor(T2[:, qk, :], pQ[:, 2 * qk + 1, :],
                                                   BQK[:, 2 * qk + 1:2 * qk + 2],
                                                   ROT[:, 1, :], ALU.add, ALU.mult).then_inc(rot_done, 1)

            dve.wait_ge(w_in, 80)
            nc.vector.tensor_copy(WH[:], W[:, 0:4, :]).then_inc(w_split, 1)
            dve.wait_ge(w_split, 1)
            nc.vector.tensor_tensor(WL[:], W[:, 0:4, :], WH[:].bitcast(F32), ALU.subtract).then_inc(w_split, 1)
            dve.wait_ge(v_ready0, 2)
            stage_ln(0)
            stage_rest(0, True)
            with dve.Fori(1, B - 1) as c:
                stage_rest(c, True)
            stage_rest(B - 1, False)


def phase_a_attention(nc, IDENT, d, scratch, o_d):
    q_d, k_d, v_d = scratch
    SLOTS = B * NG
    with ExitStack() as ctx:
        sb = lambda n, s, t: ctx.enter_context(nc.sbuf_tensor(n, s, t))
        ps = lambda n, s, t: ctx.enter_context(nc.psum_tensor(n, s, t))
        sem = lambda n: ctx.enter_context(nc.semaphore(n))
        KR = 96
        Q = [sb(f"q_stack{g}", [KR, GH, N], F32R) for g in range(NG)]
        K = [sb(f"k_stack{g}", [KR, GH, N], F32R) for g in range(NG)]
        V = [sb(f"v_stack{g}", [P, TT, GH, 32], F32) for g in range(NG)]
        PR = [sb(f"probs{kt}", [P, GH, N], F32) for kt in range(TT)]
        NM = [sb(f"neg_max{r}", [P, TT, GH], F32) for r in range(2)]
        NMF = sb("neg_max_rows", [GH, N], F32)
        ZERO = sb("zero", [GH, N], F32)
        NMH = sb("neg_max_hi", [GH, N], F32R)
        NML = sb("neg_max_lo", [GH, N], F32R)
        OT = sb("o_t", [P, N], F32)
        SEL = sb("select_rows", [P, 36], F32)
        RD = sb("recip_den", [P, 4, GH], F32)
        OX = [sb(f"o_rows{r}", [32, GH, 16, DA], F32) for r in range(2)]
        pM = ps("p_max", [P, 2, N], F32)
        pS = [ps(f"p_scores{u}", [P, 2, N], F32) for u in range(2)]
        pO = ps("p_out", [P, N], F32)
        pX = ps("p_misc", [P, N], F32)

        stacks_set = sem("a_stacks_set")
        loaded = [sem(f"a_loaded{g}") for g in range(NG)]
        rows_in = [sem(f"a_rows{g}") for g in range(NG)]
        sm_filled = sem("a_sm_filled")
        sm_reduced = sem("a_sm_reduced")
        nm_turned = sem("a_nm_turned")
        nm_copied = sem("a_nm_copied")
        nm_split = sem("a_nm_split")
        st_filled = sem("a_st_filled")
        exp_done = sem("a_exp")
        pv_done = sem("a_pv")
        ot_copied = sem("a_ot_copied")
        o_turned = sem("a_o_turned")
        o_recip = sem("a_o_recip")
        o_done = sem("a_o_done")
        sel_in = sem("a_sel_in")
        zero_set = sem("a_zero_set")
        o_stored = [sem(f"a_o_stored{r}") for r in range(2)]

        block = ctx.enter_context(nc.Block())

        def batch_of(s_b, g, ahead):
            j = g + ahead
            return s_b + j // NG, j % NG

        def over_batches(eng, body):
            body(0, True, False)
            with eng.Fori(1, B - 1) as b:
                body(b, False, False)
            body(B - 1, False, True)

        @block.sync
        def _(sp):
            sp.wait_ge(stacks_set, 5)

            def load(b, g):
                wait(sp, pv_done, (b * NG + g - NG) * TT + TT)
                sp.dma_start(Q[g][0:32].bitcast(F32), q_d[b, g * GH:(g + 1) * GH].rearrange("h r n -> r h n"))\
                    .then_inc(loaded[g], 16)
                sp.dma_start(K[g][0:32].bitcast(F32), k_d[b, g * GH:(g + 1) * GH].rearrange("h r n -> r h n"))\
                    .then_inc(loaded[g], 16)
                sp.dma_start(V[g][:], v_d[b, :, g]).then_inc(loaded[g], 16)

            def rows(b, g):
                n = b * NG + g
                sp.wait_ge(nm_split, n * 2 + 1)
                sp.dma_start(Q[g][32:33].bitcast(F32), NMH[:].bitcast(F32)).then_inc(rows_in[g], 16)
                sp.wait_ge(nm_split, n * 2 + 2)
                sp.dma_start(Q[g][33:34].bitcast(F32), NML[:].bitcast(F32)).then_inc(rows_in[g], 16)

            def store(b, g):
                sp.wait_ge(o_done, b * NG + g + 1)
                sp.dma_start(o_d[g * GH:(g + 1) * GH, b].rearrange("h r c -> r h c"),
                             OX[g % 2][:].rearrange("r h j d -> r h (j d)")).then_inc(o_stored[g % 2], 16)

            sp.dma_start(SEL[:], d["sel"]).then_inc(sel_in, 16)
            for g in range(NG):
                load(0, g)
                if g >= 2:
                    rows(0, g - 2)
            with sp.Fori(1, B) as b:
                for g in range(NG):
                    load(b, g)
                    rows(*batch_of(b, g, -2))
                    store(*batch_of(b, g, -4))
            for g in range(NG):
                if g < 2:
                    rows(B - 1, g + 2)
                store(B - 1, g)
            for r in range(2):
                sp.wait_ge(o_stored[r], B * NG // 2 * 16)

        @block.gpsimd
        def _(pool):
            def split(b, g):
                n = b * NG + g
                pool.wait_ge(nm_copied, n + 1)
                pb, pg = batch_of(b, g, -1)
                wait(pool, rows_in[pg], (pb + 1) * 32)
                nc.gpsimd.tensor_tensor(NMH[:], NMF[:], ZERO[:], ALU.add).then_inc(nm_split, 1)
                pool.wait_ge(nm_split, n * 2 + 1)
                nc.gpsimd.tensor_tensor(NML[:], NMF[:], NMH[:].bitcast(F32), ALU.subtract).then_inc(nm_split, 1)

            nc.gpsimd.memset(ZERO[:], 0.0).then_inc(zero_set, 1)
            pool.wait_ge(zero_set, 1)
            for g in range(NG):
                split(0, g)
            with pool.Fori(1, B) as b:
                for g in range(NG):
                    split(b, g)

        @block.tensor
        def _(pe):
            def smax_unit(b, g, h, qt):
                n = (b * NG + g) * 16 + h * TT + qt
                if h == 0 and qt == 0:
                    pe.wait_ge(loaded[g], (b + 1) * 48)
                wait(pe, sm_reduced, n - 1)
                nc.tensor.matmul(pM[:, qt % 2, :], Q[g][0:32, h, qt * P:(qt + 1) * P], K[g][0:32, h, :],
                                 start=True, stop=True).then_inc(sm_filled, 1)

            def st_unit(b, g, kt, u):
                n = (b * NG + g) * 8 + kt * 2 + u
                if kt == 0 and u == 0:
                    pe.wait_ge(rows_in[g], (b + 1) * 32)
                wait(pe, exp_done, n - 1)
                for j in range(2):
                    last = nc.tensor.matmul(pS[u][:, j, :], K[g][:, 2 * u + j, kt * P:(kt + 1) * P],
                                            Q[g][:, 2 * u + j, :], start=True, stop=True)
                last.then_inc(st_filled, 1)

            def pv(b, g, kt):
                s = b * NG + g
                pe.wait_ge(exp_done, s * 8 + kt * 2 + 2)
                if kt == 0:
                    wait(pe, ot_copied, s)
                for h in range(GH):
                    last = nc.tensor.matmul(pO[32 * h:32 * h + 32, :], V[g][:, kt, h, :], PR[kt][:, h, :],
                                            start=(kt == 0), stop=(kt == TT - 1), skip_group_check=True)
                last.then_inc(pv_done, 1)

            def turn_max(b, g):
                s = b * NG + g
                pe.wait_ge(sm_reduced, s * 16 + 16)
                wait(pe, o_done, s - 2)
                for qt in range(TT):
                    last = nc.tensor.transpose(pX[0:GH, qt * P:(qt + 1) * P], NM[g % 2][:, qt, :], IDENT[:])
                last.then_inc(nm_turned, 1)

            def turn_out(b, g, next_turned):
                s = b * NG + g
                pe.wait_ge(ot_copied, s + 1)
                if next_turned:
                    pe.wait_ge(nm_copied, s + 3)
                else:
                    pe.wait_ge(o_done, s)
                tokens = OT[:].rearrange("p (r j) -> p j r", j=16)
                for j in range(16):
                    m = 32 * (j % 4)
                    last = nc.tensor.matmul(pX[m:m + 32, (j // 4) * 36:(j // 4 + 1) * 36], tokens[:, j, :], SEL[:],
                                            start=True, stop=True)
                last.then_inc(o_turned, 1)

            def body(b, first, last):
                for g in range(NG):
                    b2, g2 = batch_of(b, g, 2)
                    b1, g1 = batch_of(b, g, 1)
                    b0, g0 = batch_of(b, g, -1)
                    ahead = not (last and g >= NG - 2)
                    for kt in range(TT):
                        if ahead:
                            smax_unit(b2, g2, kt, 0)
                        st_unit(b, g, kt, 0)
                        if ahead:
                            smax_unit(b2, g2, kt, 1)
                        if kt == 0 and not (last and g == NG - 1):
                            turn_max(b1, g1)
                        if kt > 0:
                            pv(b, g, kt - 1)
                        if ahead:
                            smax_unit(b2, g2, kt, 2)
                        st_unit(b, g, kt, 1)
                        if kt == 1 and not (first and g == 0):
                            turn_out(b0, g0, not (last and g == NG - 1))
                        if ahead:
                            smax_unit(b2, g2, kt, 3)
                    pv(b, g, TT - 1)

            pe.wait_ge(sel_in, 16)
            for h in range(GH):
                for qt in range(TT):
                    smax_unit(0, 0, h, qt)
            for h in range(GH):
                for qt in range(TT):
                    smax_unit(0, 1, h, qt)
                if h == 0:
                    turn_max(0, 0)
            over_batches(pe, body)
            turn_out(B - 1, NG - 1, False)

        @block.scalar
        def _(act):
            def exp_unit(b, g, kt, u):
                s = b * NG + g
                act.wait_ge(st_filled, s * 8 + kt * 2 + u + 1)
                if u == 0:
                    wait(act, pv_done, (s - 1) * TT + kt + 1)
                nc.scalar.activation(PR[kt][:, 2 * u:2 * u + 2, :], pS[u][:], ACT.Exp, scale=SCALE_A)\
                    .then_inc(exp_done, 1)

            def copy_max(b, g):
                s = b * NG + g
                act.wait_ge(nm_turned, s + 1)
                wait(act, nm_split, s * 2)
                nc.scalar.activation(NMF[:], pX[0:GH, :], ACT.Copy).then_inc(nm_copied, 1)

            def copy_out(b, g):
                s = b * NG + g
                act.wait_ge(pv_done, s * TT + TT)
                wait(act, o_turned, s)
                nc.scalar.activation(OT[:], pO[:], ACT.Copy).then_inc(ot_copied, 1)

            def body(b, first, last):
                for g in range(NG):
                    for kt in range(TT):
                        exp_unit(b, g, kt, 0)
                        if kt == 0 and not (first and g == 0):
                            copy_out(*batch_of(b, g, -1))
                        exp_unit(b, g, kt, 1)
                        if kt == 0 and not (last and g == NG - 1):
                            copy_max(*batch_of(b, g, 1))

            copy_max(0, 0)
            over_batches(act, body)
            copy_out(B - 1, NG - 1)

        @block.vector
        def _(dve):
            def reduce_unit(b, g, h, qt):
                s = b * NG + g
                dve.wait_ge(sm_filled, s * 16 + h * TT + qt + 1)
                if h == 0 and qt == 0:
                    wait(dve, nm_turned, s - 1)
                nc.vector.tensor_reduce(NM[g % 2][:, qt, h:h + 1], pM[:, qt % 2, :], AX.X, ALU.max,
                                        negate=True).then_inc(sm_reduced, 1)

            def finish(b, g):
                s = b * NG + g
                dve.wait_ge(o_turned, s + 1)
                o = pX[:, 0:4 * 36].rearrange("p (k c) -> p k c", k=4)
                nc.vector.reciprocal(RD[:], o[:, :, 32:36]).then_inc(o_recip, 1)
                dve.wait_ge(o_recip, s + 1)
                pb, pg = batch_of(b, g, -2)
                wait(dve, o_stored[g % 2], (pb * 2 + pg // 2 + 1) * 16)
                for m in range(4):
                    part = slice(32 * m, 32 * m + 32)
                    dst = OX[g % 2][:, :, m:16:4, :].rearrange("r h k d -> r k h d")
                    last = nc.vector.tensor_tensor(dst, o[part, :, 0:32].rearrange("p k (h d) -> p k h d", h=GH),
                                                   RD[part].unsqueeze(3).broadcast_to([32, 4, GH, DA]), ALU.mult)
                last.then_inc(o_done, 1)

            def body(b, first, last):
                for g in range(NG):
                    ahead = not (last and g >= NG - 2)
                    for h in range(GH):
                        if ahead:
                            for qt in range(TT):
                                reduce_unit(*batch_of(b, g, 2), h, qt)
                        if h == 1 and not (first and g == 0):
                            finish(*batch_of(b, g, -1))

            for g in range(NG):
                nc.vector.memset(Q[g][:].bitcast(F32), 0.0)
                last = nc.vector.memset(K[g][:].bitcast(F32), 0.0)
            last.then_inc(stacks_set, 1)
            dve.wait_ge(stacks_set, 1)
            for g in range(NG):
                nc.vector.memset(K[g][32:34].bitcast(F32), 1.0).then_inc(stacks_set, 1)
            for g in range(2):
                for h in range(GH):
                    for qt in range(TT):
                        reduce_unit(0, g, h, qt)
            over_batches(dve, body)
            finish(B - 1, NG - 1)

def phase_ffn(nc, X, IDENT, d, name, attn=None, tail=None, out=None):
    with ExitStack() as ctx:
        sb = lambda n, s, t: ctx.enter_context(nc.sbuf_tensor(f"{name}_{n}", s, t))
        ps = lambda n, s, t: ctx.enter_context(nc.psum_tensor(f"{name}_{n}", s, t))
        sem = lambda n: ctx.enter_context(nc.semaphore(f"{name}_{n}"))
        Q1 = sb("fc1_q", [P, FF], I32)
        S1 = sb("fc1_scale", [P, FF], F32)
        W1 = sb("fc1_w", [P, FF], F32)
        W1H = sb("fc1_hi", [P, FF], F32R)
        W1L = sb("fc1_lo", [P, FF], F32R)
        Q2 = sb("fc2_q", [P, FT, P], I32)
        S2 = sb("fc2_scale", [P, FT, P], F32)
        W2 = sb("fc2_w", [P, FT, P], F32)
        GB = sb("gamma_beta", [P, 2], F32)
        B1 = sb("fc1_bias", [P, FT], F32)
        B2 = sb("fc2_bias", [P, P], F32)
        stats = sb("ln_stats", [P, TT, 6], F32)
        mv = sb("ln_mv", [P, TT, 2], F32)
        root = [sb(f"ln_root{k}", [P, TT], F32) for k in range(6)]
        minus_half = sb("minus_half", [P, TT], F32)
        XN = sb("xn", [P, TT, P], F32)
        H = sb("h", [P, TT, P], F32)
        XS = sb("xn_bias", [P, TT, P], F32)
        XR = sb("residual", [P, TT, P], F32)
        HT = sb("ht", [P, N], F32)
        HTH = sb("ht_hi", [P, N], F32R)
        HTL = sb("ht_lo", [P, N], F32R)
        Y = sb("silu", [P, FT, N], F32)
        pT = ps("p_t", [P, N], F32)
        pF = ps("p_f", [P, 2, N], F32)
        pZ = ps("p_z", [P, TT, P], F32)

        w_in = sem("w_in")
        w_deq = sem("w_deq")
        w_split = sem("w_split")
        pool_set = sem("pool_set")
        ln_stats = sem("ln_stats")
        ln_mv = sem("ln_mv")
        ln_root = sem("ln_root")
        ln_rstd = sem("ln_rstd")
        h_ready = sem("h")
        xn_ready = sem("xn")
        ht_turned = sem("ht_turned")
        ht_full = sem("ht_full")
        ht_hi = sem("ht_hi")
        ht_lo = sem("ht_lo")
        fc1_done = sem("fc1")
        silu_done = sem("silu")
        fc2_done = sem("fc2")
        xs_ready = sem("xn_plus_bias")
        xr_ready = sem("residual")
        x_new = sem("x_new")
        W_LOADS = 7
        if attn is not None:
            o_d = attn
            WP = sb("proj_w", [P, P], F32)
            PB = sb("proj_b", [P, P], F32)
            OT = sb("o_t", [P, N], F32)
            pP = ps("p_proj", [P, TT, P], F32)
            OC = sb("o_now", [P, TT, P], F32)
            oc_in = sem("oc_in")
            biased = sem("x_biased")
            ot_turned = sem("ot_turned")
            ot_copied = sem("ot_copied")
            proj_done = sem("proj")
            x_mid = sem("x_mid")
            W_LOADS += 2
        if tail is not None:
            XTH_all, XTL_all, v_d = tail
            WV = sb("v_w", [P, HB * DB], F32)
            WVH = sb("v_w_hi", [P, HB * DB], F32R)
            WVL = sb("v_w_lo", [P, HB * DB], F32R)
            WO = sb("o_w", [P, NP, P], F32)
            BV = sb("v_b", [P, NP], F32)
            BVB = sb("v_b_wide", [P, NP, P], F32)
            BO = sb("o_b", [P, P], F32)
            BOV = sb("o_b_total", [P, P], F32)
            stats3 = sb("ln3_stats", [P, TT, 6], F32)
            mv3 = sb("ln3_mv", [P, TT, 2], F32)
            ve3 = sb("ln3_ve", [P, TT], F32)
            rstd3 = sb("ln3_rstd", [P, TT], F32)
            XN3 = sb("xn3", [P, TT, P], F32)
            XTH = sb("xt_hi", [P, N], F32R)
            XTL = sb("xt_lo", [P, N], F32R)
            V = sb("v", [P, TT, HB * DB], F32)
            pT3 = ps("p_t3", [P, N], F32)
            pV = ps("p_v", [P, 2, N], F32)
            bias_wide = sem("bias_wide")
            bias_sum = sem("bias_sum")
            bias_total = sem("bias_total")
            ln3_stats = sem("ln3_stats")
            ln3_mv = sem("ln3_mv")
            ln3_root = sem("ln3_root")
            ln3_rstd = sem("ln3_rstd")
            xn3_ready = sem("xn3")
            x_out_biased = sem("x_out_biased")
            xt_turned = sem("xt_turned")
            xt_hi = sem("xt_hi")
            xt_lo = sem("xt_lo")
            v_mm = sem("v_mm")
            v_act = sem("v_act")
            v_dve = sem("v_dve")
            xt_kept = sem("xt_kept")
            v_stored = sem("v_stored")
            W_LOADS += 4
        stored = sem("stored")

        block = ctx.enter_context(nc.Block())

        def tiles(c):
            return bass.ds(c * TT, TT) if not isinstance(c, int) else slice(c * TT, c * TT + TT)

        def over_batches(eng, first, ahead, body, behind):
            first(0)
            body(0, True, False)
            with eng.Fori(1, B - 1) as c:
                body(c, True, True)
            body(B - 1, False, True)
            behind(B - 1)

        @block.sync
        def _(sp):
            sp.dma_start(Q1[:], d["fc1_q"]).then_inc(w_in, 16)
            sp.dma_start(S1[:], d["fc1_s"].partition_broadcast(P)).then_inc(w_in, 16)
            sp.dma_start(Q2[:], d["fc2_q"].rearrange("(f p) n -> p f n", p=P)).then_inc(w_in, 16)
            sp.dma_start(S2[:], d["fc2_s"].partition_broadcast(P)).then_inc(w_in, 16)
            sp.dma_start(GB[:], d["gb"]).then_inc(w_in, 16)
            sp.dma_start(B1[:], d["b1"]).then_inc(w_in, 16)
            sp.dma_start(B2[:], d["b2"].partition_broadcast(P)).then_inc(w_in, 16)
            if attn is not None:
                sp.dma_start(WP[:], d["wp"]).then_inc(w_in, 16)
                sp.dma_start(PB[:], d["bp"].partition_broadcast(P)).then_inc(w_in, 16)
            if tail is not None:
                sp.dma_start(WV[:], d["wv2"]).then_inc(w_in, 16)
                sp.dma_start(WO[:], d["wo"].rearrange("(p r) n -> r p n", r=P)).then_inc(w_in, 16)
                sp.dma_start(BV[:], d["bv2"]).then_inc(w_in, 16)
                sp.dma_start(BO[:], d["bo"].partition_broadcast(P)).then_inc(w_in, 16)

            if attn is not None:
                o_rows = o_d.rearrange("(c a) b r n -> c (a b r) n", c=B)

            def load_o(c):
                if attn is not None:
                    wait(sp, ot_turned, c)
                    sp.dma_start(OC[:], o_rows[c].rearrange("(t p) n -> p t n", p=P)).then_inc(oc_in, 16)

            def keep(c):
                if tail is not None:
                    waits(sp, (w_in, 16 * W_LOADS), (xt_hi, c + 1))
                    sp.dma_start(XTH_all[:, bass.ds(c * N, N)].bitcast(F32), XTH[:].bitcast(F32)).then_inc(xt_kept, 16)
                    waits(sp, (w_in, 16 * W_LOADS), (xt_lo, c + 1))
                    sp.dma_start(XTL_all[:, bass.ds(c * N, N)].bitcast(F32), XTL[:].bitcast(F32)).then_inc(xt_kept, 16)
                    for t in range(TT):
                        sp.wait_ge(v_act, c * TT + t + 1)
                        sp.wait_ge(v_dve, c * TT + t + 1)
                        sp.dma_start(v_d[c, :, :, t, :].rearrange("j p e -> p j e"),
                                     V[:, t, :].rearrange("p (j e) -> p j e", j=NP)).then_inc(v_stored, 16)

            def body(c, ahead, behind):
                if ahead:
                    load_o(c + 1)
                if behind:
                    keep(c - 1)

            if tail is not None:
                over_batches(sp, load_o, None, body, keep)
                sp.wait_ge(xt_kept, 32 * B)
                sp.wait_ge(v_stored, 16 * TT * B)
            if out is not None:
                with sp.Fori(0, B) as c:
                    sp.wait_ge(x_new, c + 1)
                    sp.dma_start(out[c].rearrange("(t p) d -> p t d", p=P), X[:, tiles(c), :]).then_inc(stored, 16)
                sp.wait_ge(stored, 16 * B)

        @block.gpsimd
        def _(pool):
            def bias_x(c):
                nc.gpsimd.tensor_tensor(X[:, tiles(c), :], X[:, tiles(c), :],
                                        PB[:].unsqueeze(1).broadcast_to([P, TT, P]), ALU.add).then_inc(biased, 1)

            def roots(c):
                def step(k, ins):
                    ins.then_inc(ln_root, 1)
                    waits(pool, (pool_set, 1), (ln_root, c * 5 + k))
                waits(pool, (pool_set, 1), (ln_mv, c + 1), (xn_ready, c))
                step(1, nc.gpsimd.tensor_scalar(root[0][:], mv[:, :, 1], EPS, None, ALU.add))
                step(2, nc.gpsimd.tensor_tensor(root[1][:], root[0][:], minus_half[:], ALU.pow))
                step(3, nc.gpsimd.tensor_tensor(root[2][:], root[1][:], root[1][:], ALU.mult))
                step(4, nc.gpsimd.tensor_tensor(root[3][:], root[2][:], mv[:, :, 1], ALU.mult))
                step(5, nc.gpsimd.tensor_scalar(root[4][:], root[3][:], EPS, None, ALU.add))
                nc.gpsimd.tensor_tensor(root[2][:], root[4][:], minus_half[:], ALU.pow).then_inc(ln_rstd, 1)
                pool.wait_ge(ln_rstd, c * 2 + 1)
                nc.gpsimd.tensor_tensor(root[5][:], root[2][:], root[1][:], ALU.mult).then_inc(ln_rstd, 1)

            def residual(c):
                pool.wait_ge(xn_ready, c + 1)
                nc.gpsimd.tensor_tensor(XS[:], XN[:], B2[:].unsqueeze(1).broadcast_to([P, TT, P]), ALU.add)\
                    .then_inc(xs_ready, 1)
                waits(pool, (pool_set, 1), (xs_ready, c + 1), (x_new, c))
                nc.gpsimd.tensor_tensor(XR[:], XS[:], X[:, tiles(c), :], ALU.add).then_inc(xr_ready, 1)

            def first(c):
                if attn is not None:
                    bias_x(c)
                roots(c)
                residual(c)

            def root3(c):
                waits(pool, (pool_set, 1), (ln3_mv, c + 1))
                nc.gpsimd.tensor_scalar(ve3[:], mv3[:, :, 1], EPS, None, ALU.add).then_inc(ln3_root, 1)
                pool.wait_ge(ln3_root, c + 1)
                nc.gpsimd.tensor_tensor(rstd3[:], ve3[:], minus_half[:], ALU.pow).then_inc(ln3_rstd, 1)

            def bias_out(c):
                waits(pool, (pool_set, 1), (xn3_ready, c + 1))
                nc.gpsimd.tensor_tensor(X[:, tiles(c), :], X[:, tiles(c), :],
                                        BOV[:].unsqueeze(1).broadcast_to([P, TT, P]), ALU.add)\
                    .then_inc(x_out_biased, 1)

            def body(c, ahead, behind):
                if ahead:
                    if attn is not None:
                        bias_x(c + 1)
                    roots(c + 1)
                if tail is not None:
                    root3(c)
                if ahead:
                    residual(c + 1)
                if tail is not None:
                    bias_out(c)

            nc.gpsimd.memset(minus_half[:], -0.5).then_inc(pool_set, 1)
            pool.wait_ge(pool_set, 1)
            pool.wait_ge(w_in, 16 * W_LOADS)
            pool.wait_ge(w_deq, 5)
            if tail is not None:
                pool.wait_ge(bias_total, 1)
            over_batches(pool, first, None, body, lambda c: None)

        @block.scalar
        def _(act):
            def copy_ot(c):
                act.wait_ge(ot_turned, c + 1)
                wait(act, proj_done, c)
                nc.scalar.activation(OT[:], pT[:], ACT.Copy).then_inc(ot_copied, 1)

            def copy_ht(c):
                act.wait_ge(ht_turned, c + 1)
                wait(act, ht_lo, c)
                wait(act, ht_hi, c)
                nc.scalar.activation(HT[:], pT[:], ACT.Identity, scale=GB[:, 0:1], bias=GB[:, 1:2])\
                    .then_inc(ht_full, 1)

            def silu(c, f):
                act.wait_ge(fc1_done, c * FT + f + 1)
                if f == 0:
                    wait(act, fc2_done, c)
                nc.scalar.activation(Y[:, f, :], pF[:, f % 2, :], ACT.Silu, bias=B1[:, f:f + 1])\
                    .then_inc(silu_done, 1)

            def turn_hi(c):
                act.wait_ge(xt_turned, c + 1)
                wait(act, v_mm, c * 8)
                wait(act, xt_kept, c * 32)
                nc.scalar.activation(XTH[:], pT3[:], ACT.Copy).then_inc(xt_hi, 1)

            def v_left(c, t):
                act.wait_ge(v_mm, c * 8 + t * 2 + 1)
                if t == 0:
                    wait(act, v_stored, c * 64)
                nc.scalar.activation(V[:, t, 0:N], pV[:, 0, :], ACT.Copy).then_inc(v_act, 1)

            def first(c):
                if attn is not None:
                    copy_ot(c)
                copy_ht(c)

            def body(c, ahead, behind):
                if behind and tail is not None:
                    turn_hi(c - 1)
                silu(c, 0)
                silu(c, 1)
                if ahead and attn is not None:
                    copy_ot(c + 1)
                silu(c, 2)
                silu(c, 3)
                if behind and tail is not None:
                    for t in range(TT):
                        v_left(c - 1, t)
                if ahead:
                    copy_ht(c + 1)

            def behind(c):
                if tail is not None:
                    turn_hi(c)
                    for t in range(TT):
                        v_left(c, t)

            act.wait_ge(w_in, 16 * W_LOADS)
            over_batches(act, first, None, body, behind)

        @block.tensor
        def _(pe):
            def turn_ot(c):
                pe.wait_ge(oc_in, (c + 1) * 16)
                wait(pe, ht_full, c)
                for t in range(TT):
                    last = nc.tensor.transpose(pT[:, t * P:(t + 1) * P], OC[:, t, :], IDENT[:])
                last.then_inc(ot_turned, 1)

            def project(c):
                pe.wait_ge(ot_copied, c + 1)
                wait(pe, x_mid, c)
                for t in range(TT):
                    last = nc.tensor.matmul(pP[:, t, :], OT[:, t * P:(t + 1) * P], WP[:], start=True, stop=True)
                last.then_inc(proj_done, 1)

            def turn_h(c):
                pe.wait_ge(h_ready, c + 1)
                if attn is not None:
                    pe.wait_ge(ot_copied, c + 1)
                else:
                    wait(pe, ht_full, c)
                for t in range(TT):
                    last = nc.tensor.transpose(pT[:, t * P:(t + 1) * P], H[:, t, :], IDENT[:])
                last.then_inc(ht_turned, 1)

            def fc1(c, f):
                if f == 0:
                    pe.wait_ge(ht_hi, c + 1)
                    pe.wait_ge(ht_lo, c + 1)
                wait(pe, silu_done, c * FT + f - 1)
                w = slice(f * P, (f + 1) * P)
                nc.tensor.matmul(pF[:, f % 2, :], W1H[:, w], HTH[:], start=True, stop=False)
                nc.tensor.matmul(pF[:, f % 2, :], W1L[:, w], HTH[:], start=False, stop=False)
                nc.tensor.matmul(pF[:, f % 2, :], W1H[:, w], HTL[:], start=False, stop=True).then_inc(fc1_done, 1)

            def fc2(c):
                pe.wait_ge(silu_done, c * FT + FT)
                wait(pe, x_new, c)
                for t in range(TT):
                    for f in range(FT):
                        last = nc.tensor.matmul(pZ[:, t, :], Y[:, f, t * P:(t + 1) * P], W2[:, f, :],
                                                start=(f == 0), stop=(f == FT - 1))
                last.then_inc(fc2_done, 1)

            def turn_xt(c):
                pe.wait_ge(xn3_ready, c + 1)
                wait(pe, xt_lo, c)
                for t in range(TT):
                    last = nc.tensor.transpose(pT3[:, t * P:(t + 1) * P], XN3[:, t, :], IDENT[:])
                last.then_inc(xt_turned, 1)

            def values(c, t):
                if t == 0:
                    pe.wait_ge(xt_hi, c + 1)
                    pe.wait_ge(xt_lo, c + 1)
                xt = slice(t * P, (t + 1) * P)
                for half in range(2):
                    w = slice(half * N, (half + 1) * N)
                    wait(pe, (v_act, v_dve)[half], c * TT + t)
                    nc.tensor.matmul(pV[:, half, :], XTH[:, xt], WVH[:, w], start=True, stop=False)
                    nc.tensor.matmul(pV[:, half, :], XTH[:, xt], WVL[:, w], start=False, stop=False)
                    nc.tensor.matmul(pV[:, half, :], XTL[:, xt], WVH[:, w], start=False, stop=True)\
                        .then_inc(v_mm, 1)

            def first(c):
                if attn is not None:
                    turn_ot(c)
                    project(c)
                turn_h(c)

            def body(c, ahead, behind):
                if behind and tail is not None:
                    turn_xt(c - 1)
                fc1(c, 0)
                fc1(c, 1)
                if ahead and attn is not None:
                    turn_ot(c + 1)
                fc1(c, 2)
                fc1(c, 3)
                if ahead and attn is not None:
                    project(c + 1)
                if behind and tail is not None:
                    values(c - 1, 0)
                    values(c - 1, 1)
                fc2(c)
                if behind and tail is not None:
                    values(c - 1, 2)
                    values(c - 1, 3)
                if ahead:
                    turn_h(c + 1)

            def behind(c):
                if tail is not None:
                    turn_xt(c)
                    for t in range(TT):
                        values(c, t)

            pe.wait_ge(w_split, 2 if tail is None else 4)
            pe.wait_ge(w_in, 16 * W_LOADS)
            if tail is not None:
                pe.wait_ge(bias_wide, 1)
                for j in range(NP):
                    last = nc.tensor.matmul(pV[:, 0, 0:P], BVB[:, j, :], WO[:, j, :], start=(j == 0), stop=(j == NP - 1))
                last.then_inc(bias_sum, 1)
                pe.wait_ge(bias_total, 1)
            over_batches(pe, first, None, body, behind)

        @block.vector
        def _(dve):
            def x_middle(c):
                dve.wait_ge(proj_done, c + 1)
                dve.wait_ge(biased, c + 1)
                nc.vector.tensor_tensor(X[:, tiles(c), :], pP[:], X[:, tiles(c), :], ALU.add).then_inc(x_mid, 1)

            def tile_of(c):
                return lambda t: X[:, c * TT + t, :]

            def ln(c):
                if attn is not None:
                    x_middle(c)
                    waits(dve, (w_in, 16 * W_LOADS), (x_mid, c + 1), (ln_rstd, c * 2))
                else:
                    waits(dve, (w_in, 16 * W_LOADS), (ln_rstd, c * 2))
                mean_and_variance(nc, dve, ln_stats, c, tile_of(c), stats, mv, (w_in, 16 * W_LOADS)).then_inc(ln_mv, 1)

            def norms(c):
                dve.wait_ge(ln_rstd, c * 2 + 2)
                wait(dve, ht_turned, c)
                wait(dve, xs_ready, c)
                normalize(nc, tile_of(c), H, mv, root[5]).then_inc(h_ready, 1)
                normalize(nc, tile_of(c), XN, mv, root[1]).then_inc(xn_ready, 1)

            def split_h(c):
                dve.wait_ge(ht_full, c + 1)
                wait(dve, fc1_done, c * FT)
                nc.vector.tensor_copy(HTH[:], HT[:]).then_inc(ht_hi, 1)
                dve.wait_ge(ht_hi, c + 1)
                nc.vector.tensor_tensor(HTL[:], HT[:], HTH[:].bitcast(F32), ALU.subtract).then_inc(ht_lo, 1)

            def x_final(c):
                dve.wait_ge(fc2_done, c + 1)
                dve.wait_ge(xr_ready, c + 1)
                nc.vector.scalar_tensor_tensor(X[:, tiles(c), :], pZ[:], 0.5, XR[:], ALU.mult, ALU.add)\
                    .then_inc(x_new, 1)

            def ln3(c):
                waits(dve, (w_in, 16 * W_LOADS), (x_new, c + 1), (ln3_rstd, c))
                mean_and_variance(nc, dve, ln3_stats, c, tile_of(c), stats3, mv3, (w_in, 16 * W_LOADS)).then_inc(ln3_mv, 1)

            def norm3(c):
                dve.wait_ge(ln3_rstd, c + 1)
                wait(dve, xt_turned, c)
                normalize(nc, tile_of(c), XN3, mv3, rstd3).then_inc(xn3_ready, 1)

            def turn_lo(c):
                dve.wait_ge(xt_hi, c + 1)
                wait(dve, v_mm, c * 8)
                wait(dve, xt_kept, c * 32)
                nc.vector.tensor_tensor(XTL[:], pT3[:], XTH[:].bitcast(F32), ALU.subtract).then_inc(xt_lo, 1)

            def v_right(c, t):
                dve.wait_ge(v_mm, c * 8 + t * 2 + 2)
                if t == 0:
                    wait(dve, v_stored, c * 64)
                nc.vector.tensor_copy(V[:, t, N:2 * N], pV[:, 1, :]).then_inc(v_dve, 1)

            def first(c):
                ln(c)
                norms(c)
                split_h(c)

            def body(c, ahead, behind):
                if behind and tail is not None:
                    turn_lo(c - 1)
                if ahead:
                    ln(c + 1)
                if behind and tail is not None:
                    v_right(c - 1, 0)
                    v_right(c - 1, 1)
                if ahead:
                    norms(c + 1)
                x_final(c)
                if tail is not None:
                    ln3(c)
                if behind and tail is not None:
                    v_right(c - 1, 2)
                    v_right(c - 1, 3)
                if tail is not None:
                    norm3(c)
                if ahead:
                    split_h(c + 1)

            def behind(c):
                if tail is not None:
                    turn_lo(c)
                    for t in range(TT):
                        v_right(c, t)

            dve.wait_ge(w_in, 16 * W_LOADS)
            nc.vector.scalar_tensor_tensor(W1[:], Q1[:], -128.0, S1[:], ALU.add, ALU.mult).then_inc(w_deq, 1)
            nc.vector.scalar_tensor_tensor(W2[:], Q2[:], -128.0, S2[:], ALU.add, ALU.mult).then_inc(w_deq, 1)
            nc.vector.tensor_scalar(B2[:], B2[:], 0.5, None, ALU.mult).then_inc(w_deq, 3)
            dve.wait_ge(w_deq, 5)
            nc.vector.tensor_copy(W1H[:], W1[:]).then_inc(w_split, 1)
            dve.wait_ge(w_split, 1)
            nc.vector.tensor_tensor(W1L[:], W1[:], W1H[:].bitcast(F32), ALU.subtract).then_inc(w_split, 1)
            if tail is not None:
                nc.vector.tensor_copy(WVH[:], WV[:]).then_inc(w_split, 1)
                dve.wait_ge(w_split, 3)
                nc.vector.tensor_tensor(WVL[:], WV[:], WVH[:].bitcast(F32), ALU.subtract).then_inc(w_split, 1)
                for j in range(NP):
                    last = nc.vector.tensor_copy(BVB[:, j, :], BV[:, j:j + 1].broadcast_to([P, P]))
                last.then_inc(bias_wide, 1)
                dve.wait_ge(bias_sum, 1)
                nc.vector.tensor_tensor(BOV[:], pV[:, 0, 0:P], BO[:], ALU.add).then_inc(bias_total, 1)
            over_batches(dve, first, None, body, behind)

def phase_b_attention(nc, X, IDENT, d, XTH, XTL, v_d):
    with ExitStack() as ctx:
        sb = lambda n, s, t: ctx.enter_context(nc.sbuf_tensor(f"b_{n}", s, t))
        ps = lambda n, s, t: ctx.enter_context(nc.psum_tensor(f"b_{n}", s, t))
        sem = lambda n: ctx.enter_context(nc.semaphore(f"b_{n}"))
        MH, ML = DB, DB + 32
        R = range(2)
        WQK = [sb(f"w{r}", [P, 2, P], F32) for r in R]
        WH = [sb(f"w_hi{r}", [P, 2, P], F32R) for r in R]
        WL = [sb(f"w_lo{r}", [P, 2, P], F32R) for r in R]
        V = [sb(f"v{r}", [P, TT, P], F32) for r in R]
        Q1 = [sb(f"q1_{r}", [P, 2, N], F32R) for r in R]
        K1 = [sb(f"k1_{r}", [P, 2, N], F32R) for r in R]
        Q2 = [sb(f"q2_{r}", [P, 2, N], F32R) for r in R]
        K2 = [sb(f"k2_{r}", [P, 2, N], F32R) for r in R]
        BQ = sb("bq", [DB, HB], F32)
        BK = sb("bk", [DB, HB], F32)
        WO = sb("wo", [P, NP, P], F32)
        GATHER = sb("gather_den", [P, 2, 32], F32)
        SPREAD = sb("spread_den", [P, TT, P], F32)
        ZERO = sb("zero", [P, 2, P], F32)
        EYE = sb("eye", [P, P], BF16)
        MQ = sb("mask_q", [P, 2 * P], BF16)
        MK = sb("mask_k", [P, 3 * P], BF16)
        PA = [sb(f"probs_a{h}", [P, 2, N], F32) for h in R]
        PB = [sb(f"probs_b{h}", [P, N], F32) for h in R]
        DS = [sb(f"den_sum{h}", [P, N - P], F32) for h in R]
        NM = [sb(f"neg_max{r}", [P, TT, 2], F32) for r in R]
        RDC = sb("recip_den", [P, P], F32)
        RD = sb("recip_den_rows", [P, N], F32)
        Z = [sb(f"z{r}", [P, N], F32) for r in R]
        pM = ps("p_max", [P, 2, N], F32)
        pA = ps("p_scores_a", [P, 2 * N], F32)
        pB = ps("p_scores_b", [P, N], F32)
        pZ = ps("p_z", [P, N], F32)
        pO = ps("p_out", [P, N], F32)
        pT = ps("p_max_rows", [2, N], F32)

        const_in = sem("const_in")
        masks_set = sem("masks_set")
        stacks_set = sem("stacks_set")
        w_in = [sem(f"w_in{r}") for r in R]
        v_in = [sem(f"v_in{r}") for r in R]
        w_split = sem("w_split")
        q_mm = sem("q_mm")
        k_mm = sem("k_mm")
        hi_done = sem("hi")
        lo_done = sem("lo")
        copied = [sem(f"copied{r}") for r in R]
        sm_filled = sem("sm_filled")
        sm_reduced = sem("sm_reduced")
        nm_turned = sem("nm_turned")
        max_hi = sem("max_hi")
        max_lo = sem("max_lo")
        st_filled = sem("st_filled")
        exp_done = sem("exp")
        den_step = sem("den_step")
        pv_done = sem("pv")
        den_done = sem("den")
        den_spread = sem("den_spread")
        rd_copied = sem("recip_copied")
        recip_done = sem("recip")
        z_done = sem("z")
        wo_done = sem("wo_mm")
        x_added = sem("x_added")

        block = ctx.enter_context(nc.Block())

        HALF = NP // 2

        def over_slots(eng, body):
            body(0, 0, True, False, True)
            body(0, 1, False, False, True)
            with eng.Fori(1, B * HALF - 1) as m:
                body(m, 0, False, False, True)
                body(m, 1, False, False, True)
            body(B * HALF - 1, 0, False, False, False)
            body(B * HALF - 1, 1, False, True, False)

        def next_of(m, r):
            return (m, 1) if r == 0 else (m + 1, 0)

        def before(m, r):
            return (m, 0) if r == 1 else (m - 1, 1)

        def batch(m):
            return m // HALF

        def pair(m, r):
            return (m % HALF) * 2 + r

        def span(start, n):
            return slice(start, start + n) if isinstance(start, int) else bass.ds(start, n)

        def both_heads():
            return pT[:].rearrange("p (o n) -> p o n", o=1).to_broadcast([2, 2, N])

        @block.sync
        def _(sp):
            sp.dma_start(BQ[:], d["bq2"]).then_inc(const_in, 16)
            sp.dma_start(BK[:], d["bk2"]).then_inc(const_in, 16)
            sp.dma_start(WO[:], d["wo"].rearrange("(j r) n -> r j n", r=P)).then_inc(const_in, 16)

            def load_w(m, r):
                now = pair(m, r) if isinstance(m, int) else sp.snap(pair(m, r))
                waits(sp, (stacks_set, 2), (w_split, 2 * (2 * m + r) - 2))
                sp.dma_start(WQK[r][:], d["wqk2"][:, now]).then_inc(w_in[r], 16)

            def load_v(m, r):
                now = pair(m, r) if isinstance(m, int) else sp.snap(pair(m, r))
                rows_of = batch(m) if isinstance(m, int) else sp.snap(batch(m))
                waits(sp, (stacks_set, 2), (pv_done, 4 * (2 * m + r) - 4))
                sp.dma_start(V[r][:], v_d[rows_of, now]).then_inc(v_in[r], 16)

            def copy_high(m, r):
                sp.wait_ge(hi_done, 6 * (2 * m + r) + 2)
                sp.dma_start(Q2[r][0:DB].bitcast(F32), Q1[r][0:DB].bitcast(F32)).then_inc(copied[r], 16)

            def body(m, r, first, last, ahead):
                n = next_of(m, r)
                if ahead:
                    load_w(m + 1, r)
                if not last:
                    load_v(*n)
                if ahead:
                    copy_high(m + 1, r)

            sp.wait_ge(stacks_set, 2)
            for r in R:
                load_w(0, r)
            load_v(0, 0)
            copy_high(0, 0)
            copy_high(0, 1)
            over_slots(sp, body)

        @block.gpsimd
        def _(pool):
            def split(m, r):
                i = 2 * m + r
                pool.wait_ge(w_in[r], (m + 1) * 16)
                wait(pool, k_mm, i - 1)
                nc.gpsimd.tensor_tensor(WH[r][:], WQK[r][:], ZERO[:], ALU.add).then_inc(w_split, 1)
                pool.wait_ge(w_split, 2 * i + 1)
                nc.gpsimd.tensor_tensor(WL[r][:], WQK[r][:], WH[r][:].bitcast(F32), ALU.subtract)\
                    .then_inc(w_split, 1)

            def body(m, r, first, last, ahead):
                i = 2 * m + r
                if ahead:
                    split(m + 1, r)
                for h in R:
                    n = i * 6 + h * 3
                    pool.wait_ge(exp_done, i * 4 + h * 2 + 1)
                    wait(pool, den_done, i)
                    nc.gpsimd.tensor_tensor(DS[h][:], PA[h][:, 0, P:N], PA[h][:, 1, 0:N - P], ALU.add)\
                        .then_inc(den_step, 1)
                    pool.wait_ge(exp_done, i * 4 + h * 2 + 2)
                    for k in range(2):
                        pool.wait_ge(den_step, n + k + 1)
                        nc.gpsimd.tensor_tensor(DS[h][:, P:N - P], DS[h][:, P:N - P],
                                                PB[h][:, k * 256:k * 256 + 256], ALU.add).then_inc(den_step, 1)

            nc.gpsimd.memset(MQ[:], MASKED).then_inc(masks_set, 1)
            nc.gpsimd.memset(MK[:, 0:2 * P], MASKED).then_inc(masks_set, 1)
            nc.gpsimd.memset(SPREAD[:], 1.0).then_inc(masks_set, 1)
            nc.gpsimd.memset(GATHER[:], 0.0).then_inc(masks_set, 1)
            nc.gpsimd.memset(EYE[:], 1.0).then_inc(masks_set, 1)
            nc.gpsimd.memset(ZERO[:], 0.0).then_inc(masks_set, 1)
            pool.wait_ge(masks_set, 6)
            nc.gpsimd.affine_select(out=MQ[:], in_=MQ[:], compare_op=ALU.is_gt, fill=0.0, base=0,
                                    pattern=[[1, 2 * P]], channel_multiplier=-1).then_inc(masks_set, 1)
            nc.gpsimd.affine_select(out=MK[:, P:2 * P], in_=MK[:, P:2 * P], compare_op=ALU.is_gt, fill=0.0,
                                    base=0, pattern=[[-1, P]], channel_multiplier=1).then_inc(masks_set, 1)
            nc.gpsimd.affine_select(out=EYE[:], in_=EYE[:], compare_op=ALU.is_equal, fill=0.0, base=0,
                                    pattern=[[-1, P]], channel_multiplier=1).then_inc(masks_set, 1)
            nc.gpsimd.affine_select(out=SPREAD[:].rearrange("p t (h c) -> p t h c", h=2),
                                    in_=SPREAD[:].rearrange("p t (h c) -> p t h c", h=2),
                                    compare_op=ALU.is_equal, fill=0.0, base=0,
                                    pattern=[[-32, TT], [-16, 2], [0, DB]], channel_multiplier=1)\
                .then_inc(masks_set, 1)
            nc.gpsimd.memset(GATHER[:, 0, 0:16], 1.0).then_inc(masks_set, 1)
            nc.gpsimd.memset(GATHER[:, 1, 16:32], 1.0).then_inc(masks_set, 1)
            for r in R:
                split(0, r)
            over_slots(pool, body)

        @block.tensor
        def _(pe):
            def project(m, r, qk):
                i = 2 * m + r
                pe.wait_ge(w_split, 2 * i + 2)
                wait(pe, sm_reduced, 6 * i - 1 + qk)
                xt = span(batch(m) * N, N)
                u = pM[:, qk, :]
                nc.tensor.matmul(u, WH[r][:, qk, :], XTH[:, xt], start=True, stop=False)
                nc.tensor.matmul(u, WL[r][:, qk, :], XTH[:, xt], start=False, stop=False)
                nc.tensor.matmul(u, WH[r][:, qk, :], XTL[:, xt], start=False, stop=True)\
                    .then_inc((q_mm, k_mm)[qk], 1)

            def out_product(m, r):
                i = 2 * m + r
                pe.wait_ge(z_done, i + 1)
                for t in range(TT):
                    last = nc.tensor.matmul(pO[:, t * P:(t + 1) * P], Z[r][:, t * P:(t + 1) * P],
                                            WO[:, pair(m, r), :], start=True, stop=True)
                last.then_inc(wo_done, 1)

            def smax_unit(m, r, h, part):
                i = 2 * m + r
                if h == 0 and part == 0:
                    pe.wait_ge(hi_done, i * 6 + 4)
                    pe.wait_ge(lo_done, i * 4 + 2)
                elif h == 0 and part == 1:
                    pe.wait_ge(lo_done, i * 4 + 4)
                wait(pe, sm_reduced, i * 6 + h * 3 + part - 1)
                bank = pM[:, (h * 3 + part) % 2, :]
                for qt, keys in ((0, bank[:, 0:256]), (1, bank[:, 256:512])) if part == 0 else \
                        ((part + 1, bank[:, 0:(part + 2) * P]),):
                    nc.tensor.matmul(keys, Q1[r][:, h, qt * P:(qt + 1) * P], K1[r][:, h, 0:max(256, (qt + 1) * P)],
                                     start=True, stop=False)
                    if qt == 0:
                        last = nc.tensor.matmul(keys, EYE[:], MQ[:], start=False, stop=True)
                    else:
                        last = nc.tensor.matmul(keys[:, qt * P:(qt + 1) * P], EYE[:], MQ[:, 0:P], start=False, stop=True)
                last.then_inc(sm_filled, 1)

            def scores(m, r, h, part):
                i = 2 * m + r
                if h == 0 and part == 0:
                    pe.wait_ge(copied[r], (m + 1) * 16)
                    pe.wait_ge(max_lo, i + 1)
                if h == 0 and part == 1:
                    wait(pe, recip_done, i)
                wait(pe, exp_done, i * 4 + h * 2 + part - 1)
                for kt in (2 * part, 2 * part + 1):
                    q0 = min(kt * P, 256)
                    n = N - q0
                    bank = pA[:, kt * N:kt * N + n] if part == 0 else pB[:, (kt - 2) * 256:(kt - 2) * 256 + n]
                    keys = slice(kt * P, (kt + 1) * P)
                    nc.tensor.matmul(bank, K1[r][:, h, keys], Q1[r][:, h, q0:N], start=True, stop=False)
                    nc.tensor.matmul(bank, K2[r][:, h, keys], Q2[r][:, h, q0:N], start=False, stop=False)
                    if kt < 3:
                        last = nc.tensor.matmul(bank[:, 0:P], EYE[:], MK[:, P:2 * P], start=False, stop=True)
                    else:
                        last = nc.tensor.matmul(bank, EYE[:], MK[:, 0:2 * P], start=False, stop=True)
                last.then_inc(st_filled, 1)

            def pv(m, r, kt):
                i = 2 * m + r
                pe.wait_ge(exp_done, i * 4 + (3 if kt < 2 else 4))
                if kt == 0:
                    pe.wait_ge(v_in[r], (m + 1) * 16)
                    wait(pe, z_done, i)
                for h in R:
                    probs = PA[h][:, kt, 0:N - kt * P] if kt < 2 else \
                        PB[h][:, (kt - 2) * 256 + (kt - 2) * P:(kt - 1) * 256]
                    last = nc.tensor.matmul(pZ[h * DB:(h + 1) * DB, kt * P:N], V[r][:, kt, h * DB:(h + 1) * DB],
                                            probs, start=(kt == 0), stop=(kt == TT - 1), skip_group_check=True)
                last.then_inc(pv_done, 1)

            def denominators(m, r):
                i = 2 * m + r
                pe.wait_ge(exp_done, i * 4 + 4)
                for h in R:
                    pe.wait_ge(den_step, i * 6 + h * 3 + 3)
                    for t in range(TT):
                        sums = PA[h][:, 0, 0:P] if t == 0 else DS[h][:, (t - 1) * P:t * P]
                        last = nc.tensor.matmul(pB[32 * t:32 * t + 32, 0:P], GATHER[:, h, :], sums,
                                                start=(h == 0), stop=(h == 1), skip_group_check=True)
                last.then_inc(den_done, 1)

            def spread(m, r):
                i = 2 * m + r
                pe.wait_ge(recip_done, i + 1)
                wait(pe, x_added, i)
                for t in range(TT):
                    last = nc.tensor.matmul(pO[:, t * P:(t + 1) * P], SPREAD[:, t, :], RDC[:],
                                            start=True, stop=True)
                last.then_inc(den_spread, 1)

            def turn_max(m, r):
                i = 2 * m + r
                pe.wait_ge(sm_reduced, i * 6 + 6)
                wait(pe, max_lo, i)
                for qt in range(TT):
                    last = nc.tensor.transpose(pT[:, qt * P:(qt + 1) * P], NM[r][:, qt, :], IDENT[:])
                last.then_inc(nm_turned, 1)

            def body(m, r, first, last, ahead):
                n = next_of(m, r)

                def smax(h, part):
                    if not last:
                        smax_unit(*n, h, part)

                scores(m, r, 0, 0)
                if not first:
                    spread(*before(m, r))
                scores(m, r, 0, 1)
                smax(0, 0)
                smax(0, 1)
                scores(m, r, 1, 0)
                smax(0, 2)
                if not first:
                    out_product(*before(m, r))
                smax(1, 0)
                scores(m, r, 1, 1)
                smax(1, 1)
                pv(m, r, 0)
                smax(1, 2)
                if ahead:
                    project(m + 1, r, 0)
                if not last:
                    turn_max(*n)
                pv(m, r, 1)
                if ahead:
                    project(m + 1, r, 1)
                pv(m, r, 2)
                pv(m, r, 3)
                denominators(m, r)

            pe.wait_ge(const_in, 48)
            pe.wait_ge(masks_set, 12)
            pe.wait_ge(stacks_set, 2)
            project(0, 0, 0)
            project(0, 0, 1)
            for h in R:
                for part in range(3):
                    smax_unit(0, 0, h, part)
            turn_max(0, 0)
            project(0, 1, 0)
            project(0, 1, 1)
            over_slots(pe, body)
            spread(B * HALF - 1, 1)
            out_product(B * HALF - 1, 1)

        @block.scalar
        def _(act):
            def high(m, r, qk):
                i = 2 * m + r
                dst, bias = ((Q1, BQ), (K1, BK))[qk]
                act.wait_ge((q_mm, k_mm)[qk], i + 1)
                wait(act, st_filled, 4 * (i - 1))
                for h in R:
                    for half in range(1 + qk):
                        nc.scalar.activation(dst[r][half * DB:(half + 1) * DB, h, :],
                                             pM[h * DB:(h + 1) * DB, qk, :], ACT.Identity,
                                             bias=bias[:, bias_col(m, r, h)]).then_inc(hi_done, 1)

            def max_high(m, r):
                i = 2 * m + r
                act.wait_ge(nm_turned, i + 1)
                wait(act, st_filled, 4 * (i - 1))
                nc.scalar.activation(Q2[r][MH:MH + 2], both_heads(), ACT.Copy).then_inc(max_hi, 1)

            def copy_recip(m, r):
                i = 2 * m + r
                act.wait_ge(den_spread, i + 1)
                wait(act, z_done, i)
                nc.scalar.activation(RD[:], pO[:], ACT.Copy).then_inc(rd_copied, 1)

            def bias_col(m, r, h):
                return span(pair(m, r) * 2 + h, 1)

            def exp_unit(m, r, h, part):
                i = 2 * m + r
                act.wait_ge(st_filled, i * 4 + h * 2 + part + 1)
                if part == 0:
                    wait(act, pv_done, 4 * i)
                    wait(act, den_done, i)
                    nc.scalar.activation(PA[h][:].rearrange("p a n -> p (a n)")[:, 0:2 * N - P], pA[:, 0:2 * N - P],
                                         ACT.Exp, scale=SCALE_B).then_inc(exp_done, 1)
                else:
                    nc.scalar.activation(PB[h][:], pB[:], ACT.Exp, scale=SCALE_B).then_inc(exp_done, 1)

            def body(m, r, first, last, ahead):
                exp_unit(m, r, 0, 0)
                if not first:
                    copy_recip(*before(m, r))
                exp_unit(m, r, 0, 1)
                exp_unit(m, r, 1, 0)
                exp_unit(m, r, 1, 1)
                if ahead:
                    high(m + 1, r, 0)
                if not last:
                    max_high(*next_of(m, r))
                if ahead:
                    high(m + 1, r, 1)

            act.wait_ge(const_in, 48)
            high(0, 0, 0)
            high(0, 0, 1)
            max_high(0, 0)
            high(0, 1, 0)
            high(0, 1, 1)
            over_slots(act, body)
            copy_recip(B * HALF - 1, 1)

        @block.vector
        def _(dve):
            def low(m, r, qk):
                i = 2 * m + r
                for h in R:
                    dve.wait_ge(hi_done, i * 6 + (h + 1 if qk == 0 else 2 * h + 4))
                    src, hi, bias = ((pM[:, 0, :], Q1, BQ), (pM[:, 1, :], K1, BK))[qk]
                    dst = Q1[r][DB:2 * DB, h, :] if qk == 0 else K2[r][0:DB, h, :]
                    nc.vector.scalar_tensor_tensor(dst, src[h * DB:(h + 1) * DB, :],
                                                   bias[:, span(pair(m, r) * 2 + h, 1)],
                                                   hi[r][0:DB, h, :].bitcast(F32), ALU.add, ALU.subtract)\
                        .then_inc(lo_done, 1)

            def reduce_unit(m, r, h, part):
                i = 2 * m + r
                dve.wait_ge(sm_filled, i * 6 + h * 3 + part + 1)
                if h == 0 and part == 0:
                    wait(dve, nm_turned, i - 1)
                bank = pM[:, (h * 3 + part) % 2, :]
                if part == 0:
                    nc.vector.tensor_reduce(NM[r][:, 0:2, h], bank.rearrange("p (t k) -> p t k", t=2), AX.X,
                                            ALU.max, negate=True).then_inc(sm_reduced, 1)
                else:
                    nc.vector.tensor_reduce(NM[r][:, part + 1, h:h + 1], bank[:, 0:(part + 2) * P], AX.X,
                                            ALU.max, negate=True).then_inc(sm_reduced, 1)

            def max_low(m, r):
                i = 2 * m + r
                dve.wait_ge(max_hi, i + 1)
                nc.vector.tensor_tensor(Q2[r][ML:ML + 2], both_heads(), Q2[r][MH:MH + 2].bitcast(F32),
                                        ALU.subtract).then_inc(max_lo, 1)

            def recip_den(m, r):
                i = 2 * m + r
                dve.wait_ge(den_done, i + 1)
                wait(dve, den_spread, i)
                nc.vector.reciprocal(RDC[:], pB[:, 0:P]).then_inc(recip_done, 1)

            def normalize_z(m, r):
                i = 2 * m + r
                dve.wait_ge(rd_copied, i + 1)
                dve.wait_ge(pv_done, 4 * i + 4)
                wait(dve, wo_done, i - 1)
                nc.vector.tensor_tensor(Z[r][:], pZ[:], RD[:], ALU.mult).then_inc(z_done, 1)

            def add_out(m, r):
                i = 2 * m + r
                dve.wait_ge(wo_done, i + 1)
                xb = X[:, span(batch(m) * TT, TT), :]
                nc.vector.tensor_tensor(xb, pO[:].rearrange("p (t n) -> p t n", t=TT), xb, ALU.add)\
                    .then_inc(x_added, 1)

            def body(m, r, first, last, ahead):
                n = next_of(m, r)
                if not last:
                    low(*n, 0)
                    low(*n, 1)
                if not first:
                    normalize_z(*before(m, r))
                for h in R:
                    for part in range(3):
                        if not last:
                            reduce_unit(*n, h, part)
                        if (h, part) == (1, 0) and not first:
                            add_out(*before(m, r))
                if not last:
                    max_low(*n)
                recip_den(m, r)

            for r in R:
                nc.vector.memset(Q2[r][:].bitcast(F32), 0.0)
                last_set = nc.vector.memset(K2[r][:].bitcast(F32), 0.0)
            last_set.then_inc(stacks_set, 1)
            dve.wait_ge(stacks_set, 1)
            for r in R:
                for h in R:
                    for row in (MH, ML):
                        last_set = nc.vector.tensor_copy(K2[r][row:row + 2, h, :],
                                                         IDENT[row:row + 2, row + h:row + h + 1].to_broadcast([2, N]))
            last_set.then_inc(stacks_set, 1)
            dve.wait_ge(const_in, 48)
            low(0, 0, 0)
            low(0, 0, 1)
            for h in R:
                for part in range(3):
                    reduce_unit(0, 0, h, part)
            max_low(0, 0)
            over_slots(dve, body)
            normalize_z(B * HALF - 1, 1)
            add_out(B * HALF - 1, 1)


def program(nc, d, out):
    q_d = nc.dram_tensor("q_stacks", (B, HA, 4 * DA, N), F32).ap()
    k_d = nc.dram_tensor("k_stacks", (B, HA, 4 * DA, N), F32).ap()
    va_d = nc.dram_tensor("v_first", (B, P, NG, TT, GH, 32), F32).ap()
    vb_d = nc.dram_tensor("v_second", (B, NP, P, TT, P), F32).ap()
    o_d = nc.dram_tensor("o_first", (HA, B, 32, P), F32).ap()
    with nc.sbuf_tensor("x", [P, B * TT, P], F32) as X, nc.sbuf_tensor("ident", [P, P], F32) as IDENT:
        phase_a_inputs(nc, X, IDENT, d, (q_d, k_d, va_d))
        phase_a_attention(nc, IDENT, d, (q_d, k_d, va_d), o_d)
        with nc.sbuf_tensor("xt_all_hi", [P, B * N], F32R) as XTH, nc.sbuf_tensor("xt_all_lo", [P, B * N], F32R) as XTL:
            phase_ffn(nc, X, IDENT, d, "f1", attn=o_d, tail=(XTH, XTL, vb_d))
            phase_b_attention(nc, X, IDENT, d, XTH, XTL, vb_d)
        phase_ffn(nc, X, IDENT, d, "f2", out=out)


def lay_out(i):
    wq, wk, wv = np.split(i["L0_attn_a_qkv_w"], 3, axis=0)
    bq, bk, bv = np.split(i["L0_attn_a_qkv_b"], 3)
    half = np.arange(D).reshape(HA, DA)
    half = np.roll(half, DA // 2, axis=1).reshape(D)
    inv = (1.0 / 10000.0 ** (np.arange(0, DA, 2, dtype=np.float32) / DA)).astype(np.float32)
    ang = np.arange(N, dtype=np.float32)[:, None] * inv[None, :]
    cos = np.concatenate([np.cos(ang), np.cos(ang)], 1).T
    sin = np.concatenate([-np.sin(ang), np.sin(ang)], 1).T
    rot = np.stack([np.tile(cos, (HA, 1)), np.tile(sin, (HA, 1))], 1).astype(np.float32)
    sel = np.zeros((P, 36), np.float32)
    for h in range(GH):
        sel[32 * h:32 * h + DA, h * DA:(h + 1) * DA] = np.eye(DA)
        sel[32 * h + DA, 32 + h] = 1.0
    c = np.ascontiguousarray
    return {
        "x": c(i["L0_attn_a_x"]),
        "wa": c(np.stack([wq.T, wq[half].T, wk.T, wk[half].T, wv.T], 1)),
        "bqk": c(np.stack([bq, bq[half], bk, bk[half]], 1)),
        "bv": c(bv),
        "rot": c(rot),
        "sel": sel,
        "ident": np.eye(P, dtype=np.float32),
        "wp": c(i["L0_attn_a_proj_w"].T),
        "bp": c(i["L0_attn_a_proj_b"]),
        "fc1_q": c(i["L0_ffn_fc1_q"]),
        "fc1_s": c(i["L0_ffn_fc1_scales"].reshape(FF)),
        "fc2_q": c(i["L0_ffn_fc2_q"]),
        "fc2_s": c(i["L0_ffn_fc2_scales"]),
        "gb": c(np.stack([i["L0_ffn_ln_gamma"], i["L0_ffn_ln_beta"]], 1)),
        "b1": c(i["L0_ffn_fc1_bias"].reshape(FT, P).T),
        "b2": c(i["L0_ffn_fc2_bias"]),
        "wqk2": c(np.stack([i["L0_attn_b_Wq"].transpose(1, 0, 2).reshape(D, NP, P),
                            i["L0_attn_b_Wk"].transpose(1, 0, 2).reshape(D, NP, P)], 2)),
        "wv2": c(i["L0_attn_b_Wv"].transpose(1, 0, 2).reshape(D, HB * DB)),
        "wo": c(i["L0_attn_b_Wo"].reshape(HB * DB, D)),
        "bq2": c(i["L0_attn_b_bq"].T),
        "bk2": c(i["L0_attn_b_bk"].T),
        "bv2": c(i["L0_attn_b_bv"].reshape(NP, P).T),
        "bo": c(i["L0_attn_b_bo"]),
    }


def kernel(**inputs):
    import concourse.bacc as bacc
    from concourse.bass_utils import run_bass_kernel_spmd

    nc = bacc.Bacc("TRN2", target_bir_lowering=False, num_devices=1)
    arrays = lay_out({name: np.asarray(a) for name, a in inputs.items()})
    d = {name: nc.dram_tensor(f"in_{name}", a.shape, mybir.dt.from_np(a.dtype), kind="ExternalInput").ap()
         for name, a in arrays.items()}
    out = nc.dram_tensor("out", (B, N, D), F32, kind="ExternalOutput").ap()
    program(nc, d, out)
    r = run_bass_kernel_spmd(nc, [{f"in_{name}": a for name, a in arrays.items()}], core_ids=[0])
    return r.results[0]["out"]
```

```python
from contextlib import ExitStack

import numpy as np

import concourse.bass as bass
from concourse import mybir

F32 = mybir.dt.float32
F32R = mybir.dt.float32r
BF16 = mybir.dt.bfloat16
I32 = mybir.dt.int32
ALU = mybir.AluOpType
ACT = mybir.ActivationFunctionType
AX = mybir.AxisListType

P = 128
D = 128
B, N = 8, 512
TT = N // P
BANK = 512
EPS = 1e-5
HA, DA = 16, 8
GH = 4
AR = 128
NG = HA // GH
HB, DB = 16, 64
NP = HB // 2
FF = 512
FT = FF // P
SCALE_A = float(DA) ** -0.5
SCALE_B = float(DB) ** -0.5
MASKED = -1e30


def fits(v):
    return not isinstance(v, int) or v > 0


def wait(eng, sem, v):
    if fits(v):
        eng.wait_ge(sem, v)


def waits(eng, met, *pairs):
    if all(isinstance(n, int) for _, n in pairs):
        for sem, n in pairs:
            wait(eng, sem, n)
        return
    for _, n in pairs:
        if not isinstance(n, int):
            eng.compute_val(n)
    eng.wait_ge(*met)
    for sem, n in pairs:
        wait(eng, sem, n)


def mean_and_variance(nc, dve, stats_done, n, x_of_tile, stats, mv, consts):
    for t in range(TT):
        last = nc.vector.bn_stats(stats[:, t, :], x_of_tile(t))
    last.then_inc(stats_done, 1)
    waits(dve, consts, (stats_done, n + 1))
    for t in range(TT):
        last = nc.vector.bn_aggr(mv[:, t, :], stats[:, t, :])
    return last


def inverse_root(nc, pool, step, n, mv, ve, minus_half, out):
    nc.gpsimd.tensor_scalar(ve[:], mv[:, :, 1], EPS, None, ALU.add).then_inc(step, 1)
    pool.wait_ge(step, n + 2)
    return nc.gpsimd.tensor_tensor(out[:], ve[:], minus_half[:], ALU.pow)


def normalize(nc, x_of_tile, out, mv, rstd):
    for t in range(TT):
        last = nc.vector.tensor_scalar(out[:, t, :], x_of_tile(t), mv[:, t, 0:1], rstd[:, t:t + 1],
                                       ALU.subtract, ALU.mult)
    return last


class SharedWeights:

    def __init__(self, nc, ctx, d):
        sb = lambda n, s, t: ctx.enter_context(nc.sbuf_tensor(f"w_{n}", s, t))
        sem = lambda n: ctx.enter_context(nc.semaphore(f"w_{n}"))
        self.nc, self.d = nc, d
        self.W1H = sb("fc1_hi", [P, FF], F32R)
        self.W1L = sb("fc1_lo", [P, FF], F32R)
        self.W2 = sb("fc2", [P, FT, P], F32)
        self.GB = sb("gamma_beta", [P, 2], F32)
        self.B1 = sb("fc1_bias", [P, FT], F32)
        self.B2 = sb("fc2_bias", [P, P], F32)
        self.WVH = sb("v_hi", [P, HB * DB], F32R)
        self.WVL = sb("v_lo", [P, HB * DB], F32R)
        self.WO = sb("o", [P, NP, P], F32)
        self.BOV = sb("o_b_total", [P, P], F32)
        self.WP = sb("proj", [P, P], F32)
        self.PB = sb("proj_b", [P, P], F32)
        self.BQ = sb("bq", [DB, HB], F32)
        self.BK = sb("bk", [DB, HB], F32)
        self.loaded = sem("loaded")
        self.ready = sem("ready")
        self.bias_wide = sem("bias_wide")
        self.bias_sum = sem("bias_sum")
        self.LOADS = 15

    def allocate_raw(self, ctx):
        sb = lambda n, s, t: ctx.enter_context(self.nc.sbuf_tensor(f"w_{n}", s, t))
        self.Q1 = sb("fc1_q", [P, FF], I32)
        self.S1 = sb("fc1_scale", [P, FF], F32)
        self.W1 = sb("fc1", [P, FF], F32)
        self.Q2 = sb("fc2_q", [P, FT, P], I32)
        self.S2 = sb("fc2_scale", [P, FT, P], F32)
        self.WV = sb("v", [P, HB * DB], F32)
        self.BV = sb("v_b", [P, NP], F32)
        self.BO = sb("o_b", [P, P], F32)
        self.BVB = sb("v_b_wide", [P, NP, P], F32)

    def load(self, queue):
        d = self.d
        for dst, src in ((self.Q1, d["fc1_q"]), (self.S1, d["fc1_s"].partition_broadcast(P)),
                         (self.Q2, d["fc2_q"].rearrange("(f p) n -> p f n", p=P)),
                         (self.S2, d["fc2_s"].partition_broadcast(P)), (self.GB, d["gb"]),
                         (self.B1, d["b1"]), (self.B2, d["b2"].partition_broadcast(P)),
                         (self.WP, d["wp"]), (self.PB, d["bp"].partition_broadcast(P)),
                         (self.WV, d["wv2"]), (self.WO, d["wo"].rearrange("(p r) n -> r p n", r=P)),
                         (self.BV, d["bv2"]), (self.BO, d["bo"].partition_broadcast(P)),
                         (self.BQ, d["bq2"]), (self.BK, d["bk2"])):
            queue.dma_start(dst[:], src).then_inc(self.loaded, 16)

    def prepare(self, dve):
        nc = self.nc
        dve.wait_ge(self.loaded, 16 * self.LOADS)
        for j in range(NP):
            last = nc.vector.tensor_copy(self.BVB[:, j, :], self.BV[:, j:j + 1].broadcast_to([P, P]))
        last.then_inc(self.bias_wide, 1)
        nc.vector.scalar_tensor_tensor(self.W1[:], self.Q1[:], -128.0, self.S1[:], ALU.add, ALU.mult)\
            .then_inc(self.ready, 1)
        nc.vector.scalar_tensor_tensor(self.W2[:], self.Q2[:], -128.0, self.S2[:], ALU.add, ALU.mult)
        nc.vector.tensor_scalar(self.B2[:], self.B2[:], 0.5, None, ALU.mult)
        nc.vector.tensor_copy(self.WVH[:], self.WV[:]).then_inc(self.ready, 1)
        dve.wait_ge(self.ready, 2)
        nc.vector.tensor_copy(self.W1H[:], self.W1[:]).then_inc(self.ready, 1)
        nc.vector.tensor_tensor(self.WVL[:], self.WV[:], self.WVH[:].bitcast(F32), ALU.subtract)
        dve.wait_ge(self.ready, 3)
        nc.vector.tensor_tensor(self.W1L[:], self.W1[:], self.W1H[:].bitcast(F32), ALU.subtract)

    def sum_bias(self, pe, bank):
        pe.wait_ge(self.bias_wide, 1)
        for j in range(NP):
            last = self.nc.tensor.matmul(bank, self.BVB[:, j, :], self.WO[:, j, :], start=(j == 0), stop=(j == NP - 1))
        last.then_inc(self.bias_sum, 1)

    def total_bias(self, dve, bank):
        dve.wait_ge(self.bias_sum, 1)
        self.nc.vector.tensor_tensor(self.BOV[:], bank, self.BO[:], ALU.add).then_inc(self.ready, 1)


def phase_a_inputs(nc, X, IDENT, d, scratch, stacks, weights):
    q_d, k_d, v_d = scratch
    with ExitStack() as ctx:
        sb = lambda n, s, t: ctx.enter_context(nc.sbuf_tensor(n, s, t))
        ps = lambda n, s, t: ctx.enter_context(nc.psum_tensor(n, s, t))
        sem = lambda n: ctx.enter_context(nc.semaphore(n))
        W = sb("wa_raw", [P, 5, P], F32)
        WH = sb("wa_hi", [P, 4, P], F32R)
        WL = sb("wa_lo", [P, 4, P], F32R)
        BQK = sb("qk_bias", [P, 4], F32)
        BV = sb("v_bias", [P, P], F32)
        ROT = sb("rotary", [P, 2, N], F32)
        stats = sb("ln_stats", [P, TT, 6], F32)
        mv = sb("ln_mv", [P, TT, 2], F32)
        ve = sb("ln_var_eps", [P, TT], F32)
        minus_half = sb("minus_half", [P, TT], F32)
        rstd = sb("ln_rstd", [P, TT], F32)
        XN = sb("xn", [P, TT, P], F32)
        XT = sb("xt", [P, N], F32)
        XTH = sb("xt_hi", [P, N], F32R)
        XTL = sb("xt_lo", [P, N], F32R)
        T1 = sb("rot_cos", [P, 2, N], F32)
        T2 = sb("rot_sin", [P, 2, N], F32)
        QK = sb("qk_full", [P, 2, N], F32)
        QKH = sb("qk_hi", [P, 2, N], F32R)
        QKL = sb("qk_lo", [P, 2, N], F32R)
        V = sb("v_rows", [P, NG, TT, GH, 32], F32)
        FILL = sb("fill", [AR, 2, N], F32)
        pT = ps("p_xt", [P, N], F32)
        pQ = ps("p_qk", [P, 4, N], F32)
        pV = ps("p_v", [P, TT, P], F32)

        fill_set = sem("a0_fill")
        zeros_set = sem("a0_zeros")
        w_in = sem("a0_w_in")
        x_in = sem("a0_x_in")
        w_split = sem("a0_w_split")
        v_ready0 = sem("a0_v_const")
        ln_stats = sem("a0_ln_stats")
        ln_mv = sem("a0_ln_mv")
        ln_rstd = sem("a0_ln_rstd")
        root_step = sem("a0_root_step")
        xn_ready = sem("a0_xn")
        xt_ready = sem("a0_xt_psum")
        xt_copied = sem("a0_xt_copied")
        xt_split = sem("a0_xt_split")
        v_done = sem("a0_v_psum")
        qk_done = sem("a0_qk_psum")
        rot_done = sem("a0_rot")
        qk_sum = sem("a0_qk_sum")
        qk_hi = sem("a0_qk_hi")
        qk_lo = sem("a0_qk_lo")
        v_out = sem("a0_v_sbuf")
        stored_h = sem("a0_hi_stored")
        stored_l = sem("a0_lo_stored")
        stored_v = sem("a0_v_stored")

        block = ctx.enter_context(nc.Block())

        def each_batch(eng, batch):
            batch(0)
            with eng.Fori(1, B) as c:
                batch(c)

        @block.sync
        def _(sp):
            sp.dma_start(W[:], d["wa"]).then_inc(w_in, 16)
            for c in range(B):
                sp.dma_start(X[:, c * TT:(c + 1) * TT, :],
                             d["x"][c].rearrange("(t p) d -> p t d", p=P)).then_inc(x_in, 16)
                sp.wait_ge(x_in, 16 * (c + 1))
            def batch(c):
                sp.wait_ge(v_out, c + 1)
                sp.dma_start(v_d[c], V[:]).then_inc(stored_v, 16)
                for qk, dst in ((0, q_d), (1, k_d)):
                    sp.wait_ge(qk_hi, c * 2 + qk + 1)
                    for j in ((0, 3), (0, 2))[qk]:
                        sp.dma_start(dst[c, :, j * DA:(j + 1) * DA, :], QKH[:, qk, :].bitcast(F32))\
                            .then_inc(stored_h, 16)
                    sp.wait_ge(qk_lo, c * 2 + qk + 1)
                    for j in ((1, 2), (1, 3))[qk]:
                        sp.dma_start(dst[c, :, j * DA:(j + 1) * DA, :], QKL[:, qk, :].bitcast(F32))\
                            .then_inc(stored_l, 16)

            each_batch(sp, batch)
            sp.wait_ge(stored_h, 64 * B)
            sp.wait_ge(stored_l, 64 * B)
            sp.wait_ge(stored_v, 16 * B)

        @block.scalar
        def _(act):
            act.dma_start(BQK[:], d["bqk"]).then_inc(w_in, 16)
            act.dma_start(BV[:], d["bv"].partition_broadcast(P)).then_inc(w_in, 16)
            act.dma_start(ROT[:], d["rot"]).then_inc(w_in, 16)
            act.dma_start(IDENT[:], d["ident"]).then_inc(w_in, 16)

            def turned(c):
                act.wait_ge(xt_ready, c + 1)
                wait(act, v_done, c)
                wait(act, qk_done, c * 4)
                nc.scalar.activation(XT[:], pT[:], ACT.Copy).then_inc(xt_copied, 1)
                nc.scalar.activation(XTH[:], pT[:], ACT.Copy).then_inc(xt_copied, 1)

            def high(c):
                for qk in range(2):
                    act.wait_ge(qk_sum, c * 2 + qk + 1)
                    wait(act, stored_h, c * 64)
                    nc.scalar.activation(QKH[:, qk, :], QK[:, qk, :], ACT.Copy).then_inc(qk_hi, 1)

            def fill(stack, rows, value):
                src = FILL[rows, value:value + 1, :].to_broadcast([rows.stop - rows.start, GH, N])
                return nc.scalar.activation(stack[rows], src, ACT.Copy)

            turned(0)
            act.wait_ge(fill_set, 2)
            for stack in stacks:
                fill(stack, slice(0, AR), 0).then_inc(zeros_set, 1)
            act.wait_ge(zeros_set, 2 * NG)
            for stack in stacks[NG:]:
                fill(stack, slice(32, 34), 1)
            turned(1)
            high(0)
            weights.load(act)
            with act.Fori(1, B - 1) as c:
                turned(c + 1)
                high(c)
            high(B - 1)

        @block.gpsimd
        def _(pool):
            nc.gpsimd.memset(FILL[:, 0], 0.0).then_inc(fill_set, 1)
            nc.gpsimd.memset(FILL[:, 1], 1.0).then_inc(fill_set, 1)
            nc.gpsimd.memset(V[:], 0.0).then_inc(v_ready0, 1)
            pool.wait_ge(v_ready0, 1)
            nc.gpsimd.memset(V[:, :, :, :, DA:DA + 1], 1.0).then_inc(v_ready0, 1)

            def root(c):
                waits(pool, (root_step, 1), (ln_mv, c + 1))
                inverse_root(nc, pool, root_step, c, mv, ve, minus_half, rstd).then_inc(ln_rstd, 1)

            def rest(c, ahead):
                if ahead:
                    root(c + 1)
                for qk in range(2):
                    pool.wait_ge(rot_done, c * 2 + qk + 1)
                    wait(pool, qk_hi, c * 2)
                    wait(pool, qk_lo, c * 2)
                    nc.gpsimd.tensor_tensor(QK[:, qk, :], T1[:, qk, :], T2[:, qk, :], ALU.add)\
                        .then_inc(qk_sum, 1)
                for qk in range(2):
                    pool.wait_ge(qk_hi, c * 2 + qk + 1)
                    wait(pool, stored_l, c * 64)
                    nc.gpsimd.tensor_tensor(QKL[:, qk, :], QK[:, qk, :], QKH[:, qk, :].bitcast(F32),
                                            ALU.subtract).then_inc(qk_lo, 1)

            nc.gpsimd.memset(minus_half[:], -0.5).then_inc(root_step, 1)
            root(0)
            rest(0, True)
            with pool.Fori(1, B - 1) as c:
                rest(c, True)
            rest(B - 1, False)

        @block.tensor
        def _(pe):
            pe.wait_ge(w_in, 80)
            pe.wait_ge(w_split, 2)
            def batch(c):
                pe.wait_ge(xn_ready, c + 1)
                wait(pe, xt_split, c)
                for t in range(TT):
                    last = nc.tensor.transpose(pT[:, t * P:(t + 1) * P], XN[:, t, :], IDENT[:])
                last.then_inc(xt_ready, 1)
                pe.wait_ge(xt_copied, c * 2 + 1)
                wait(pe, v_out, c)
                for t in range(TT):
                    last = nc.tensor.matmul(pV[:, t, :], XT[:, t * P:(t + 1) * P], W[:, 4, :],
                                            start=True, stop=True)
                last.then_inc(v_done, 1)
                pe.wait_ge(xt_copied, c * 2 + 2)
                pe.wait_ge(xt_split, c + 1)
                for j in range(4):
                    wait(pe, rot_done, (c * 2 if j < 2 else c * 2))
                    nc.tensor.matmul(pQ[:, j, :], WH[:, j, :], XTH[:], start=True, stop=False)
                    nc.tensor.matmul(pQ[:, j, :], WL[:, j, :], XTH[:], start=False, stop=False)
                    nc.tensor.matmul(pQ[:, j, :], WH[:, j, :], XTL[:], start=False, stop=True)\
                        .then_inc(qk_done, 1)

            each_batch(pe, batch)
            pe.wait_ge(v_out, B)
            weights.sum_bias(pe, pV[:, 0, :])

        @block.vector
        def _(dve):
            def tile_of(c):
                return lambda t: X[:, c * TT + t, :]

            def statistics(c):
                waits(dve, (w_in, 80), (x_in, (c + 1) * 16))
                mean_and_variance(nc, dve, ln_stats, c, tile_of(c), stats, mv, (w_in, 80)).then_inc(ln_mv, 1)

            def norm(c):
                dve.wait_ge(ln_rstd, c + 1)
                wait(dve, xt_ready, c)
                normalize(nc, tile_of(c), XN, mv, rstd).then_inc(xn_ready, 1)

            def stage_rest(c, ahead):
                dve.wait_ge(xt_copied, c * 2 + 2)
                wait(dve, qk_done, c * 4)
                nc.vector.tensor_tensor(XTL[:], pT[:], XTH[:].bitcast(F32), ALU.subtract)\
                    .then_inc(xt_split, 1)
                if ahead:
                    statistics(c + 1)
                dve.wait_ge(v_done, c + 1)
                wait(dve, stored_v, c * 16)
                for g in range(NG):
                    src = pV[:, :, g * 32:(g + 1) * 32].rearrange("p t (h d) -> p t h d", h=GH)
                    bias = BV[:, g * 32:(g + 1) * 32].rearrange("p (h d) -> p h d", h=GH)
                    for t in range(TT):
                        last = nc.vector.tensor_tensor(V[:, g, t, :, 0:DA], src[:, t], bias, ALU.add)
                last.then_inc(v_out, 1)
                for qk in range(2):
                    if qk == 1 and ahead:
                        norm(c + 1)
                    dve.wait_ge(qk_done, c * 4 + qk * 2 + 1)
                    wait(dve, qk_sum, c * 2)
                    nc.vector.scalar_tensor_tensor(T1[:, qk, :], pQ[:, 2 * qk, :], BQK[:, 2 * qk:2 * qk + 1],
                                                   ROT[:, 0, :], ALU.add, ALU.mult)
                    dve.wait_ge(qk_done, c * 4 + qk * 2 + 2)
                    nc.vector.scalar_tensor_tensor(T2[:, qk, :], pQ[:, 2 * qk + 1, :],
                                                   BQK[:, 2 * qk + 1:2 * qk + 2],
                                                   ROT[:, 1, :], ALU.add, ALU.mult).then_inc(rot_done, 1)

            dve.wait_ge(w_in, 80)
            nc.vector.tensor_copy(WH[:], W[:, 0:4, :]).then_inc(w_split, 1)
            dve.wait_ge(w_split, 1)
            nc.vector.tensor_tensor(WL[:], W[:, 0:4, :], WH[:].bitcast(F32), ALU.subtract).then_inc(w_split, 1)
            dve.wait_ge(v_ready0, 2)
            statistics(0)
            norm(0)
            stage_rest(0, True)
            with dve.Fori(1, B - 1) as c:
                stage_rest(c, True)
            stage_rest(B - 1, False)
            weights.prepare(dve)
            weights.total_bias(dve, pV[:, 0, :])


def phase_a_attention(nc, IDENT, d, scratch, stacks, weights, o_d):
    q_d, k_d, v_d = scratch
    with ExitStack() as ctx:
        sb = lambda n, s, t: ctx.enter_context(nc.sbuf_tensor(n, s, t))
        ps = lambda n, s, t: ctx.enter_context(nc.psum_tensor(n, s, t))
        sem = lambda n: ctx.enter_context(nc.semaphore(n))
        Q, K = stacks[:NG], stacks[NG:]
        V = [sb(f"v_stack{g}", [P, TT, GH, 32], F32) for g in range(NG)]
        PR = [sb(f"probs{kt}", [P, GH, N], F32) for kt in range(TT)]
        NM = [sb(f"neg_max{r}", [P, TT, GH], F32) for r in range(2)]
        NMF = sb("neg_max_rows", [GH, N], F32)
        ZERO = sb("zero", [GH, N], F32)
        NMH = sb("neg_max_hi", [GH, N], F32R)
        NML = sb("neg_max_lo", [GH, N], F32R)
        OT = sb("o_t", [P, N], F32)
        SEL = sb("select_rows", [P, 36], F32)
        RD = sb("recip_den", [P, 4, GH], F32)
        OX = [sb(f"o_rows{r}", [32, GH, 16, DA], F32) for r in range(2)]
        pM = [ps(f"p_max{u}", [P, N], F32) for u in range(3)]
        pS = [ps(f"p_scores{u}", [P, N], F32) for u in range(3)]
        pO = ps("p_out", [P, N], F32)
        pX = ps("p_misc", [P, N], F32)

        loaded = [sem(f"a_loaded{g}") for g in range(NG)]
        rows_in = [sem(f"a_rows{g}") for g in range(NG)]
        sm_filled = sem("a_sm_filled")
        sm_reduced = sem("a_sm_reduced")
        nm_turned = sem("a_nm_turned")
        nm_copied = sem("a_nm_copied")
        nm_split = sem("a_nm_split")
        st_filled = sem("a_st_filled")
        exp_done = sem("a_exp")
        pv_done = sem("a_pv")
        ot_copied = sem("a_ot_copied")
        o_turned = sem("a_o_turned")
        o_recip = sem("a_o_recip")
        o_done = sem("a_o_done")
        sel_in = sem("a_sel_in")
        zero_set = sem("a_zero_set")
        o_stored = [sem(f"a_o_stored{r}") for r in range(2)]

        block = ctx.enter_context(nc.Block())

        def batch_of(s_b, g, ahead):
            j = g + ahead
            return s_b + j // NG, j % NG

        def over_batches(eng, body):
            body(0, True, False)
            with eng.Fori(1, B - 1) as b:
                body(b, False, False)
            body(B - 1, False, True)

        def bank_of(g, unit):
            return (g * 16 + unit) % 3

        def bank_read(b, g, unit):
            n = (b * NG + g) * 16 + unit
            return n if g == 0 and unit == 0 else n - 2

        @block.sync
        def _(sp):
            def load(b, g):
                wait(sp, pv_done, (b * NG + g - NG) * TT + TT)
                sp.dma_start(Q[g][0:32].bitcast(F32), q_d[b, g * GH:(g + 1) * GH].rearrange("h r n -> r h n"))\
                    .then_inc(loaded[g], 16)
                sp.dma_start(K[g][0:32].bitcast(F32), k_d[b, g * GH:(g + 1) * GH].rearrange("h r n -> r h n"))\
                    .then_inc(loaded[g], 16)
                sp.dma_start(V[g][:], v_d[b, :, g]).then_inc(loaded[g], 16)

            def rows(b, g):
                n = b * NG + g
                sp.wait_ge(nm_split, n * 2 + 1)
                sp.dma_start(Q[g][32:33].bitcast(F32), NMH[:].bitcast(F32)).then_inc(rows_in[g], 16)
                sp.wait_ge(nm_split, n * 2 + 2)
                sp.dma_start(Q[g][33:34].bitcast(F32), NML[:].bitcast(F32)).then_inc(rows_in[g], 16)

            def store(b, g):
                sp.wait_ge(o_done, b * NG + g + 1)
                sp.dma_start(o_d[g * GH:(g + 1) * GH, b].rearrange("h r c -> r h c"),
                             OX[g % 2][:].rearrange("r h j d -> r h (j d)")).then_inc(o_stored[g % 2], 16)

            sp.dma_start(SEL[:], d["sel"]).then_inc(sel_in, 16)
            for g in range(NG):
                load(0, g)
                if g >= 2:
                    rows(0, g - 2)
            with sp.Fori(1, B) as b:
                for g in range(NG):
                    load(b, g)
                    rows(*batch_of(b, g, -2))
                    store(*batch_of(b, g, -4))
            for g in range(NG):
                if g < 2:
                    rows(B - 1, g + 2)
                store(B - 1, g)
            for r in range(2):
                sp.wait_ge(o_stored[r], B * NG // 2 * 16)

        @block.gpsimd
        def _(pool):
            def split(b, g):
                n = b * NG + g
                pool.wait_ge(nm_copied, n + 1)
                pb, pg = batch_of(b, g, -1)
                wait(pool, rows_in[pg], (pb + 1) * 32)
                nc.gpsimd.tensor_tensor(NMH[:], NMF[:], ZERO[:], ALU.add).then_inc(nm_split, 1)
                pool.wait_ge(nm_split, n * 2 + 1)
                nc.gpsimd.tensor_tensor(NML[:], NMF[:], NMH[:].bitcast(F32), ALU.subtract).then_inc(nm_split, 1)

            nc.gpsimd.memset(ZERO[:], 0.0).then_inc(zero_set, 1)
            pool.wait_ge(zero_set, 1)
            for g in range(NG):
                split(0, g)
            with pool.Fori(1, B) as b:
                for g in range(NG):
                    split(b, g)

        @block.tensor
        def _(pe):
            def smax_unit(b, g, h, qt):
                unit = h * TT + qt
                if unit == 0:
                    pe.wait_ge(loaded[g], (b + 1) * 48)
                wait(pe, sm_reduced, bank_read(b, g, unit))
                nc.tensor.matmul(pM[bank_of(g, unit)][:], Q[g][0:32, h, qt * P:(qt + 1) * P], K[g][0:32, h, :],
                                 start=True, stop=True).then_inc(sm_filled, 1)

            def st_unit(b, g, kt, h):
                unit = kt * GH + h
                if unit == 0:
                    pe.wait_ge(rows_in[g], (b + 1) * 32)
                wait(pe, exp_done, bank_read(b, g, unit))
                nc.tensor.matmul(pS[bank_of(g, unit)][:], K[g][:, h, kt * P:(kt + 1) * P], Q[g][:, h, :],
                                 start=True, stop=True).then_inc(st_filled, 1)

            def pv(b, g, kt):
                s = b * NG + g
                pe.wait_ge(exp_done, s * 16 + kt * GH + GH)
                if kt == 0:
                    wait(pe, ot_copied, s)
                for h in range(GH):
                    last = nc.tensor.matmul(pO[32 * h:32 * h + 32, :], V[g][:, kt, h, :], PR[kt][:, h, :],
                                            start=(kt == 0), stop=(kt == TT - 1), skip_group_check=True)
                last.then_inc(pv_done, 1)

            def turn_max(b, g):
                s = b * NG + g
                pe.wait_ge(sm_reduced, s * 16 + 16)
                wait(pe, o_done, s - 2)
                for qt in range(TT):
                    last = nc.tensor.transpose(pX[0:GH, qt * P:(qt + 1) * P], NM[g % 2][:, qt, :], IDENT[:])
                last.then_inc(nm_turned, 1)

            def turn_out(b, g, next_turned):
                s = b * NG + g
                pe.wait_ge(ot_copied, s + 1)
                if next_turned:
                    pe.wait_ge(nm_copied, s + 3)
                else:
                    pe.wait_ge(o_done, s)
                tokens = OT[:].rearrange("p (r j) -> p j r", j=16)
                for j in range(16):
                    m = 32 * (j % 4)
                    last = nc.tensor.matmul(pX[m:m + 32, (j // 4) * 36:(j // 4 + 1) * 36], tokens[:, j, :], SEL[:],
                                            start=True, stop=True)
                last.then_inc(o_turned, 1)

            def body(b, first, last):
                for g in range(NG):
                    b2, g2 = batch_of(b, g, 2)
                    b1, g1 = batch_of(b, g, 1)
                    b0, g0 = batch_of(b, g, -1)
                    ahead = not (last and g >= NG - 2)
                    for kt in range(TT):
                        for h in range(GH):
                            st_unit(b, g, kt, h)
                            if ahead:
                                smax_unit(b2, g2, kt, h)
                            if (kt, h) == (0, 1) and not (last and g == NG - 1):
                                turn_max(b1, g1)
                            if h == 2 and kt > 0:
                                pv(b, g, kt - 1)
                            elif h == 2 and not (first and g == 0):
                                pv(b0, g0, TT - 1)
                            if (kt, h) == (1, 3) and not (first and g == 0):
                                turn_out(b0, g0, not (last and g == NG - 1))

            pe.wait_ge(sel_in, 16)
            for h in range(GH):
                for qt in range(TT):
                    smax_unit(0, 0, h, qt)
            for h in range(GH):
                for qt in range(TT):
                    smax_unit(0, 1, h, qt)
                if h == 0:
                    turn_max(0, 0)
            over_batches(pe, body)
            pv(B - 1, NG - 1, TT - 1)
            turn_out(B - 1, NG - 1, False)

        @block.scalar
        def _(act):
            def exp_unit(b, g, kt, h):
                s = b * NG + g
                unit = kt * GH + h
                act.wait_ge(st_filled, s * 16 + unit + 1)
                if h == 0:
                    wait(act, pv_done, (s - 1) * TT + kt + 1)
                nc.scalar.activation(PR[kt][:, h, :], pS[bank_of(g, unit)][:], ACT.Exp, scale=SCALE_A)\
                    .then_inc(exp_done, 1)

            def copy_max(b, g):
                s = b * NG + g
                act.wait_ge(nm_turned, s + 1)
                wait(act, nm_split, s * 2)
                nc.scalar.activation(NMF[:], pX[0:GH, :], ACT.Copy).then_inc(nm_copied, 1)

            def copy_out(b, g):
                s = b * NG + g
                act.wait_ge(pv_done, s * TT + TT)
                wait(act, o_turned, s)
                nc.scalar.activation(OT[:], pO[:], ACT.Copy).then_inc(ot_copied, 1)

            def body(b, first, last):
                for g in range(NG):
                    for kt in range(TT):
                        for h in range(GH):
                            exp_unit(b, g, kt, h)
                            if (kt, h) == (0, 2) and not (last and g == NG - 1):
                                copy_max(*batch_of(b, g, 1))
                            if (kt, h) == (0, 3) and not (first and g == 0):
                                copy_out(*batch_of(b, g, -1))

            copy_max(0, 0)
            over_batches(act, body)
            copy_out(B - 1, NG - 1)

        @block.vector
        def _(dve):
            def reduce_unit(b, g, h, qt):
                s = b * NG + g
                dve.wait_ge(sm_filled, s * 16 + h * TT + qt + 1)
                if h == 0 and qt == 0:
                    wait(dve, nm_turned, s - 1)
                nc.vector.tensor_reduce(NM[g % 2][:, qt, h:h + 1], pM[bank_of(g, h * TT + qt)][:], AX.X, ALU.max,
                                        negate=True).then_inc(sm_reduced, 1)

            def finish(b, g):
                s = b * NG + g
                dve.wait_ge(o_turned, s + 1)
                o = pX[:, 0:4 * 36].rearrange("p (k c) -> p k c", k=4)
                nc.vector.reciprocal(RD[:], o[:, :, 32:36]).then_inc(o_recip, 1)
                dve.wait_ge(o_recip, s + 1)
                pb, pg = batch_of(b, g, -2)
                wait(dve, o_stored[g % 2], (pb * 2 + pg // 2 + 1) * 16)
                for m in range(4):
                    part = slice(32 * m, 32 * m + 32)
                    dst = OX[g % 2][:, :, m:16:4, :].rearrange("r h k d -> r k h d")
                    last = nc.vector.tensor_tensor(dst, o[part, :, 0:32].rearrange("p k (h d) -> p k h d", h=GH),
                                                   RD[part].unsqueeze(3).broadcast_to([32, 4, GH, DA]), ALU.mult)
                last.then_inc(o_done, 1)

            def body(b, first, last):
                for g in range(NG):
                    ahead = not (last and g >= NG - 2)
                    for h in range(GH):
                        if ahead:
                            for qt in range(TT):
                                reduce_unit(*batch_of(b, g, 2), h, qt)
                        if h == 1 and not (first and g == 0):
                            finish(*batch_of(b, g, -1))

            for g in range(2):
                for h in range(GH):
                    for qt in range(TT):
                        reduce_unit(0, g, h, qt)
            over_batches(dve, body)
            finish(B - 1, NG - 1)

def phase_ffn(nc, X, IDENT, weights, name, attn=None, tail=None, out=None):
    with ExitStack() as ctx:
        sb = lambda n, s, t: ctx.enter_context(nc.sbuf_tensor(f"{name}_{n}", s, t))
        ps = lambda n, s, t: ctx.enter_context(nc.psum_tensor(f"{name}_{n}", s, t))
        sem = lambda n: ctx.enter_context(nc.semaphore(f"{name}_{n}"))
        W1H, W1L, W2, GB, B1, B2 = (weights.W1H, weights.W1L, weights.W2, weights.GB, weights.B1, weights.B2)
        stats = sb("ln_stats", [P, TT, 6], F32)
        mv = sb("ln_mv", [P, TT, 2], F32)
        root = [sb(f"ln_root{k}", [P, TT], F32) for k in range(6)]
        minus_half = sb("minus_half", [P, TT], F32)
        XN = sb("xn", [P, TT, P], F32)
        H = sb("h", [P, TT, P], F32)
        XS = sb("xn_bias", [P, TT, P], F32)
        XR = sb("residual", [P, TT, P], F32)
        HT = sb("ht", [P, N], F32)
        HTH = sb("ht_hi", [P, N], F32R)
        HTL = sb("ht_lo", [P, N], F32R)
        Y = sb("silu", [P, FT, N], F32)
        pT = ps("p_t", [P, N], F32)
        pF = ps("p_f", [P, 2, N], F32)
        pZ = ps("p_z", [P, TT, P], F32)

        w_ready = (weights.ready, 4)
        pool_set = sem("pool_set")
        ln_stats = sem("ln_stats")
        ln_mv = sem("ln_mv")
        ln_root = sem("ln_root")
        ln_rstd = sem("ln_rstd")
        h_ready = sem("h")
        xn_ready = sem("xn")
        ht_turned = sem("ht_turned")
        ht_full = sem("ht_full")
        ht_hi = sem("ht_hi")
        ht_lo = sem("ht_lo")
        fc1_done = sem("fc1")
        silu_done = sem("silu")
        fc2_done = sem("fc2")
        xs_ready = sem("xn_plus_bias")
        xr_ready = sem("residual")
        x_new = sem("x_new")
        if attn is not None:
            o_d = attn
            WP, PB = weights.WP, weights.PB
            OT = sb("o_t", [P, N], F32)
            pP = ps("p_proj", [P, TT, P], F32)
            OC = sb("o_now", [P, TT, P], F32)
            oc_in = sem("oc_in")
            biased = sem("x_biased")
            ot_turned = sem("ot_turned")
            ot_copied = sem("ot_copied")
            proj_done = sem("proj")
            x_mid = sem("x_mid")
        if tail is not None:
            XTH_all, XTL_all, v_d = tail
            WVH, WVL, BOV = weights.WVH, weights.WVL, weights.BOV
            stats3 = sb("ln3_stats", [P, TT, 6], F32)
            mv3 = sb("ln3_mv", [P, TT, 2], F32)
            ve3 = sb("ln3_ve", [P, TT], F32)
            rstd3 = sb("ln3_rstd", [P, TT], F32)
            XN3 = sb("xn3", [P, TT, P], F32)
            XTH = sb("xt_hi", [P, N], F32R)
            XTL = sb("xt_lo", [P, N], F32R)
            V = sb("v", [P, TT, HB * DB], F32)
            pT3 = ps("p_t3", [P, N], F32)
            pV = ps("p_v", [P, 2, N], F32)
            ln3_stats = sem("ln3_stats")
            ln3_mv = sem("ln3_mv")
            ln3_root = sem("ln3_root")
            ln3_rstd = sem("ln3_rstd")
            xn3_ready = sem("xn3")
            x_out_biased = sem("x_out_biased")
            xt_turned = sem("xt_turned")
            xt_hi = sem("xt_hi")
            xt_lo = sem("xt_lo")
            v_mm = sem("v_mm")
            v_copied = sem("v_copied")
            xt_kept = sem("xt_kept")
            v_stored = sem("v_stored")
        stored = sem("stored")

        block = ctx.enter_context(nc.Block())

        def tiles(c):
            return bass.ds(c * TT, TT) if not isinstance(c, int) else slice(c * TT, c * TT + TT)

        def over_batches(eng, first, body, behind):
            first(0)
            body(0, True, False, True)
            body(1, True, True, True)
            with eng.Fori(2, B - 2) as c:
                body(c, True, True, True)
            body(B - 2, True, True, False)
            body(B - 1, False, True, False)
            behind(B - 1)

        @block.sync
        def _(sp):
            def keep(c):
                if tail is not None:
                    waits(sp, w_ready, (xt_hi, c + 1))
                    sp.dma_start(XTH_all[:, bass.ds(c * N, N)].bitcast(F32), XTH[:].bitcast(F32)).then_inc(xt_kept, 16)
                    waits(sp, w_ready, (xt_lo, c + 1))
                    sp.dma_start(XTL_all[:, bass.ds(c * N, N)].bitcast(F32), XTL[:].bitcast(F32)).then_inc(xt_kept, 16)
                    for t in range(TT):
                        sp.wait_ge(v_copied, c * 8 + t * 2 + 2)
                        sp.dma_start(v_d[c, :, :, t, :].rearrange("j p e -> p j e"),
                                     V[:, t, :].rearrange("p (j e) -> p j e", j=NP)).then_inc(v_stored, 16)

            def body(c, ahead, behind, far):
                if behind:
                    keep(c - 1)

            if tail is not None:
                over_batches(sp, lambda c: None, body, keep)
                sp.wait_ge(xt_kept, 32 * B)
                sp.wait_ge(v_stored, 16 * TT * B)
            if out is not None:
                with sp.Fori(0, B) as c:
                    sp.wait_ge(x_new, c + 1)
                    sp.dma_start(out[c].rearrange("(t p) d -> p t d", p=P), X[:, tiles(c), :]).then_inc(stored, 16)
                sp.wait_ge(stored, 16 * B)

        @block.gpsimd
        def _(pool):
            def bias_x(c):
                nc.gpsimd.tensor_tensor(X[:, tiles(c), :], X[:, tiles(c), :],
                                        PB[:].unsqueeze(1).broadcast_to([P, TT, P]), ALU.add).then_inc(biased, 1)

            def roots(c):
                def step(k, ins):
                    ins.then_inc(ln_root, 1)
                    waits(pool, (pool_set, 1), (ln_root, c * 5 + k))
                waits(pool, (pool_set, 1), (ln_mv, c + 1), (xn_ready, c))
                step(1, nc.gpsimd.tensor_scalar(root[0][:], mv[:, :, 1], EPS, None, ALU.add))
                step(2, nc.gpsimd.tensor_tensor(root[1][:], root[0][:], minus_half[:], ALU.pow))
                step(3, nc.gpsimd.tensor_tensor(root[2][:], root[1][:], root[1][:], ALU.mult))
                step(4, nc.gpsimd.tensor_tensor(root[3][:], root[2][:], mv[:, :, 1], ALU.mult))
                step(5, nc.gpsimd.tensor_scalar(root[4][:], root[3][:], EPS, None, ALU.add))
                nc.gpsimd.tensor_tensor(root[2][:], root[4][:], minus_half[:], ALU.pow).then_inc(ln_rstd, 1)
                pool.wait_ge(ln_rstd, c * 2 + 1)
                nc.gpsimd.tensor_tensor(root[5][:], root[2][:], root[1][:], ALU.mult).then_inc(ln_rstd, 1)

            def residual(c):
                pool.wait_ge(xn_ready, c + 1)
                wait(pool, xr_ready, c)
                nc.gpsimd.tensor_tensor(XS[:], XN[:], B2[:].unsqueeze(1).broadcast_to([P, TT, P]), ALU.add)\
                    .then_inc(xs_ready, 1)
                waits(pool, (pool_set, 1), (xs_ready, c + 1), (x_new, c))
                nc.gpsimd.tensor_tensor(XR[:], XS[:], X[:, tiles(c), :], ALU.add).then_inc(xr_ready, 1)

            def first(c):
                if attn is not None:
                    bias_x(c)
                roots(c)
                if attn is None:
                    roots(c + 1)
                residual(c)

            def root3(c):
                waits(pool, (pool_set, 1), (ln3_mv, c + 1))
                nc.gpsimd.tensor_scalar(ve3[:], mv3[:, :, 1], EPS, None, ALU.add).then_inc(ln3_root, 1)
                pool.wait_ge(ln3_root, c + 1)
                nc.gpsimd.tensor_tensor(rstd3[:], ve3[:], minus_half[:], ALU.pow).then_inc(ln3_rstd, 1)

            def bias_out(c):
                waits(pool, (pool_set, 1), (xn3_ready, c + 1))
                nc.gpsimd.tensor_tensor(X[:, tiles(c), :], X[:, tiles(c), :],
                                        BOV[:].unsqueeze(1).broadcast_to([P, TT, P]), ALU.add)\
                    .then_inc(x_out_biased, 1)

            def body(c, ahead, behind, far):
                if ahead and attn is not None:
                    bias_x(c + 1)
                    roots(c + 1)
                if far and attn is None:
                    roots(c + 2)
                if tail is not None:
                    root3(c)
                if ahead:
                    residual(c + 1)
                if tail is not None:
                    bias_out(c)

            nc.gpsimd.memset(minus_half[:], -0.5).then_inc(pool_set, 1)
            pool.wait_ge(pool_set, 1)
            pool.wait_ge(*w_ready)
            over_batches(pool, first, body, lambda c: None)

        @block.scalar
        def _(act):
            if attn is not None:
                o_rows = o_d.rearrange("(c a) b r n -> c (a b r) n", c=B)

            def load_o(c):
                wait(act, ot_turned, c)
                act.dma_start(OC[:], o_rows[c].rearrange("(t p) n -> p t n", p=P)).then_inc(oc_in, 16)

            def copy_ot(c):
                act.wait_ge(ot_turned, c + 1)
                wait(act, proj_done, c)
                nc.scalar.activation(OT[:], pT[:], ACT.Copy).then_inc(ot_copied, 1)

            def copy_ht(c):
                act.wait_ge(ht_turned, c + 1)
                wait(act, ht_lo, c)
                wait(act, ht_hi, c)
                nc.scalar.activation(HT[:], pT[:], ACT.Identity, scale=GB[:, 0:1], bias=GB[:, 1:2])\
                    .then_inc(ht_full, 1)

            def silu(c, f):
                act.wait_ge(fc1_done, c * FT + f + 1)
                if f == 0:
                    wait(act, fc2_done, c)
                nc.scalar.activation(Y[:, f, :], pF[:, f % 2, :], ACT.Silu, bias=B1[:, f:f + 1])\
                    .then_inc(silu_done, 1)

            def turn_hi(c):
                act.wait_ge(xt_turned, c + 1)
                wait(act, v_mm, c * 8)
                wait(act, xt_kept, c * 32)
                nc.scalar.activation(XTH[:], pT3[:], ACT.Copy).then_inc(xt_hi, 1)

            def copy_v(c, t):
                for half in range(2):
                    act.wait_ge(v_mm, c * 8 + t * 2 + half + 1)
                    if t == 0 and half == 0:
                        wait(act, v_stored, c * 64)
                    nc.scalar.activation(V[:, t, half * N:(half + 1) * N], pV[:, half, :], ACT.Copy)\
                        .then_inc(v_copied, 1)

            def first(c):
                if attn is not None:
                    copy_ot(c)
                    load_o(c + 1)
                copy_ht(c)

            def body(c, ahead, behind, far):
                silu(c, 0)
                silu(c, 1)
                if behind and tail is not None:
                    turn_hi(c - 1)
                if ahead and attn is not None:
                    copy_ot(c + 1)
                    if far:
                        load_o(c + 2)
                silu(c, 2)
                silu(c, 3)
                if behind and tail is not None:
                    copy_v(c - 1, 0)
                    copy_v(c - 1, 1)
                if ahead:
                    copy_ht(c + 1)
                if behind and tail is not None:
                    copy_v(c - 1, 2)
                    copy_v(c - 1, 3)

            def behind(c):
                if tail is not None:
                    turn_hi(c)
                    for t in range(TT):
                        copy_v(c, t)

            if attn is not None:
                load_o(0)
            act.wait_ge(*w_ready)
            over_batches(act, first, body, behind)

        @block.tensor
        def _(pe):
            def turn_ot(c):
                pe.wait_ge(oc_in, (c + 1) * 16)
                wait(pe, ht_full, c)
                for t in range(TT):
                    last = nc.tensor.transpose(pT[:, t * P:(t + 1) * P], OC[:, t, :], IDENT[:])
                last.then_inc(ot_turned, 1)

            def project(c):
                pe.wait_ge(ot_copied, c + 1)
                wait(pe, x_mid, c)
                for t in range(TT):
                    last = nc.tensor.matmul(pP[:, t, :], OT[:, t * P:(t + 1) * P], WP[:], start=True, stop=True)
                last.then_inc(proj_done, 1)

            def turn_h(c):
                pe.wait_ge(h_ready, c + 1)
                if attn is not None:
                    pe.wait_ge(ot_copied, c + 1)
                else:
                    wait(pe, ht_full, c)
                for t in range(TT):
                    last = nc.tensor.transpose(pT[:, t * P:(t + 1) * P], H[:, t, :], IDENT[:])
                last.then_inc(ht_turned, 1)

            def fc1(c, f):
                if f == 0:
                    pe.wait_ge(ht_hi, c + 1)
                    pe.wait_ge(ht_lo, c + 1)
                wait(pe, silu_done, c * FT + f - 1)
                w = slice(f * P, (f + 1) * P)
                nc.tensor.matmul(pF[:, f % 2, :], W1H[:, w], HTH[:], start=True, stop=False)
                nc.tensor.matmul(pF[:, f % 2, :], W1L[:, w], HTH[:], start=False, stop=False)
                nc.tensor.matmul(pF[:, f % 2, :], W1H[:, w], HTL[:], start=False, stop=True).then_inc(fc1_done, 1)

            def fc2(c):
                pe.wait_ge(silu_done, c * FT + FT)
                wait(pe, x_new, c)
                for t in range(TT):
                    for f in range(FT):
                        last = nc.tensor.matmul(pZ[:, t, :], Y[:, f, t * P:(t + 1) * P], W2[:, f, :],
                                                start=(f == 0), stop=(f == FT - 1))
                last.then_inc(fc2_done, 1)

            def turn_xt(c):
                pe.wait_ge(xn3_ready, c + 1)
                wait(pe, xt_lo, c)
                for t in range(TT):
                    last = nc.tensor.transpose(pT3[:, t * P:(t + 1) * P], XN3[:, t, :], IDENT[:])
                last.then_inc(xt_turned, 1)

            def values(c, t):
                if t == 0:
                    pe.wait_ge(xt_hi, c + 1)
                    pe.wait_ge(xt_lo, c + 1)
                xt = slice(t * P, (t + 1) * P)
                for half in range(2):
                    w = slice(half * N, (half + 1) * N)
                    wait(pe, v_copied, c * 8 if t == 0 else c * 8 + t * 2 + half - 1)
                    nc.tensor.matmul(pV[:, half, :], XTH[:, xt], WVH[:, w], start=True, stop=False)
                    nc.tensor.matmul(pV[:, half, :], XTH[:, xt], WVL[:, w], start=False, stop=False)
                    nc.tensor.matmul(pV[:, half, :], XTL[:, xt], WVH[:, w], start=False, stop=True)\
                        .then_inc(v_mm, 1)

            def first(c):
                if attn is not None:
                    turn_ot(c)
                    project(c)
                turn_h(c)

            def body(c, ahead, behind, far):
                fc1(c, 0)
                fc1(c, 1)
                if behind and tail is not None:
                    turn_xt(c - 1)
                if ahead and attn is not None:
                    turn_ot(c + 1)
                fc1(c, 2)
                fc1(c, 3)
                if ahead and attn is not None:
                    project(c + 1)
                if ahead and attn is None:
                    turn_h(c + 1)
                fc2(c)
                if behind and tail is not None:
                    values(c - 1, 0)
                    values(c - 1, 1)
                if ahead and attn is not None:
                    turn_h(c + 1)
                if behind and tail is not None:
                    values(c - 1, 2)
                    values(c - 1, 3)

            def behind(c):
                if tail is not None:
                    turn_xt(c)
                    for t in range(TT):
                        values(c, t)

            pe.wait_ge(*w_ready)
            over_batches(pe, first, body, behind)

        @block.vector
        def _(dve):
            def x_middle(c):
                dve.wait_ge(proj_done, c + 1)
                dve.wait_ge(biased, c + 1)
                nc.vector.tensor_tensor(X[:, tiles(c), :], pP[:], X[:, tiles(c), :], ALU.add).then_inc(x_mid, 1)

            def tile_of(c):
                return lambda t: X[:, c * TT + t, :]

            def ln(c):
                if attn is not None:
                    x_middle(c)
                    waits(dve, w_ready, (x_mid, c + 1), (ln_rstd, c * 2))
                else:
                    waits(dve, w_ready, (ln_rstd, c * 2))
                mean_and_variance(nc, dve, ln_stats, c, tile_of(c), stats, mv, w_ready).then_inc(ln_mv, 1)

            def norms(c):
                dve.wait_ge(ln_rstd, c * 2 + 2)
                wait(dve, ht_turned, c)
                normalize(nc, tile_of(c), H, mv, root[5]).then_inc(h_ready, 1)
                wait(dve, xs_ready, c)
                normalize(nc, tile_of(c), XN, mv, root[1]).then_inc(xn_ready, 1)

            def split_h(c):
                dve.wait_ge(ht_full, c + 1)
                wait(dve, fc1_done, c * FT)
                nc.vector.tensor_copy(HTH[:], HT[:]).then_inc(ht_hi, 1)
                dve.wait_ge(ht_hi, c + 1)
                nc.vector.tensor_tensor(HTL[:], HT[:], HTH[:].bitcast(F32), ALU.subtract).then_inc(ht_lo, 1)

            def x_final(c):
                dve.wait_ge(fc2_done, c + 1)
                dve.wait_ge(xr_ready, c + 1)
                nc.vector.scalar_tensor_tensor(X[:, tiles(c), :], pZ[:], 0.5, XR[:], ALU.mult, ALU.add)\
                    .then_inc(x_new, 1)

            def ln3(c):
                waits(dve, w_ready, (x_new, c + 1), (ln3_rstd, c))
                mean_and_variance(nc, dve, ln3_stats, c, tile_of(c), stats3, mv3, w_ready).then_inc(ln3_mv, 1)

            def norm3(c):
                dve.wait_ge(ln3_rstd, c + 1)
                wait(dve, xt_turned, c)
                normalize(nc, tile_of(c), XN3, mv3, rstd3).then_inc(xn3_ready, 1)

            def turn_lo(c):
                dve.wait_ge(xt_hi, c + 1)
                wait(dve, v_mm, c * 8)
                wait(dve, xt_kept, c * 32)
                nc.vector.tensor_tensor(XTL[:], pT3[:], XTH[:].bitcast(F32), ALU.subtract).then_inc(xt_lo, 1)

            def first(c):
                ln(c)
                norms(c)
                if attn is None:
                    ln(c + 1)
                split_h(c)

            def body(c, ahead, behind, far):
                if attn is None:
                    if ahead:
                        norms(c + 1)
                    if far:
                        ln(c + 2)
                    if ahead:
                        split_h(c + 1)
                    x_final(c)
                    return
                if behind:
                    turn_lo(c - 1)
                if ahead:
                    ln(c + 1)
                x_final(c)
                ln3(c)
                if ahead:
                    norms(c + 1)
                    split_h(c + 1)
                norm3(c)

            def behind(c):
                if tail is not None:
                    turn_lo(c)

            over_batches(dve, first, body, behind)

def phase_b_attention(nc, X, IDENT, d, weights, XTH, XTL, v_d):
    with ExitStack() as ctx:
        sb = lambda n, s, t: ctx.enter_context(nc.sbuf_tensor(f"b_{n}", s, t))
        ps = lambda n, s, t: ctx.enter_context(nc.psum_tensor(f"b_{n}", s, t))
        sem = lambda n: ctx.enter_context(nc.semaphore(f"b_{n}"))
        MH, ML = DB, DB + 32
        R = range(2)
        WQK = [sb(f"w{r}", [P, 2, P], F32) for r in R]
        WH = [sb(f"w_hi{r}", [P, 2, P], F32R) for r in R]
        WL = [sb(f"w_lo{r}", [P, 2, P], F32R) for r in R]
        V = [sb(f"v{r}", [P, TT, P], F32) for r in R]
        Q1 = [sb(f"q1_{r}", [P, 2, N], F32R) for r in R]
        K1 = [sb(f"k1_{r}", [P, 2, N], F32R) for r in R]
        Q2 = [sb(f"q2_{r}", [P, 2, N], F32R) for r in R]
        K2 = [sb(f"k2_{r}", [P, 2, N], F32R) for r in R]
        BQ, BK, WO = weights.BQ, weights.BK, weights.WO
        GATHER = sb("gather_den", [P, 2, 32], F32)
        SPREAD = sb("spread_den", [P, TT, P], F32)
        ZERO = sb("zero", [P, 2, P], F32)
        EYE = sb("eye", [P, P], BF16)
        MQ = sb("mask_q", [P, 2 * P], BF16)
        MK = sb("mask_k", [P, 3 * P], BF16)
        PA = [sb(f"probs_a{h}", [P, 2, N], F32) for h in R]
        PB = [sb(f"probs_b{h}", [P, N], F32) for h in R]
        DS = [sb(f"den_sum{h}", [P, N - P], F32) for h in R]
        NM = [sb(f"neg_max{r}", [P, TT, 2], F32) for r in R]
        RDC = sb("recip_den", [P, P], F32)
        RD = sb("recip_den_rows", [P, N], F32)
        Z = [sb(f"z{r}", [P, N], F32) for r in R]
        pM = ps("p_max", [P, 2, N], F32)
        pA = ps("p_scores_a", [P, 2 * N], F32)
        pB = ps("p_scores_b", [P, N], F32)
        pZ = ps("p_z", [P, N], F32)
        pO = ps("p_out", [P, N], F32)
        pT = ps("p_max_rows", [2, N], F32)

        masks_set = sem("masks_set")
        stacks_set = sem("stacks_set")
        w_in = [sem(f"w_in{r}") for r in R]
        v_in = [sem(f"v_in{r}") for r in R]
        w_split = sem("w_split")
        q_mm = sem("q_mm")
        k_mm = sem("k_mm")
        hi_done = sem("hi")
        lo_done = sem("lo")
        copied = [sem(f"copied{r}") for r in R]
        sm_filled = sem("sm_filled")
        sm_reduced = sem("sm_reduced")
        nm_turned = sem("nm_turned")
        max_hi = sem("max_hi")
        max_lo = sem("max_lo")
        st_filled = sem("st_filled")
        exp_done = sem("exp")
        den_step = sem("den_step")
        pv_done = sem("pv")
        den_done = sem("den")
        den_spread = sem("den_spread")
        rd_copied = sem("recip_copied")
        recip_done = sem("recip")
        z_done = sem("z")
        wo_done = sem("wo_mm")
        x_added = sem("x_added")

        block = ctx.enter_context(nc.Block())

        HALF = NP // 2

        def over_slots(eng, body):
            for m in range(2):
                body(m, 0, m == 0, False, True)
                body(m, 1, False, False, True)
            with eng.Fori(2, B * HALF - 1) as m:
                body(m, 0, False, False, True)
                body(m, 1, False, False, True)
            body(B * HALF - 1, 0, False, False, False)
            body(B * HALF - 1, 1, False, True, False)

        def next_of(m, r):
            return (m, 1) if r == 0 else (m + 1, 0)

        def before(m, r):
            return (m, 0) if r == 1 else (m - 1, 1)

        def batch(m):
            return m // HALF

        def pair(m, r):
            return (m % HALF) * 2 + r

        def span(start, n):
            return slice(start, start + n) if isinstance(start, int) else bass.ds(start, n)

        def both_heads():
            return pT[:].rearrange("p (o n) -> p o n", o=1).to_broadcast([2, 2, N])

        @block.sync
        def _(sp):
            def load_w(m, r):
                now = pair(m, r) if isinstance(m, int) else sp.snap(pair(m, r))
                waits(sp, (stacks_set, 2), (w_split, 2 * (2 * m + r) - 2))
                sp.dma_start(WQK[r][:], d["wqk2"][:, now]).then_inc(w_in[r], 16)

            def load_v(m, r):
                now = pair(m, r) if isinstance(m, int) else sp.snap(pair(m, r))
                rows_of = batch(m) if isinstance(m, int) else sp.snap(batch(m))
                waits(sp, (stacks_set, 2), (pv_done, 4 * (2 * m + r) - 4))
                sp.dma_start(V[r][:], v_d[rows_of, now]).then_inc(v_in[r], 16)

            def copy_high(m, r):
                sp.wait_ge(hi_done, 6 * (2 * m + r) + 2)
                sp.dma_start(Q2[r][0:DB].bitcast(F32), Q1[r][0:DB].bitcast(F32)).then_inc(copied[r], 16)

            def body(m, r, first, last, ahead):
                n = next_of(m, r)
                if ahead:
                    load_w(m + 1, r)
                if not last:
                    load_v(*n)
                if ahead:
                    copy_high(m + 1, r)

            for r in R:
                load_w(0, r)
            load_v(0, 0)
            sp.wait_ge(stacks_set, 2)
            copy_high(0, 0)
            copy_high(0, 1)
            over_slots(sp, body)

        @block.gpsimd
        def _(pool):
            def split(m, r):
                i = 2 * m + r
                pool.wait_ge(w_in[r], (m + 1) * 16)
                wait(pool, k_mm, i - 1)
                nc.gpsimd.tensor_tensor(WH[r][:], WQK[r][:], ZERO[:], ALU.add).then_inc(w_split, 1)
                pool.wait_ge(w_split, 2 * i + 1)
                nc.gpsimd.tensor_tensor(WL[r][:], WQK[r][:], WH[r][:].bitcast(F32), ALU.subtract)\
                    .then_inc(w_split, 1)

            def body(m, r, first, last, ahead):
                i = 2 * m + r
                if ahead:
                    split(m + 1, r)
                for h in R:
                    n = i * 6 + h * 3
                    pool.wait_ge(exp_done, i * 4 + h * 2 + 1)
                    wait(pool, den_done, i)
                    nc.gpsimd.tensor_tensor(DS[h][:], PA[h][:, 0, P:N], PA[h][:, 1, 0:N - P], ALU.add)\
                        .then_inc(den_step, 1)
                    pool.wait_ge(exp_done, i * 4 + h * 2 + 2)
                    for k in range(2):
                        pool.wait_ge(den_step, n + k + 1)
                        nc.gpsimd.tensor_tensor(DS[h][:, P:N - P], DS[h][:, P:N - P],
                                                PB[h][:, k * 256:k * 256 + 256], ALU.add).then_inc(den_step, 1)

            nc.gpsimd.memset(MQ[:], MASKED).then_inc(masks_set, 1)
            nc.gpsimd.memset(MK[:, 0:2 * P], MASKED).then_inc(masks_set, 1)
            nc.gpsimd.memset(SPREAD[:], 1.0).then_inc(masks_set, 1)
            nc.gpsimd.memset(GATHER[:], 0.0).then_inc(masks_set, 1)
            nc.gpsimd.memset(EYE[:], 1.0).then_inc(masks_set, 1)
            nc.gpsimd.memset(ZERO[:], 0.0).then_inc(masks_set, 1)
            pool.wait_ge(masks_set, 6)
            nc.gpsimd.affine_select(out=MQ[:], in_=MQ[:], compare_op=ALU.is_gt, fill=0.0, base=0,
                                    pattern=[[1, 2 * P]], channel_multiplier=-1).then_inc(masks_set, 1)
            nc.gpsimd.affine_select(out=MK[:, P:2 * P], in_=MK[:, P:2 * P], compare_op=ALU.is_gt, fill=0.0,
                                    base=0, pattern=[[-1, P]], channel_multiplier=1).then_inc(masks_set, 1)
            nc.gpsimd.affine_select(out=EYE[:], in_=EYE[:], compare_op=ALU.is_equal, fill=0.0, base=0,
                                    pattern=[[-1, P]], channel_multiplier=1).then_inc(masks_set, 1)
            nc.gpsimd.affine_select(out=SPREAD[:].rearrange("p t (h c) -> p t h c", h=2),
                                    in_=SPREAD[:].rearrange("p t (h c) -> p t h c", h=2),
                                    compare_op=ALU.is_equal, fill=0.0, base=0,
                                    pattern=[[-32, TT], [-16, 2], [0, DB]], channel_multiplier=1)\
                .then_inc(masks_set, 1)
            nc.gpsimd.memset(GATHER[:, 0, 0:16], 1.0).then_inc(masks_set, 1)
            nc.gpsimd.memset(GATHER[:, 1, 16:32], 1.0).then_inc(masks_set, 1)
            for r in R:
                split(0, r)
            over_slots(pool, body)

        @block.tensor
        def _(pe):
            def project(m, r, qk):
                i = 2 * m + r
                pe.wait_ge(w_split, 2 * i + 2)
                wait(pe, sm_reduced, 6 * i - 1 + qk)
                xt = span(batch(m) * N, N)
                u = pM[:, qk, :]
                nc.tensor.matmul(u, WH[r][:, qk, :], XTH[:, xt], start=True, stop=False)
                nc.tensor.matmul(u, WL[r][:, qk, :], XTH[:, xt], start=False, stop=False)
                nc.tensor.matmul(u, WH[r][:, qk, :], XTL[:, xt], start=False, stop=True)\
                    .then_inc((q_mm, k_mm)[qk], 1)

            def out_product(m, r):
                i = 2 * m + r
                pe.wait_ge(z_done, i + 1)
                for t in range(TT):
                    last = nc.tensor.matmul(pO[:, t * P:(t + 1) * P], Z[r][:, t * P:(t + 1) * P],
                                            WO[:, pair(m, r), :], start=True, stop=True)
                last.then_inc(wo_done, 1)

            def smax_unit(m, r, h, part):
                i = 2 * m + r
                if h == 0 and part == 0:
                    pe.wait_ge(hi_done, i * 6 + 4)
                    pe.wait_ge(lo_done, i * 4 + 2)
                elif h == 0 and part == 1:
                    pe.wait_ge(lo_done, i * 4 + 4)
                wait(pe, sm_reduced, i * 6 + h * 3 + part - 1)
                bank = pM[:, (h * 3 + part) % 2, :]
                for qt, keys in ((0, bank[:, 0:256]), (1, bank[:, 256:512])) if part == 0 else \
                        ((part + 1, bank[:, 0:(part + 2) * P]),):
                    nc.tensor.matmul(keys, Q1[r][:, h, qt * P:(qt + 1) * P], K1[r][:, h, 0:max(256, (qt + 1) * P)],
                                     start=True, stop=False)
                    if qt == 0:
                        last = nc.tensor.matmul(keys, EYE[:], MQ[:], start=False, stop=True)
                    else:
                        last = nc.tensor.matmul(keys[:, qt * P:(qt + 1) * P], EYE[:], MQ[:, 0:P], start=False, stop=True)
                last.then_inc(sm_filled, 1)

            def scores(m, r, h, part):
                i = 2 * m + r
                if h == 0 and part == 0:
                    pe.wait_ge(copied[r], (m + 1) * 16)
                    pe.wait_ge(max_lo, i + 1)
                wait(pe, exp_done, i * 4 + h * 2 + part - 1)
                for kt in (2 * part, 2 * part + 1):
                    q0 = min(kt * P, 256)
                    n = N - q0
                    bank = pA[:, kt * N:kt * N + n] if part == 0 else pB[:, (kt - 2) * 256:(kt - 2) * 256 + n]
                    keys = slice(kt * P, (kt + 1) * P)
                    nc.tensor.matmul(bank, K1[r][:, h, keys], Q1[r][:, h, q0:N], start=True, stop=False)
                    nc.tensor.matmul(bank, K2[r][:, h, keys], Q2[r][:, h, q0:N], start=False, stop=False)
                    if kt < 3:
                        last = nc.tensor.matmul(bank[:, 0:P], EYE[:], MK[:, P:2 * P], start=False, stop=True)
                    else:
                        last = nc.tensor.matmul(bank, EYE[:], MK[:, 0:2 * P], start=False, stop=True)
                last.then_inc(st_filled, 1)

            def pv(m, r, kt):
                i = 2 * m + r
                pe.wait_ge(exp_done, i * 4 + (3 if kt < 2 else 4))
                if kt == 0:
                    pe.wait_ge(v_in[r], (m + 1) * 16)
                    wait(pe, z_done, i)
                for h in R:
                    probs = PA[h][:, kt, 0:N - kt * P] if kt < 2 else \
                        PB[h][:, (kt - 2) * 256 + (kt - 2) * P:(kt - 1) * 256]
                    last = nc.tensor.matmul(pZ[h * DB:(h + 1) * DB, kt * P:N], V[r][:, kt, h * DB:(h + 1) * DB],
                                            probs, start=(kt == 0), stop=(kt == TT - 1), skip_group_check=True)
                last.then_inc(pv_done, 1)

            def denominators(m, r):
                i = 2 * m + r
                wait(pe, x_added, i)
                for h in R:
                    pe.wait_ge(den_step, i * 6 + h * 3 + 3)
                    for t in range(TT):
                        sums = PA[h][:, 0, 0:P] if t == 0 else DS[h][:, (t - 1) * P:t * P]
                        last = nc.tensor.matmul(pO[32 * t:32 * t + 32, 0:P], GATHER[:, h, :], sums,
                                                start=(h == 0), stop=(h == 1), skip_group_check=True)
                last.then_inc(den_done, 1)

            def spread(m, r):
                i = 2 * m + r
                pe.wait_ge(recip_done, i + 1)
                for t in range(TT):
                    last = nc.tensor.matmul(pO[:, t * P:(t + 1) * P], SPREAD[:, t, :], RDC[:],
                                            start=True, stop=True)
                last.then_inc(den_spread, 1)

            def turn_max(m, r):
                i = 2 * m + r
                pe.wait_ge(sm_reduced, i * 6 + 6)
                wait(pe, max_lo, i)
                for qt in range(TT):
                    last = nc.tensor.transpose(pT[:, qt * P:(qt + 1) * P], NM[r][:, qt, :], IDENT[:])
                last.then_inc(nm_turned, 1)

            def body(m, r, first, last, ahead):
                n = next_of(m, r)

                def smax(h, part):
                    if not last:
                        smax_unit(*n, h, part)

                scores(m, r, 0, 0)
                scores(m, r, 0, 1)
                smax(0, 0)
                if not first:
                    spread(*before(m, r))
                smax(0, 1)
                scores(m, r, 1, 0)
                smax(0, 2)
                smax(1, 0)
                if not first:
                    out_product(*before(m, r))
                smax(1, 1)
                scores(m, r, 1, 1)
                smax(1, 2)
                if ahead:
                    project(m + 1, r, 0)
                if not last:
                    turn_max(*n)
                if ahead:
                    project(m + 1, r, 1)
                pv(m, r, 0)
                pv(m, r, 1)
                pv(m, r, 2)
                pv(m, r, 3)
                denominators(m, r)

            project(0, 0, 0)
            project(0, 0, 1)
            pe.wait_ge(masks_set, 12)
            pe.wait_ge(stacks_set, 2)
            for h in R:
                for part in range(3):
                    smax_unit(0, 0, h, part)
            turn_max(0, 0)
            project(0, 1, 0)
            project(0, 1, 1)
            over_slots(pe, body)
            spread(B * HALF - 1, 1)
            out_product(B * HALF - 1, 1)

        @block.scalar
        def _(act):
            def high(m, r, qk):
                i = 2 * m + r
                dst, bias = ((Q1, BQ), (K1, BK))[qk]
                act.wait_ge((q_mm, k_mm)[qk], i + 1)
                wait(act, st_filled, 4 * (i - 1))
                for h in R:
                    for half in range(1 + qk):
                        nc.scalar.activation(dst[r][half * DB:(half + 1) * DB, h, :],
                                             pM[h * DB:(h + 1) * DB, qk, :], ACT.Identity,
                                             bias=bias[:, bias_col(m, r, h)]).then_inc(hi_done, 1)

            def max_high(m, r):
                i = 2 * m + r
                act.wait_ge(nm_turned, i + 1)
                wait(act, st_filled, 4 * (i - 1))
                nc.scalar.activation(Q2[r][MH:MH + 2], both_heads(), ACT.Copy).then_inc(max_hi, 1)

            def copy_recip(m, r):
                i = 2 * m + r
                act.wait_ge(den_spread, i + 1)
                wait(act, z_done, i)
                nc.scalar.activation(RD[:], pO[:], ACT.Copy).then_inc(rd_copied, 1)

            def bias_col(m, r, h):
                return span(pair(m, r) * 2 + h, 1)

            def exp_unit(m, r, h, part):
                i = 2 * m + r
                act.wait_ge(st_filled, i * 4 + h * 2 + part + 1)
                if part == 0:
                    wait(act, pv_done, 4 * i)
                    wait(act, den_done, i)
                    nc.scalar.activation(PA[h][:].rearrange("p a n -> p (a n)")[:, 0:2 * N - P], pA[:, 0:2 * N - P],
                                         ACT.Exp, scale=SCALE_B).then_inc(exp_done, 1)
                else:
                    nc.scalar.activation(PB[h][:], pB[:], ACT.Exp, scale=SCALE_B).then_inc(exp_done, 1)

            def body(m, r, first, last, ahead):
                exp_unit(m, r, 0, 0)
                if not first:
                    copy_recip(*before(m, r))
                exp_unit(m, r, 0, 1)
                exp_unit(m, r, 1, 0)
                exp_unit(m, r, 1, 1)
                if not last:
                    max_high(*next_of(m, r))
                if ahead:
                    high(m + 1, r, 0)
                    high(m + 1, r, 1)

            high(0, 0, 0)
            high(0, 0, 1)
            max_high(0, 0)
            high(0, 1, 0)
            high(0, 1, 1)
            over_slots(act, body)
            copy_recip(B * HALF - 1, 1)

        @block.vector
        def _(dve):
            def low(m, r, qk):
                i = 2 * m + r
                for h in R:
                    dve.wait_ge(hi_done, i * 6 + (h + 1 if qk == 0 else 2 * h + 4))
                    src, hi, bias = ((pM[:, 0, :], Q1, BQ), (pM[:, 1, :], K1, BK))[qk]
                    dst = Q1[r][DB:2 * DB, h, :] if qk == 0 else K2[r][0:DB, h, :]
                    nc.vector.scalar_tensor_tensor(dst, src[h * DB:(h + 1) * DB, :],
                                                   bias[:, span(pair(m, r) * 2 + h, 1)],
                                                   hi[r][0:DB, h, :].bitcast(F32), ALU.add, ALU.subtract)\
                        .then_inc(lo_done, 1)

            def reduce_unit(m, r, h, part):
                i = 2 * m + r
                dve.wait_ge(sm_filled, i * 6 + h * 3 + part + 1)
                if h == 0 and part == 0:
                    wait(dve, nm_turned, i - 1)
                bank = pM[:, (h * 3 + part) % 2, :]
                if part == 0:
                    nc.vector.tensor_reduce(NM[r][:, 0:2, h], bank.rearrange("p (t k) -> p t k", t=2), AX.X,
                                            ALU.max, negate=True).then_inc(sm_reduced, 1)
                else:
                    nc.vector.tensor_reduce(NM[r][:, part + 1, h:h + 1], bank[:, 0:(part + 2) * P], AX.X,
                                            ALU.max, negate=True).then_inc(sm_reduced, 1)

            def max_low(m, r):
                i = 2 * m + r
                dve.wait_ge(max_hi, i + 1)
                nc.vector.tensor_tensor(Q2[r][ML:ML + 2], both_heads(), Q2[r][MH:MH + 2].bitcast(F32),
                                        ALU.subtract).then_inc(max_lo, 1)

            def recip_den(m, r):
                i = 2 * m + r
                dve.wait_ge(den_done, i + 1)
                wait(dve, den_spread, i)
                nc.vector.reciprocal(RDC[:], pO[:, 0:P]).then_inc(recip_done, 1)

            def normalize_z(m, r):
                i = 2 * m + r
                dve.wait_ge(rd_copied, i + 1)
                dve.wait_ge(pv_done, 4 * i + 4)
                wait(dve, wo_done, i - 1)
                nc.vector.tensor_tensor(Z[r][:], pZ[:], RD[:], ALU.mult).then_inc(z_done, 1)

            def add_out(m, r):
                i = 2 * m + r
                dve.wait_ge(wo_done, i + 1)
                xb = X[:, span(batch(m) * TT, TT), :]
                nc.vector.tensor_tensor(xb, pO[:].rearrange("p (t n) -> p t n", t=TT), xb, ALU.add)\
                    .then_inc(x_added, 1)

            def body(m, r, first, last, ahead):
                n = next_of(m, r)
                if not last:
                    low(*n, 0)
                if not first:
                    recip_den(*before(m, r))
                if not last:
                    low(*n, 1)
                for h in R:
                    for part in range(3):
                        if not last:
                            reduce_unit(*n, h, part)
                        if (h, part) == (0, 1) and not first:
                            normalize_z(*before(m, r))
                if not first:
                    add_out(*before(m, r))
                if not last:
                    max_low(*n)

            for r in R:
                nc.vector.memset(Q2[r][:].bitcast(F32), 0.0)
                last_set = nc.vector.memset(K2[r][:].bitcast(F32), 0.0)
            last_set.then_inc(stacks_set, 1)
            dve.wait_ge(stacks_set, 1)
            for r in R:
                for h in R:
                    for row in (MH, ML):
                        last_set = nc.vector.tensor_copy(K2[r][row:row + 2, h, :],
                                                         IDENT[row:row + 2, row + h:row + h + 1].to_broadcast([2, N]))
            last_set.then_inc(stacks_set, 1)
            low(0, 0, 0)
            low(0, 0, 1)
            for h in R:
                for part in range(3):
                    reduce_unit(0, 0, h, part)
            max_low(0, 0)
            over_slots(dve, body)
            recip_den(B * HALF - 1, 1)
            normalize_z(B * HALF - 1, 1)
            add_out(B * HALF - 1, 1)


def program(nc, d, out):
    q_d = nc.dram_tensor("q_stacks", (B, HA, 4 * DA, N), F32).ap()
    k_d = nc.dram_tensor("k_stacks", (B, HA, 4 * DA, N), F32).ap()
    va_d = nc.dram_tensor("v_first", (B, P, NG, TT, GH, 32), F32).ap()
    vb_d = nc.dram_tensor("v_second", (B, NP, P, TT, P), F32).ap()
    o_d = nc.dram_tensor("o_first", (HA, B, 32, P), F32).ap()
    with ExitStack() as ctx:
        X = ctx.enter_context(nc.sbuf_tensor("x", [P, B * TT, P], F32))
        IDENT = ctx.enter_context(nc.sbuf_tensor("ident", [P, P], F32))
        weights = SharedWeights(nc, ctx, d)
        with ExitStack() as first:
            weights.allocate_raw(first)
            stacks = [first.enter_context(nc.sbuf_tensor(f"{qk}_stack{g}", [AR, GH, N], F32R))
                      for qk in "qk" for g in range(NG)]
            phase_a_inputs(nc, X, IDENT, d, (q_d, k_d, va_d), stacks, weights)
            phase_a_attention(nc, IDENT, d, (q_d, k_d, va_d), stacks, weights, o_d)
        with nc.sbuf_tensor("xt_all_hi", [P, B * N], F32R) as XTH, nc.sbuf_tensor("xt_all_lo", [P, B * N], F32R) as XTL:
            phase_ffn(nc, X, IDENT, weights, "f1", attn=o_d, tail=(XTH, XTL, vb_d))
            phase_b_attention(nc, X, IDENT, d, weights, XTH, XTL, vb_d)
        phase_ffn(nc, X, IDENT, weights, "f2", out=out)


def lay_out(i):
    wq, wk, wv = np.split(i["L0_attn_a_qkv_w"], 3, axis=0)
    bq, bk, bv = np.split(i["L0_attn_a_qkv_b"], 3)
    half = np.arange(D).reshape(HA, DA)
    half = np.roll(half, DA // 2, axis=1).reshape(D)
    inv = (1.0 / 10000.0 ** (np.arange(0, DA, 2, dtype=np.float32) / DA)).astype(np.float32)
    ang = np.arange(N, dtype=np.float32)[:, None] * inv[None, :]
    cos = np.concatenate([np.cos(ang), np.cos(ang)], 1).T
    sin = np.concatenate([-np.sin(ang), np.sin(ang)], 1).T
    rot = np.stack([np.tile(cos, (HA, 1)), np.tile(sin, (HA, 1))], 1).astype(np.float32)
    sel = np.zeros((P, 36), np.float32)
    for h in range(GH):
        sel[32 * h:32 * h + DA, h * DA:(h + 1) * DA] = np.eye(DA)
        sel[32 * h + DA, 32 + h] = 1.0
    c = np.ascontiguousarray
    return {
        "x": c(i["L0_attn_a_x"]),
        "wa": c(np.stack([wq.T, wq[half].T, wk.T, wk[half].T, wv.T], 1)),
        "bqk": c(np.stack([bq, bq[half], bk, bk[half]], 1)),
        "bv": c(bv),
        "rot": c(rot),
        "sel": sel,
        "ident": np.eye(P, dtype=np.float32),
        "wp": c(i["L0_attn_a_proj_w"].T),
        "bp": c(i["L0_attn_a_proj_b"]),
        "fc1_q": c(i["L0_ffn_fc1_q"]),
        "fc1_s": c(i["L0_ffn_fc1_scales"].reshape(FF)),
        "fc2_q": c(i["L0_ffn_fc2_q"]),
        "fc2_s": c(i["L0_ffn_fc2_scales"]),
        "gb": c(np.stack([i["L0_ffn_ln_gamma"], i["L0_ffn_ln_beta"]], 1)),
        "b1": c(i["L0_ffn_fc1_bias"].reshape(FT, P).T),
        "b2": c(i["L0_ffn_fc2_bias"]),
        "wqk2": c(np.stack([i["L0_attn_b_Wq"].transpose(1, 0, 2).reshape(D, NP, P),
                            i["L0_attn_b_Wk"].transpose(1, 0, 2).reshape(D, NP, P)], 2)),
        "wv2": c(i["L0_attn_b_Wv"].transpose(1, 0, 2).reshape(D, HB * DB)),
        "wo": c(i["L0_attn_b_Wo"].reshape(HB * DB, D)),
        "bq2": c(i["L0_attn_b_bq"].T),
        "bk2": c(i["L0_attn_b_bk"].T),
        "bv2": c(i["L0_attn_b_bv"].reshape(NP, P).T),
        "bo": c(i["L0_attn_b_bo"]),
    }


def kernel(**inputs):
    import concourse.bacc as bacc
    from concourse.bass_utils import run_bass_kernel_spmd

    nc = bacc.Bacc("TRN2", target_bir_lowering=False, num_devices=1)
    arrays = lay_out({name: np.asarray(a) for name, a in inputs.items()})
    d = {name: nc.dram_tensor(f"in_{name}", a.shape, mybir.dt.from_np(a.dtype), kind="ExternalInput").ap()
         for name, a in arrays.items()}
    out = nc.dram_tensor("out", (B, N, D), F32, kind="ExternalOutput").ap()
    program(nc, d, out)
    r = run_bass_kernel_spmd(nc, [{f"in_{name}": a for name, a in arrays.items()}], core_ids=[0])
    return r.results[0]["out"]
```
